# Optimizing a Trainium2 kernel written in Bass

```python
import numpy as np
import jax
import jax.numpy as jnp

def _softmax(x, axis=-1):
    return jax.nn.softmax(x, axis=axis)

def _gelu(x):
    return jax.nn.gelu(x, approximate=True)

def _silu(x):
    return jax.nn.silu(x)

def _sigmoid(x):
    return jax.nn.sigmoid(x)

def _layernorm(x, axis=-1, eps=1e-05):
    m = jnp.mean(x, axis=axis, keepdims=True)
    v = jnp.var(x, axis=axis, keepdims=True)
    return (x - m) / jnp.sqrt(v + eps)

def _scatter_add(tgt, idx, src, axis=0):
    return tgt.at[idx].add(src)

def _segment_sum(src, seg, n):
    return jax.ops.segment_sum(src, seg, n)
kernel_name = 'mk_decoder_preln_d2_seqx_r8_db69da'

def setup_inputs(seed: int=0):
    np.random.seed(seed)
    _w = jnp.asarray

    def _rec_inputs():
        import jax
        import jax.numpy as jnp
        _rk = jax.random.key(seed)
        x = 7.22e-05 + 1 * jax.random.normal(jax.random.fold_in(_rk, 1), (8, 128, 128), jnp.float32)
        _lenS = 128 - jax.random.randint(jax.random.fold_in(_rk, 7), (8,), 0, max(1, 128 // 4) + 1, jnp.int32)
        _lenS2 = 128 - jax.random.randint(jax.random.fold_in(_rk, 8), (8,), 0, max(1, 128 // 4) + 1, jnp.int32)
        _ctx_768P = jax.random.normal(jax.random.fold_in(_rk, 11), (8, 16, 96), jnp.float32)
        _ctx_768c = jax.random.dirichlet(jax.random.fold_in(_rk, 511), 0.3 * jnp.ones((16,), jnp.float32), (8, 128))
        _ctx_768t = jnp.einsum('bsk,bkd->bsd', _ctx_768c, _ctx_768P)
        _ctx_768t = _ctx_768t * jax.lax.rsqrt(jnp.mean(jnp.square(_ctx_768t)) + 1e-12) * 0.953939
        ctx_768 = -7.36909e-05 + 0.999899 * (_ctx_768t + 0.3 * jax.random.normal(jax.random.fold_in(_rk, 611), (8, 128, 96), jnp.float32))
        return (x, ctx_768)
    x, ctx_768 = _rec_inputs()

    def _L0_attn_setup():
        import jax, jax.numpy as jnp
        import numpy as np
        from jax import lax
        D_MODEL = 128
        D_STATE = 64
        EXPAND = 2
        HEADDIM = 64
        D_INNER = EXPAND * D_MODEL
        NH = D_INNER // HEADDIM
        N_ANG = D_STATE // 2
        A_FLOOR = 0.0001
        BATCH, SEQ = (2, 64)
        D_IN_PROJ = D_INNER + D_INNER + D_STATE + D_STATE + NH + NH + NH + N_ANG

        def _layernorm(x, g, b, eps=1e-05):
            m = x.mean(-1, keepdims=True)
            v = ((x - m) ** 2).mean(-1, keepdims=True)
            return (x - m) / jnp.sqrt(v + eps) * g + b

        def _rope_pairs(v, ang):
            ve, vo = (v[..., 0::2], v[..., 1::2])
            c, s = (jnp.cos(ang), jnp.sin(ang))
            re = ve * c - vo * s
            ro = ve * s + vo * c
            return jnp.stack([re, ro], axis=-1).reshape(v.shape)
        key = jax.random.key(seed)
        ks = jax.random.split(key, 9)
        u = jax.random.normal(ks[0], (BATCH, SEQ, D_MODEL), jnp.float32)
        W_in = jax.random.normal(ks[1], (D_MODEL, D_IN_PROJ), jnp.float32) * 0.02
        W_out = jax.random.normal(ks[2], (D_INNER, D_MODEL), jnp.float32) * 0.02
        dt_bias = jax.random.normal(ks[3], (NH,), jnp.float32) * 0.1
        D_param = jnp.ones((NH,), jnp.float32)
        Bn_g = 1.0 + 0.1 * jax.random.normal(ks[4], (D_STATE,), jnp.float32)
        Bn_b = 0.1 * jax.random.normal(ks[5], (D_STATE,), jnp.float32)
        Cn_g = 1.0 + 0.1 * jax.random.normal(ks[6], (D_STATE,), jnp.float32)
        Cn_b = 0.1 * jax.random.normal(ks[7], (D_STATE,), jnp.float32)
        return {'u': u, 'W_in': W_in, 'W_out': W_out, 'dt_bias': dt_bias, 'D_param': D_param, 'Bn_g': Bn_g, 'Bn_b': Bn_b, 'Cn_g': Cn_g, 'Cn_b': Cn_b}
    _L0_attn_all = _L0_attn_setup()
    _L0_attn_in = {k: v for k, v in _L0_attn_all.items() if k in ('W_in', 'W_out', 'dt_bias', 'D_param', 'Bn_g', 'Bn_b', 'Cn_g', 'Cn_b')}
    del _L0_attn_all

    def _L0_xattn_setup():
        import jax, jax.numpy as jnp
        import numpy as np
        NUM_HEADS = 16
        HEAD_DIM = 64
        INNER = NUM_HEADS * HEAD_DIM
        QUERY_DIM = 128
        CONTEXT_DIM = 96
        SCALE = HEAD_DIM ** (-0.5)
        key = jax.random.key(seed)
        ks = jax.random.split(key, 6)
        B, NQ, NKV = (8, 128, 256)
        query = jax.random.normal(ks[0], (B, NQ, QUERY_DIM), dtype=jnp.float32)
        context = jax.random.normal(ks[1], (B, NKV, CONTEXT_DIM), dtype=jnp.float32)
        w_q = jax.random.normal(ks[2], (QUERY_DIM, INNER), dtype=jnp.float32) * QUERY_DIM ** (-0.5)
        w_kv = jax.random.normal(ks[3], (CONTEXT_DIM, 2 * INNER), dtype=jnp.float32) * CONTEXT_DIM ** (-0.5)
        w_out = jax.random.normal(ks[4], (INNER, QUERY_DIM), dtype=jnp.float32) * INNER ** (-0.5)
        b_out = jax.random.normal(ks[5], (QUERY_DIM,), dtype=jnp.float32) * 0.01
        return {'query': query, 'context': context, 'w_q': w_q, 'w_kv': w_kv, 'w_out': w_out, 'b_out': b_out}
    _L0_xattn_all = _L0_xattn_setup()
    _L0_xattn_in = {k: v for k, v in _L0_xattn_all.items() if k in ('w_q', 'w_kv', 'w_out', 'b_out')}
    del _L0_xattn_all

    def _L0_ffn_setup():
        import jax, jax.numpy as jnp
        import numpy as np
        HIDDEN = 128
        INTER = 256
        NUM_EXPERTS = 8
        TOPK = 2
        STD = 0.02
        key = jax.random.key(seed)
        k1, k2, k3, k4 = jax.random.split(key, 4)
        return {'hidden_states': jax.random.normal(k1, (1, 256, HIDDEN), dtype=jnp.float32), 'w1': jax.random.normal(k2, (NUM_EXPERTS, 2 * INTER, HIDDEN), dtype=jnp.float32) * STD, 'w2': jax.random.normal(k3, (NUM_EXPERTS, HIDDEN, INTER), dtype=jnp.float32) * STD, 'router_w': jax.random.normal(k4, (NUM_EXPERTS, HIDDEN), dtype=jnp.float32) * STD}
    _L0_ffn_all = _L0_ffn_setup()
    _L0_ffn_in = {k: v for k, v in _L0_ffn_all.items() if k in ('w1', 'w2', 'router_w')}
    del _L0_ffn_all

    def _L1_attn_setup():
        import jax, jax.numpy as jnp
        import numpy as np
        import math
        EMBED_DIM = 128
        NUM_HEADS = 16
        HEAD_DIM = EMBED_DIM // NUM_HEADS
        key = jax.random.key(seed)
        ks = jax.random.split(key, 5)
        B, S, D = (2, 256, EMBED_DIM)
        s = 1.0 / math.sqrt(D)
        x = jax.random.normal(ks[0], (B, S, D), dtype=jnp.float32)
        W_qkv = jax.random.normal(ks[1], (3 * D, D), dtype=jnp.float32) * s
        b_qkv = jax.random.normal(ks[2], (3 * D,), dtype=jnp.float32) * 0.01
        W_out = jax.random.normal(ks[3], (D, D), dtype=jnp.float32) * s
        b_out = jax.random.normal(ks[4], (D,), dtype=jnp.float32) * 0.01
        return {'x': x, 'W_qkv': W_qkv, 'b_qkv': b_qkv, 'W_out': W_out, 'b_out': b_out}
    _L1_attn_all = _L1_attn_setup()
    _L1_attn_in = {k: v for k, v in _L1_attn_all.items() if k in ('W_qkv', 'b_qkv', 'W_out', 'b_out')}
    del _L1_attn_all

    def _L1_xattn_setup():
        import jax, jax.numpy as jnp
        import numpy as np
        HEADS = 16
        DIM_HEAD = 64
        RANK = 32
        LORA_W = 1.0
        IPA_SCALE = 1.0
        IPA_TOKENS = 4
        SCALE = DIM_HEAD ** (-0.5)

        def _split_heads(t):
            b, n, _ = t.shape
            return t.reshape(b, n, HEADS, DIM_HEAD).transpose(0, 2, 1, 3)

        def _merge_heads(t):
            b, h, n, d = t.shape
            return t.transpose(0, 2, 1, 3).reshape(b, n, h * d)

        def _attention(q_in, k_in, v_in):
            q = _split_heads(q_in)
            k = _split_heads(k_in)
            v = _split_heads(v_in)
            s = jnp.einsum('bhid,bhjd->bhij', q, k) * SCALE
            p = jax.nn.softmax(s, axis=-1)
            o = jnp.einsum('bhij,bhjd->bhid', p, v)
            return _merge_heads(o)

        def _lora(t, down, up, alpha):
            return t @ down @ up * (LORA_W * alpha[0] / RANK)
        key = jax.random.key(seed)
        ks = jax.random.split(key, 20)
        B, N, QD, CD, ID = (8, 512, 128, 96, HEADS * DIM_HEAD)
        CTX = 77 + IPA_TOKENS
        s = 0.02
        return {'x': jax.random.normal(ks[0], (B, N, QD), jnp.float32), 'context': jax.random.normal(ks[1], (B, CTX, CD), jnp.float32), 'Wq': jax.random.normal(ks[2], (QD, ID), jnp.float32) * s, 'Wk': jax.random.normal(ks[3], (CD, ID), jnp.float32) * s, 'Wv': jax.random.normal(ks[4], (CD, ID), jnp.float32) * s, 'Wo': jax.random.normal(ks[5], (ID, QD), jnp.float32) * s, 'bo': jnp.zeros((QD,), jnp.float32), 'q_down': jax.random.normal(ks[6], (QD, RANK), jnp.float32) * s, 'q_up': jax.random.normal(ks[7], (RANK, ID), jnp.float32) * s, 'q_alpha': jnp.ones((1,), jnp.float32) * RANK, 'k_down': jax.random.normal(ks[8], (CD, RANK), jnp.float32) * s, 'k_up': jax.random.normal(ks[9], (RANK, ID), jnp.float32) * s, 'k_alpha': jnp.ones((1,), jnp.float32) * RANK, 'v_down': jax.random.normal(ks[10], (CD, RANK), jnp.float32) * s, 'v_up': jax.random.normal(ks[11], (RANK, ID), jnp.float32) * s, 'v_alpha': jnp.ones((1,), jnp.float32) * RANK, 'o_down': jax.random.normal(ks[12], (ID, RANK), jnp.float32) * s, 'o_up': jax.random.normal(ks[13], (RANK, QD), jnp.float32) * s, 'o_alpha': jnp.ones((1,), jnp.float32) * RANK, 'Wk_ipa': jax.random.normal(ks[14], (CD, ID), jnp.float32) * s, 'Wv_ipa': jax.random.normal(ks[15], (CD, ID), jnp.float32) * s}
    _L1_xattn_all = _L1_xattn_setup()
    _L1_xattn_in = {k: v for k, v in _L1_xattn_all.items() if k in ('Wq', 'Wk', 'Wv', 'Wo', 'bo', 'q_down', 'q_up', 'q_alpha', 'k_down', 'k_up', 'k_alpha', 'v_down', 'v_up', 'v_alpha', 'o_down', 'o_up', 'o_alpha', 'Wk_ipa', 'Wv_ipa')}
    del _L1_xattn_all

    def _L1_ffn_setup():
        import jax, jax.numpy as jnp
        import numpy as np
        B, S, H = (2, 128, 128)
        E, F = (8, 512)
        GATE_TEMP = 0.1
        key = jax.random.key(seed)
        ks = jax.random.split(key, 6)
        s_h = 1.0 / np.sqrt(H)
        s_f = 1.0 / np.sqrt(F)
        return {'hidden_states': jax.random.normal(ks[0], (B, S, H), dtype=jnp.float32), 'w_router': jax.random.normal(ks[1], (H, E), dtype=jnp.float32) * s_h, 'w_gating': jax.random.normal(ks[2], (H, E), dtype=jnp.float32) * s_h, 'w_gate': jax.random.normal(ks[3], (E, H, F), dtype=jnp.float32) * s_h, 'w_up': jax.random.normal(ks[4], (E, H, F), dtype=jnp.float32) * s_h, 'w_down': jax.random.normal(ks[5], (E, F, H), dtype=jnp.float32) * s_f}
    _L1_ffn_all = _L1_ffn_setup()
    _L1_ffn_in = {k: v for k, v in _L1_ffn_all.items() if k in ('w_router', 'w_gating', 'w_gate', 'w_up', 'w_down')}
    del _L1_ffn_all
    return {'x': x, 'ctx_768': ctx_768, 'L0_attn_W_in': _L0_attn_in['W_in'], 'L0_attn_W_out': _L0_attn_in['W_out'], 'L0_attn_dt_bias': _L0_attn_in['dt_bias'], 'L0_attn_D_param': _L0_attn_in['D_param'], 'L0_attn_Bn_g': _L0_attn_in['Bn_g'], 'L0_attn_Bn_b': _L0_attn_in['Bn_b'], 'L0_attn_Cn_g': _L0_attn_in['Cn_g'], 'L0_attn_Cn_b': _L0_attn_in['Cn_b'], 'L0_xattn_w_q': _L0_xattn_in['w_q'], 'L0_xattn_w_kv': _L0_xattn_in['w_kv'], 'L0_xattn_w_out': _L0_xattn_in['w_out'], 'L0_xattn_b_out': _L0_xattn_in['b_out'], 'L0_ffn_w1': _L0_ffn_in['w1'], 'L0_ffn_w2': _L0_ffn_in['w2'], 'L0_ffn_router_w': _L0_ffn_in['router_w'], 'L1_attn_W_qkv': _L1_attn_in['W_qkv'], 'L1_attn_b_qkv': _L1_attn_in['b_qkv'], 'L1_attn_W_out': _L1_attn_in['W_out'], 'L1_attn_b_out': _L1_attn_in['b_out'], 'L1_xattn_Wq': _L1_xattn_in['Wq'], 'L1_xattn_Wk': _L1_xattn_in['Wk'], 'L1_xattn_Wv': _L1_xattn_in['Wv'], 'L1_xattn_Wo': _L1_xattn_in['Wo'], 'L1_xattn_bo': _L1_xattn_in['bo'], 'L1_xattn_q_down': _L1_xattn_in['q_down'], 'L1_xattn_q_up': _L1_xattn_in['q_up'], 'L1_xattn_q_alpha': _L1_xattn_in['q_alpha'], 'L1_xattn_k_down': _L1_xattn_in['k_down'], 'L1_xattn_k_up': _L1_xattn_in['k_up'], 'L1_xattn_k_alpha': _L1_xattn_in['k_alpha'], 'L1_xattn_v_down': _L1_xattn_in['v_down'], 'L1_xattn_v_up': _L1_xattn_in['v_up'], 'L1_xattn_v_alpha': _L1_xattn_in['v_alpha'], 'L1_xattn_o_down': _L1_xattn_in['o_down'], 'L1_xattn_o_up': _L1_xattn_in['o_up'], 'L1_xattn_o_alpha': _L1_xattn_in['o_alpha'], 'L1_xattn_Wk_ipa': _L1_xattn_in['Wk_ipa'], 'L1_xattn_Wv_ipa': _L1_xattn_in['Wv_ipa'], 'L1_ffn_w_router': _L1_ffn_in['w_router'], 'L1_ffn_w_gating': _L1_ffn_in['w_gating'], 'L1_ffn_w_gate': _L1_ffn_in['w_gate'], 'L1_ffn_w_up': _L1_ffn_in['w_up'], 'L1_ffn_w_down': _L1_ffn_in['w_down']}

def reference(x, ctx_768, L0_attn_W_in, L0_attn_W_out, L0_attn_dt_bias, L0_attn_D_param, L0_attn_Bn_g, L0_attn_Bn_b, L0_attn_Cn_g, L0_attn_Cn_b, L0_xattn_w_q, L0_xattn_w_kv, L0_xattn_w_out, L0_xattn_b_out, L0_ffn_w1, L0_ffn_w2, L0_ffn_router_w, L1_attn_W_qkv, L1_attn_b_qkv, L1_attn_W_out, L1_attn_b_out, L1_xattn_Wq, L1_xattn_Wk, L1_xattn_Wv, L1_xattn_Wo, L1_xattn_bo, L1_xattn_q_down, L1_xattn_q_up, L1_xattn_q_alpha, L1_xattn_k_down, L1_xattn_k_up, L1_xattn_k_alpha, L1_xattn_v_down, L1_xattn_v_up, L1_xattn_v_alpha, L1_xattn_o_down, L1_xattn_o_up, L1_xattn_o_alpha, L1_xattn_Wk_ipa, L1_xattn_Wv_ipa, L1_ffn_w_router, L1_ffn_w_gating, L1_ffn_w_gate, L1_ffn_w_up, L1_ffn_w_down):
    import jax
    import jax.numpy as jnp

    def _L0_attn_ref(u, W_in, W_out, dt_bias, D_param, Bn_g, Bn_b, Cn_g, Cn_b):
        import jax, jax.numpy as jnp
        import numpy as np
        from jax import lax
        D_MODEL = 128
        D_STATE = 64
        EXPAND = 2
        HEADDIM = 64
        D_INNER = EXPAND * D_MODEL
        NH = D_INNER // HEADDIM
        N_ANG = D_STATE // 2
        A_FLOOR = 0.0001
        BATCH, SEQ = (2, 64)
        D_IN_PROJ = D_INNER + D_INNER + D_STATE + D_STATE + NH + NH + NH + N_ANG

        def _layernorm(x, g, b, eps=1e-05):
            m = x.mean(-1, keepdims=True)
            v = ((x - m) ** 2).mean(-1, keepdims=True)
            return (x - m) / jnp.sqrt(v + eps) * g + b

        def _rope_pairs(v, ang):
            ve, vo = (v[..., 0::2], v[..., 1::2])
            c, s = (jnp.cos(ang), jnp.sin(ang))
            re = ve * c - vo * s
            ro = ve * s + vo * c
            return jnp.stack([re, ro], axis=-1).reshape(v.shape)
        B_, L, _ = u.shape
        proj = u @ W_in
        idx = np.cumsum([D_INNER, D_INNER, D_STATE, D_STATE, NH, NH, NH])
        z, x, Bp, Cp, dd_dt, dd_A, trap_raw, angles = jnp.split(proj, idx, axis=-1)
        x4 = x.reshape(B_, L, NH, HEADDIM)
        z4 = z.reshape(B_, L, NH, HEADDIM)
        Bp = _layernorm(Bp, Bn_g, Bn_b)
        Cp = _layernorm(Cp, Cn_g, Cn_b)
        DT = jax.nn.softplus(dd_dt + dt_bias)
        DT_mean = DT.mean(axis=-1, keepdims=True)
        phase = jnp.cumsum(angles * DT_mean, axis=1)
        Bp_rot = _rope_pairs(Bp, phase)
        Cp_rot = _rope_pairs(Cp, phase)
        A = jnp.minimum(-jax.nn.softplus(dd_A), -A_FLOOR)
        decay = jnp.exp(A * DT)
        trap = jax.nn.sigmoid(trap_raw)
        Bx = jnp.einsum('blhp,bln->blhpn', x4, Bp_rot)
        Bx_prev = jnp.pad(Bx[:, :-1], ((0, 0), (1, 0), (0, 0), (0, 0), (0, 0)))
        te = trap[..., None, None]
        inp = (te * Bx + (1.0 - te) * Bx_prev) * DT[..., None, None]
        decay_t = jnp.moveaxis(decay, 1, 0)
        inp_t = jnp.moveaxis(inp, 1, 0)
        C_t = jnp.moveaxis(Cp_rot, 1, 0)

        def step(h, xs):
            d, ip, c = xs
            h = d[:, :, None, None] * h + ip
            y = jnp.einsum('bhpn,bn->bhp', h, c)
            return (h, y)
        h0 = jnp.zeros((B_, NH, HEADDIM, D_STATE), u.dtype)
        _, ys = lax.scan(step, h0, (decay_t, inp_t, C_t))
        y = jnp.moveaxis(ys, 0, 1)
        y = (y + D_param[None, None, :, None] * x4) * jax.nn.silu(z4)
        out = y.reshape(B_, L, D_INNER) @ W_out
        return out

    def _L0_xattn_ref(query, context, w_q, w_kv, w_out, b_out):
        import jax, jax.numpy as jnp
        import numpy as np
        NUM_HEADS = 16
        HEAD_DIM = 64
        INNER = NUM_HEADS * HEAD_DIM
        QUERY_DIM = 128
        CONTEXT_DIM = 96
        SCALE = HEAD_DIM ** (-0.5)
        B, NQ, _ = query.shape
        NKV = context.shape[1]
        q = query @ w_q
        kv = context @ w_kv
        k, v = jnp.split(kv, 2, axis=-1)
        q = q.reshape(B, NQ, NUM_HEADS, HEAD_DIM).transpose(0, 2, 1, 3)
        k = k.reshape(B, NKV, NUM_HEADS, HEAD_DIM).transpose(0, 2, 1, 3)
        v = v.reshape(B, NKV, NUM_HEADS, HEAD_DIM).transpose(0, 2, 1, 3)
        scores = jnp.einsum('bhqd,bhkd->bhqk', q, k) * SCALE
        attn = jax.nn.softmax(scores, axis=-1)
        out = jnp.einsum('bhqk,bhkd->bhqd', attn, v)
        out = out.transpose(0, 2, 1, 3).reshape(B, NQ, INNER)
        return out @ w_out + b_out

    def _L0_ffn_ref(hidden_states, w1, w2, router_w):
        import jax, jax.numpy as jnp
        import numpy as np
        HIDDEN = 128
        INTER = 256
        NUM_EXPERTS = 8
        TOPK = 2
        STD = 0.02
        orig_shape = hidden_states.shape
        dtype = hidden_states.dtype
        x = hidden_states.reshape(-1, orig_shape[-1])
        E = w1.shape[0]
        gating = x @ router_w.T
        probs = jax.nn.softmax(gating.astype(jnp.float32), axis=-1)
        topk_w, sel = jax.lax.top_k(probs, TOPK)
        topk_w = topk_w.astype(dtype)
        combine = (jax.nn.one_hot(sel, E, dtype=dtype) * topk_w[..., None]).sum(axis=1)
        h = jnp.einsum('td,eid->tei', x, w1)
        gate = jax.nn.silu(h[..., :INTER])
        y = h[..., INTER:] * gate
        out = jnp.einsum('tei,ehi,te->th', y, w2, combine)
        return out.reshape(orig_shape)

    def _L1_attn_ref(x, W_qkv, b_qkv, W_out, b_out):
        import jax, jax.numpy as jnp
        import numpy as np
        import math
        EMBED_DIM = 128
        NUM_HEADS = 16
        HEAD_DIM = EMBED_DIM // NUM_HEADS
        B, S, D = x.shape
        H, Hd = (NUM_HEADS, HEAD_DIM)
        slopes = jnp.power(2.0, 8.0 * jnp.arange(0, -H, -1, dtype=jnp.float32) / H)
        qkv = x @ W_qkv.T + b_qkv
        qkv = qkv.reshape(B, S, 3, H, Hd).transpose(2, 0, 3, 1, 4)
        q, k, v = (qkv[0], qkv[1], qkv[2])
        scores = jnp.einsum('bhqd,bhkd->bhqk', q, k) / math.sqrt(Hd)
        pos = jnp.arange(S)
        rel = jnp.abs(pos[None, :] - pos[:, None]).astype(jnp.float32)
        bias = -slopes[:, None, None] * rel
        probs = jax.nn.softmax(scores + bias[None], axis=-1)
        out = jnp.einsum('bhqk,bhkd->bhqd', probs, v)
        out = out.transpose(0, 2, 1, 3).reshape(B, S, D)
        return out @ W_out.T + b_out

    def _L1_xattn_ref(x, context, Wq, Wk, Wv, Wo, bo, q_down, q_up, q_alpha, k_down, k_up, k_alpha, v_down, v_up, v_alpha, o_down, o_up, o_alpha, Wk_ipa, Wv_ipa):
        import jax, jax.numpy as jnp
        import numpy as np
        HEADS = 16
        DIM_HEAD = 64
        RANK = 32
        LORA_W = 1.0
        IPA_SCALE = 1.0
        IPA_TOKENS = 4
        SCALE = DIM_HEAD ** (-0.5)

        def _split_heads(t):
            b, n, _ = t.shape
            return t.reshape(b, n, HEADS, DIM_HEAD).transpose(0, 2, 1, 3)

        def _merge_heads(t):
            b, h, n, d = t.shape
            return t.transpose(0, 2, 1, 3).reshape(b, n, h * d)

        def _attention(q_in, k_in, v_in):
            q = _split_heads(q_in)
            k = _split_heads(k_in)
            v = _split_heads(v_in)
            s = jnp.einsum('bhid,bhjd->bhij', q, k) * SCALE
            p = jax.nn.softmax(s, axis=-1)
            o = jnp.einsum('bhij,bhjd->bhid', p, v)
            return _merge_heads(o)

        def _lora(t, down, up, alpha):
            return t @ down @ up * (LORA_W * alpha[0] / RANK)
        q_in = x @ Wq + _lora(x, q_down, q_up, q_alpha)
        end = context.shape[1] - IPA_TOKENS
        org_ctx = context[:, :end, :]
        ipa_ctx = context[:, end:, :]
        k_in = org_ctx @ Wk + _lora(org_ctx, k_down, k_up, k_alpha)
        v_in = org_ctx @ Wv + _lora(org_ctx, v_down, v_up, v_alpha)
        out = _attention(q_in, k_in, v_in)
        ipa_k = ipa_ctx @ Wk_ipa
        ipa_v = ipa_ctx @ Wv_ipa
        out_ipa = _attention(q_in, ipa_k, ipa_v)
        out = out + IPA_SCALE * out_ipa
        return out @ Wo + bo + _lora(out, o_down, o_up, o_alpha)

    def _L1_ffn_ref(hidden_states, w_router, w_gating, w_gate, w_up, w_down):
        import jax, jax.numpy as jnp
        import numpy as np
        B, S, H = (2, 128, 128)
        E, F = (8, 512)
        GATE_TEMP = 0.1
        x = hidden_states
        router_probs = jax.nn.softmax(jnp.einsum('bsh,he->bse', x, w_router), axis=-1)
        gate_weights = jax.nn.softmax(jnp.einsum('bsh,he->bse', x, w_gating) / GATE_TEMP, axis=-1)
        g = jnp.einsum('bsh,ehf->ebsf', x, w_gate)
        u = jnp.einsum('bsh,ehf->ebsf', x, w_up)
        h = jax.nn.silu(g) * u
        expert_out = jnp.einsum('ebsf,efh->ebsh', h, w_down)
        cw = router_probs * gate_weights
        cw = cw / (jnp.sum(cw, axis=-1, keepdims=True) + 1e-09)
        out = jnp.einsum('ebsh,bse->bsh', expert_out, cw)
        return out
    x = x + _L0_attn_ref(_layernorm(x, axis=-1), L0_attn_W_in, L0_attn_W_out, L0_attn_dt_bias, L0_attn_D_param, L0_attn_Bn_g, L0_attn_Bn_b, L0_attn_Cn_g, L0_attn_Cn_b)
    x = x + _L0_xattn_ref(_layernorm(x, axis=-1), ctx_768, L0_xattn_w_q, L0_xattn_w_kv, L0_xattn_w_out, L0_xattn_b_out)
    x = x + _L0_ffn_ref(_layernorm(x, axis=-1), L0_ffn_w1, L0_ffn_w2, L0_ffn_router_w)
    x = x + _L1_attn_ref(_layernorm(x, axis=-1), L1_attn_W_qkv, L1_attn_b_qkv, L1_attn_W_out, L1_attn_b_out)
    x = x + _L1_xattn_ref(_layernorm(x, axis=-1), ctx_768, L1_xattn_Wq, L1_xattn_Wk, L1_xattn_Wv, L1_xattn_Wo, L1_xattn_bo, L1_xattn_q_down, L1_xattn_q_up, L1_xattn_q_alpha, L1_xattn_k_down, L1_xattn_k_up, L1_xattn_k_alpha, L1_xattn_v_down, L1_xattn_v_up, L1_xattn_v_alpha, L1_xattn_o_down, L1_xattn_o_up, L1_xattn_o_alpha, L1_xattn_Wk_ipa, L1_xattn_Wv_ipa)
    x = x + _L1_ffn_ref(_layernorm(x, axis=-1), L1_ffn_w_router, L1_ffn_w_gating, L1_ffn_w_gate, L1_ffn_w_up, L1_ffn_w_down)
    return x

_drawn_inputs = setup_inputs


def setup_inputs(seed=0):
    import zlib

    import numpy as np

    out = dict(_drawn_inputs(seed))
    spreads = {'L0_attn_D_param': (1.0, 0.6), 'L1_xattn_bo': (0.0, 0.461)}
    factors = {'L0_attn_dt_bias': 8.0,
     'L0_attn_Bn_g': 8.0,
     'L0_attn_Bn_b': 7.673,
     'L0_attn_Cn_g': 7.509,
     'L0_attn_Cn_b': 8.0,
     'L0_xattn_b_out': 3.0,
     'L0_ffn_w1': 8.0,
     'L0_ffn_w2': 8.0,
     'L0_ffn_router_w': 8.0,
     'L1_attn_b_qkv': 21.832,
     'L1_attn_b_out': 25.296,
     'L1_xattn_Wq': 8.0,
     'L1_xattn_Wk': 8.0,
     'L1_xattn_q_down': 8.0,
     'L1_xattn_q_up': 8.0,
     'L1_xattn_k_down': 8.0,
     'L1_xattn_k_up': 8.0,
     'L1_xattn_v_down': 7.626,
     'L1_xattn_v_up': 7.534,
     'L1_xattn_o_down': 4.907,
     'L1_xattn_o_up': 4.76,
     'L1_xattn_Wk_ipa': 8.0}
    for name, (base, spread) in spreads.items():
        noise = np.random.default_rng([zlib.crc32(name.encode()), seed]).standard_normal(out[name].shape)
        drawn = base * np.exp(spread * noise) if base else spread * noise
        out[name] = jnp.asarray(drawn.astype(out[name].dtype))
    for name, factor in factors.items():
        out[name] = (out[name] * factor).astype(out[name].dtype)
    return out
```

```python
from contextlib import ExitStack

import numpy as np

import concourse.bass as bass
from concourse import mybir

F32 = mybir.dt.float32
BF16 = mybir.dt.bfloat16
ALU = mybir.AluOpType
ACT = mybir.ActivationFunctionType
AX = mybir.AxisListType.X

P = 128
NB = 8
D = 128
DC = 96
EPS = 1e-5
NH = 16
HD = 64
INNER = NH * HD
NT = INNER // P
VS = HD + 2
NCH = 4
HPC = NH // NCH
NE = 8
HALF = NB * P // 2
IPA = 4
DI = 256
SH = 4
NS = 64
NA = 32


class Order:

    def __init__(self, eng, sem, i=0, per=0):
        self.eng, self.sem, self.i, self.per, self.n = eng, sem, i, per, 0

    def mark(self, ins):
        ins.then_inc(self.sem, 1)
        self.n += 1
        return self.n

    def wait(self, n=None):
        self.eng.wait_ge(self.sem, self.i * self.per + (self.n if n is None else n))

    def after(self, ins):
        self.mark(ins)
        self.wait()

    def close(self):
        assert self.n == self.per, f"the body has {self.n} ordered steps"


def bc(ap, shape):
    return ap.to_broadcast(list(shape))


class Program:

    def __init__(self, nc, ctx, a, out):
        self.nc, self.ctx, self.a, self.out = nc, ctx, a, out
        sb, self.sb = self.sbuf, self.sbuf
        self.bank = [ctx.enter_context(nc.psum_tensor(f"bank{n}", [P, 512], F32)) for n in range(8)]
        self.x = sb("x", [P, NB + 1, D])
        self.ctx_t = sb("ctx_t", [DC, NB + 1, P])
        self.ident = sb("ident", [P, P])
        self.ident_bf = sb("ident_bf", [P, P], BF16)
        self.sel = sb("sel", [P, NH, P], BF16)
        self.live_sems = []
        self.neg_half = sb("neg_half", [P, NB])

    def sbuf(self, name, shape, dt=F32, ctx=None):
        return (ctx or self.ctx).enter_context(self.nc.sbuf_tensor("sb_" + name, shape, dt))

    def sems(self, prefix, names):
        got = [self.nc.alloc_semaphore(name=f"{prefix}_{n}") for n in names.split()]
        self.live_sems += got
        return got

    def recycle_sems(self):
        self.nc.clear_and_free_semaphores(self.live_sems)
        self.live_sems = []
        self.nc.all_engine_barrier()


def setup(pg):
    nc, a = pg.nc, pg.a
    with ExitStack() as ctx:
        x_in, ctx_in, zeroed, const_done, ctx_tr, ctx_cp = pg.sems(
            "su", "x_in ctx_in zeroed const_done ctx_transposed ctx_copied")
        ctx_sb = pg.sbuf("ctx_sb", [P, NB, DC], ctx=ctx)
        block = ctx.enter_context(nc.Block())

        @block.sync
        def _(sp):
            sp.dma_start(ctx_sb[:, :, :], a["ctx_768"].rearrange("b k c -> k b c")).then_inc(ctx_in, 16)
            sp.dma_start(pg.x[:, 0:NB, :], a["x"].rearrange("b l d -> l b d")).then_inc(x_in, 16)
            sp.wait_ge(x_in, 16)

        @block.gpsimd
        def _(pool):
            for n, t in enumerate((pg.ident, pg.ident_bf, pg.sel)):
                nc.gpsimd.memset(t[:], 0.0).then_inc(zeroed, 1)
            nc.gpsimd.memset(pg.neg_half[:, :], -0.5).then_inc(const_done, 1)
            nc.gpsimd.memset(pg.x[:, NB, :], 0.0).then_inc(const_done, 1)
            nc.gpsimd.memset(pg.ctx_t[:, NB, :], 0.0).then_inc(const_done, 1)
            pool.wait_ge(zeroed, 3)
            for t in (pg.ident, pg.ident_bf):
                nc.gpsimd.affine_select(out=t[:, :], in_=t[:, :], compare_op=ALU.not_equal, fill=1.0,
                                        base=0, pattern=[[-1, P]], channel_multiplier=1).then_inc(const_done, 1)
            for part in range(2):
                pool.wait_ge(const_done, 5 + part)
                nc.gpsimd.affine_select(out=pg.sel[:, :, :], in_=pg.sel[:, :, :], compare_op=ALU.not_equal,
                                        fill=1.0, base=-part * NH, pattern=[[-1, NH], [0, P]],
                                        channel_multiplier=1).then_inc(const_done, 1)

        @block.tensor
        def _(pe):
            pe.wait_ge(const_done, 5)
            pe.wait_ge(ctx_in, 16)
            for b in range(NB):
                nc.tensor.transpose(pg.bank[b // 4][0:DC, (b % 4) * P:(b % 4 + 1) * P], ctx_sb[:, b, :],
                                    pg.ident[:, :]).then_inc(ctx_tr, 1)

        @block.scalar
        def _(act):
            for h in range(2):
                act.wait_ge(ctx_tr, 4 * h + 4)
                nc.scalar.copy(pg.ctx_t[:, 4 * h:4 * h + 4, :].rearrange("c b k -> c (b k)"),
                               pg.bank[h][0:DC, :]).then_inc(ctx_cp, 1)


def norm_all(pg, dve, order, st, mv, ve, var_ready, rstd_ready, rs, xn, xn_ready):
    nc = pg.nc
    for b in range(NB):
        order.mark(nc.vector.bn_stats(st[:, b, :], pg.x[:, b, :]))
    for b in range(NB):
        order.wait(b + 1)
        order.mark(nc.vector.bn_aggr(mv[:, b, :], st[:, b, :]))
    order.wait()
    nc.vector.tensor_scalar(ve[:, :], mv[:, :, 1], EPS, None, ALU.add).then_inc(var_ready, 1)
    dve.wait_ge(rstd_ready, 1)
    for b in range(NB):
        nc.vector.tensor_scalar(xn[:, b, :], pg.x[:, b, :], mv[:, b, 0:1], rs[:, b:b + 1],
                                ALU.subtract, ALU.mult).then_inc(xn_ready, 1)


def norm_all_buffers(pg, ctx, name):
    return (pg.sbuf(f"{name}_st", [P, NB, 6], ctx=ctx), pg.sbuf(f"{name}_mv", [P, NB, 2], ctx=ctx),
            pg.sbuf(f"{name}_ve", [P, NB], ctx=ctx), pg.sbuf(f"{name}_rs", [P, NB], ctx=ctx),
            pg.sbuf(f"{name}_xn", [P, NB, D], ctx=ctx))


def state_space(pg):
    nc, a = pg.nc, pg.a
    with ExitStack() as outer:
        zx = pg.sbuf("ss_zx", [P, NB, 2 * DI], ctx=outer)
        sz = pg.sbuf("ss_sz", [P, NB, DI], ctx=outer)
        br = pg.sbuf("ss_br", [P, NB, 2, NS], ctx=outer)
        logd = pg.sbuf("ss_logd", [P, NB, SH], ctx=outer)
        past = pg.sbuf("ss_past", [P, NB, SH], ctx=outer)
        now = pg.sbuf("ss_now", [P, NB, SH], ctx=outer)
        upper = pg.sbuf("ss_upper", [P, P], ctx=outer)
        strict = pg.sbuf("ss_strict", [P, P], ctx=outer)
        after = pg.sbuf("ss_after", [P, P], ctx=outer)
        w_out = pg.sbuf("ss_w_out", [P, 2, D], ctx=outer)
        w_out_in, = pg.sems("ss", "w_out_in")
        state_space_project(pg, zx, sz, br, logd, past, now, upper, strict, after, w_out, w_out_in)
        state_space_mix(pg, zx, sz, br, logd, past, now, upper, strict, after, w_out, w_out_in)


def state_space_project(pg, zx, sz, br, logd, past, now, upper, strict, after, w_out, w_out_in):
    nc, a = pg.nc, pg.a
    NBC = 2 * NS + 3 * SH + NA
    AN = 2 * NS + 3 * SH
    with ExitStack() as ctx:
        (w_in_in, par_in, var_ready, rstd_ready, xn_ready, xt_ready, xt_copied, zx_ready, small_ready, zx_copied,
         small_copied, bc_var_ready, bc_rstd_ready, masks0, masks_done, order_sem, sp_in, sp_exp, sp_one, sp_ln, sg_done,
         phase_in, phase_ready, trig_in, trig_done, adt_ready, dec_done, shift_in, shifted, silu_done) = pg.sems("sp", (
            "w_in_in par_in var_ready rstd_ready xn_ready xt_ready xt_copied zx_ready small_ready zx_copied "
            "small_copied bc_var_ready bc_rstd_ready masks_zeroed masks_done order softplus_in softplus_exp softplus_one "
            "softplus_ln sigmoid_done phase_in phase_ready trig_in trig_done adt_ready decay_done shift_in shifted silu_done"))
        sb = lambda n, s: pg.sbuf("sp_" + n, s, ctx=ctx)
        w_in = sb("w_in", [P, 2 * DI + NBC])
        st, mv, ve, rs, xn = norm_all_buffers(pg, ctx, "sp")
        xt = sb("xt", [P, NB, P])
        sm = sb("sm", [P, NB, NBC])
        gb = sb("gb", [P, 2, 2, NS])
        dtb = sb("dtb", [P, SH])
        dpar = sb("dpar", [P, SH])
        bst = sb("bst", [P, NB, 2, 6])
        bmv = sb("bmv", [P, NB, 2, 2])
        bve = sb("bve", [P, 2 * NB])
        brs = sb("brs", [P, 2 * NB])
        half2 = sb("half2", [P, 2 * NB])
        bn = sb("bn", [P, NB, 2, NS])
        shift = sb("shift", [P, P])
        u = sb("u", [P, NB, 2, SH])
        au = sb("au", [P, NB, 2, SH])
        eu = sb("eu", [P, NB, 2, SH])
        lu = sb("lu", [P, NB, 2, SH])
        pu = sb("pu", [P, NB, 2, SH])
        tr = sb("tr", [P, NB, SH])
        te = sb("te", [P, NB, SH])
        dtm = sb("dtm", [P, NB, 1])
        ang = sb("ang", [P, NB, NA])
        turns = sb("turns", [P, 2, NB * NA])
        rem = sb("rem", [P, 2, NB * NA])
        trig = sb("trig", [P, 2, NB, NA])
        r0 = sb("r0", [P, NB, NA])
        r1 = sb("r1", [P, NB, NA])
        r2 = sb("r2", [P, NB, NA])
        r3 = sb("r3", [P, NB, NA])
        sh_in = sb("sh_in", [P, 2, NB * SH])
        cb = sb("cb", [P, NB, NS])
        cbd = sb("cbd", [P, NB, 1])
        block = ctx.enter_context(nc.Block())

        @block.sync
        def _(sp):
            sp.dma_start(w_in[:, :], a["L0_attn_W_in"]).then_inc(w_in_in, 16)
            for k, n in enumerate(("Bn_g", "Cn_g", "Bn_b", "Cn_b")):
                sp.dma_start(gb[:, k // 2, k % 2, :], a["L0_attn_" + n].partition_broadcast(P)).then_inc(par_in, 16)
            sp.dma_start(dtb[:, :], a["L0_attn_dt_bias"].partition_broadcast(P)).then_inc(par_in, 16)
            sp.dma_start(dpar[:, :], a["L0_attn_D_param"].partition_broadcast(P)).then_inc(par_in, 16)
            sp.dma_start(w_out[:, :, :], a["L0_attn_W_out"].rearrange("(t p) d -> p t d", p=P)).then_inc(w_out_in, 16)

        @block.gpsimd
        def _(pool):
            nc.gpsimd.memset(half2[:, :], -0.5).then_inc(masks0, 1)
            for m in (upper, strict, after):
                nc.gpsimd.memset(m[:, :], 1.0).then_inc(masks0, 1)
            nc.gpsimd.memset(shift[:, :], 0.0).then_inc(masks0, 1)
            pool.wait_ge(var_ready, 1)
            nc.gpsimd.tensor_tensor(rs[:, :], ve[:, :], pg.neg_half[:, :], ALU.pow).then_inc(rstd_ready, 1)
            pool.wait_ge(masks0, 5)
            for m, base, mul, step, op, fill in ((upper, 0, -1, 1, ALU.is_ge, 0.0), (strict, 0, -1, 1, ALU.is_gt, 0.0),
                                                 (after, -1, 1, -1, ALU.is_gt, 0.0), (shift, -1, 1, -1, ALU.not_equal, 1.0)):
                nc.gpsimd.affine_select(out=m[:, :], in_=m[:, :], compare_op=op, fill=fill, base=base,
                                        pattern=[[step, P]], channel_multiplier=mul).then_inc(masks_done, 1)
            pool.wait_ge(bc_var_ready, 1)
            nc.gpsimd.tensor_tensor(brs[:, :], bve[:, :], half2[:, :], ALU.pow).then_inc(bc_rstd_ready, 1)

        @block.tensor
        def _(pe):
            for b in range(NB):
                pe.wait_ge(xn_ready, b + 1)
                nc.tensor.transpose(pg.bank[b // 4][:, (b % 4) * P:(b % 4 + 1) * P], xn[:, b, :],
                                    pg.ident[:, :]).then_inc(xt_ready, 1)
            pe.wait_ge(w_in_in, 16)
            for b in range(NB):
                pe.wait_ge(xt_copied, b // 4 + 1)
                if b >= 2:
                    pe.wait_ge(zx_copied, b - 1)
                nc.tensor.matmul(pg.bank[2 + b % 2][:, :], xt[:, b, :], w_in[:, 0:2 * DI],
                                 start=True, stop=True).then_inc(zx_ready, 1)
                if b >= 2:
                    pe.wait_ge(small_copied, b - 1)
                nc.tensor.matmul(pg.bank[4 + b % 2][:, 0:NBC], xt[:, b, :], w_in[:, 2 * DI:],
                                 start=True, stop=True).then_inc(small_ready, 1)
            pe.wait_ge(masks_done, 4)
            pe.wait_ge(phase_in, 1)
            nc.tensor.matmul(pg.bank[6][:, 0:NB * NA], upper[:, :], ang[:, :, :].rearrange("p b n -> p (b n)"),
                             start=True, stop=True).then_inc(phase_ready, 1)
            pe.wait_ge(shift_in, 2)
            nc.tensor.matmul(pg.bank[7][:, 0:2 * NB * SH], shift[:, :], sh_in[:, :, :].rearrange("p k n -> p (k n)"),
                             start=True, stop=True).then_inc(shifted, 1)

        @block.scalar
        def _(act):
            for h in range(2):
                act.wait_ge(xt_ready, 4 * h + 4)
                nc.scalar.copy(xt[:, 4 * h:4 * h + 4, :].rearrange("p b l -> p (b l)"),
                               pg.bank[h][:, :]).then_inc(xt_copied, 1)
            for b in range(NB):
                act.wait_ge(zx_ready, b + 1)
                nc.scalar.copy(zx[:, b, :], pg.bank[2 + b % 2][:, :]).then_inc(zx_copied, 1)
            act.wait_ge(sp_in, 1)
            nc.scalar.activation(eu[:, :, :, :], au[:, :, :, :], ACT.Exp, scale=-1.0).then_inc(sp_exp, 1)
            act.wait_ge(sp_exp, 1)
            nc.scalar.activation(lu[:, :, :, :], eu[:, :, :, :], ACT.Ln, bias=1.0).then_inc(sp_ln, 1)
            act.wait_ge(adt_ready, 1)
            nc.scalar.activation(sh_in[:, 0, :], logd[:, :, :].rearrange("p b h -> p (b h)"), ACT.Exp).then_inc(shift_in, 1)
            act.wait_ge(sg_done, 1)
            nc.scalar.activation(te[:, :, :], tr[:, :, :], ACT.Sigmoid).then_inc(dec_done, 1)
            act.wait_ge(trig_in, 1)
            nc.scalar.activation(trig[:, :, :, :].rearrange("p k b n -> p (k b n)"),
                                 rem[:, :, :].rearrange("p k n -> p (k n)"), ACT.Sin).then_inc(trig_done, 1)
            act.wait_ge(zx_copied, NB)
            nc.scalar.activation(sz[:, :, :], zx[:, :, 0:DI], ACT.Silu).then_inc(silu_done, 1)

        @block.vector
        def _(dve):
            o = Order(dve, order_sem)
            V = nc.vector
            norm_all(pg, dve, o, st, mv, ve, var_ready, rstd_ready, rs, xn, xn_ready)
            for b in range(NB):
                dve.wait_ge(small_ready, b + 1)
                V.tensor_copy(sm[:, b, :], pg.bank[4 + b % 2][:, 0:NBC]).then_inc(small_copied, 1)
            dve.wait_ge(small_copied, NB)
            dve.wait_ge(par_in, 16 * 6)
            V.tensor_tensor(u[:, :, 0, :], sm[:, :, 2 * NS:2 * NS + SH],
                            bc(dtb[:, :].unsqueeze(1), [P, NB, SH]), ALU.add).then_inc(order_sem, 1)
            o.n += 1
            o.after(V.tensor_copy(u[:, :, 1, :], sm[:, :, 2 * NS + SH:2 * NS + 2 * SH]))
            V.scalar_tensor_tensor(au[:, :, :, :].rearrange("p b k h -> p (b k h)"), u[:, :, :, :].rearrange("p b k h -> p (b k h)"),
                                   -1.0, u[:, :, :, :].rearrange("p b k h -> p (b k h)"), ALU.mult, ALU.max).then_inc(sp_in, 1)
            V.tensor_copy(tr[:, :, :], sm[:, :, 2 * NS + 2 * SH:AN]).then_inc(sg_done, 1)
            for b in range(NB):
                for k in range(2):
                    o.mark(V.bn_stats(bst[:, b, k, :], sm[:, b, k * NS:(k + 1) * NS]))
            o.wait()
            for b in range(NB):
                for k in range(2):
                    o.mark(V.bn_aggr(bmv[:, b, k, :], bst[:, b, k, :]))
            o.wait()
            V.tensor_scalar(bve[:, :], bmv[:, :, :, 1].rearrange("p b k -> p (b k)"), EPS, None,
                            ALU.add).then_inc(bc_var_ready, 1)
            dve.wait_ge(sp_ln, 1)
            o.after(V.scalar_tensor_tensor(pu[:, :, :, :].rearrange("p b k h -> p (b k h)"), u[:, :, :, :].rearrange("p b k h -> p (b k h)"),
                                           0.0, lu[:, :, :, :].rearrange("p b k h -> p (b k h)"), ALU.max, ALU.add))
            dt = pu[:, :, 0, :]
            o.mark(V.tensor_scalar(au[:, :, 1, :], pu[:, :, 1, :], -1.0, -1e-4, ALU.mult, ALU.min))
            o.after(V.tensor_reduce(dtm[:, :, 0], dt, AX, ALU.add))
            V.tensor_tensor(logd[:, :, :], au[:, :, 1, :], dt, ALU.mult).then_inc(adt_ready, 1)
            o.after(V.tensor_scalar(dtm[:, :, :], dtm[:, :, :], 1.0 / SH, None, ALU.mult))
            V.tensor_tensor(ang[:, :, :], sm[:, :, AN:], bc(dtm[:, :, :], [P, NB, NA]), ALU.mult).then_inc(phase_in, 1)
            dve.wait_ge(dec_done, 1)
            o.after(V.tensor_tensor(now[:, :, :], te[:, :, :], dt, ALU.mult))
            V.tensor_tensor(sh_in[:, 1, :].rearrange("p (b h) -> p b h", b=NB), dt, now[:, :, :],
                            ALU.subtract).then_inc(shift_in, 1)
            MAGIC, TP = 1.5 * 2.0 ** 23, 2 * np.pi
            HI = 6.28125
            ph = pg.bank[6][:, 0:NB * NA]
            dve.wait_ge(phase_ready, 1)
            for k in range(2):
                o.mark(V.tensor_scalar(turns[:, k, :], ph, 1 / TP, 0.25 * k, ALU.mult, ALU.add))
            o.wait()
            o.after(V.tensor_scalar(turns[:, :, :], turns[:, :, :], MAGIC, None, ALU.add))
            o.after(V.tensor_scalar(turns[:, :, :], turns[:, :, :], -MAGIC, None, ALU.add))
            for k in range(2):
                o.mark(V.scalar_tensor_tensor(rem[:, k, :], turns[:, k, :], -HI, ph, ALU.mult, ALU.add))
            o.wait()
            o.after(V.scalar_tensor_tensor(rem[:, :, :].rearrange("p k n -> p (k n)"), turns[:, :, :].rearrange("p k n -> p (k n)"),
                                           -(TP - HI), rem[:, :, :].rearrange("p k n -> p (k n)"), ALU.mult, ALU.add))
            o.after(V.tensor_scalar(rem[:, 1, :], rem[:, 1, :], TP / 4, None, ALU.add))
            PI = float(np.nextafter(np.float32(np.pi), np.float32(0)))
            V.tensor_scalar(rem[:, :, :], rem[:, :, :], PI, -PI, ALU.min, ALU.max).then_inc(trig_in, 1)
            dve.wait_ge(bc_rstd_ready, 1)
            o.after(V.tensor_tensor(bn[:, :, :, :], sm[:, :, 0:2 * NS].rearrange("p b (k n) -> p b k n", k=2),
                                    bc(bmv[:, :, :, 0:1], [P, NB, 2, NS]), ALU.subtract))
            o.after(V.tensor_tensor(bn[:, :, :, :], bn[:, :, :, :],
                                    bc(brs[:, :].rearrange("p (b k) -> p b k", b=NB).unsqueeze(3), [P, NB, 2, NS]), ALU.mult))
            for k, op in ((0, ALU.mult), (1, ALU.add)):
                o.after(V.tensor_tensor(bn[:, :, :, :], bn[:, :, :, :],
                                        bc(gb[:, k:k + 1, :, :], [P, NB, 2, NS]), op))
            dve.wait_ge(trig_done, 1)
            sin, cos = trig[:, 0, :, :], trig[:, 1, :, :]
            for k in range(2):
                ev = bn[:, :, k, 0:NS:2]
                od = bn[:, :, k, 1:NS:2]
                o.mark(V.tensor_tensor(r0[:, :, :], ev, cos, ALU.mult))
                o.mark(V.tensor_tensor(r1[:, :, :], od, sin, ALU.mult))
                o.mark(V.tensor_tensor(r2[:, :, :], ev, sin, ALU.mult))
                o.after(V.tensor_tensor(r3[:, :, :], od, cos, ALU.mult))
                o.mark(V.tensor_tensor(br[:, :, k, 0:NS:2], r0[:, :, :], r1[:, :, :], ALU.subtract))
                o.after(V.tensor_tensor(br[:, :, k, 1:NS:2], r2[:, :, :], r3[:, :, :], ALU.add))
            o.after(V.tensor_tensor(cb[:, :, :], br[:, :, 0, :], br[:, :, 1, :], ALU.mult))
            o.after(V.tensor_reduce(cbd[:, :, 0], cb[:, :, :], AX, ALU.add))
            dve.wait_ge(shifted, 1)
            nd = pg.bank[7][:, 0:2 * NB * SH].rearrange("p (k b h) -> p k b h", k=2, b=NB)
            o.after(V.tensor_tensor(past[:, :, :], nd[:, 0], now[:, :, :], ALU.mult))
            o.mark(V.tensor_tensor(past[:, :, :], nd[:, 1], past[:, :, :], ALU.add))
            o.after(V.tensor_tensor(now[:, :, :], now[:, :, :], bc(cbd[:, :, :], [P, NB, SH]), ALU.mult))
            o.after(V.tensor_tensor(now[:, :, :], now[:, :, :], bc(dpar[:, :].unsqueeze(1), [P, NB, SH]), ALU.add))


def state_space_mix(pg, zx, sz, br, logd, past, now, upper, strict, after, w_out, w_out_in):
    nc = pg.nc
    with ExitStack() as ctx:
        (bc_in, rl_in, bct_ready, bct_copied, cb_ready, lg_ready, cbm_done, e_done, g_done, xs_done, y_ready,
         y_done, yt_ready, yt_copied, o_ready, order_sem) = pg.sems("sm", (
            "bc_in rl_in bct_ready bct_copied cb_ready decay_sum_ready cb_masked decay_done mix_ready xs_done y_ready "
            "y_done yt_ready yt_copied out_ready order"))
        two = lambda n, s: [pg.sbuf(f"sm_{n}{p}", s, ctx=ctx) for p in range(2)]
        bcs, bct = two("bcs", [P, 3 * NS]), two("bct", [NS, 2, P])
        rl, e, g = two("rl", [P, SH, P]), two("e", [P, SH, P]), two("g", [P, SH, P])
        cbm, xs = two("cbm", [P, P]), two("xs", [P, SH, NS])
        t1, y, yt = two("t1", [P, SH, NS]), two("y", [P, DI]), two("yt", [P, 2, P])
        block = ctx.enter_context(nc.Block())

        @block.gpsimd
        def _(pool):
            with pool.Fori(0, NB // 2) as i:
                for p in range(2):
                    pool.wait_ge(bct_ready, 4 * i)
                    nc.gpsimd.tensor_copy(bcs[p][:, 0:2 * NS], br[:, 2 * i + p].rearrange("p k n -> p (k n)")).then_inc(bc_in, 1)
                    nc.gpsimd.tensor_copy(bcs[p][:, 2 * NS:], br[:, 2 * i + p, 0, :]).then_inc(bc_in, 1)

        @block.tensor
        def _(pe):
            pe.wait_ge(w_out_in, 16)
            with pe.Fori(0, NB // 2) as i:
                for p in range(2):
                    A = pg.bank[p]
                    pe.wait_ge(bc_in, 4 * i + 2 * p + 2)
                    pe.wait_ge(order_sem, 8 * i)
                    for k in range(2):
                        nc.tensor.transpose(A[:, k * P:(k + 1) * P], bcs[p][:, k * NS:k * NS + P],
                                            pg.ident[:, :]).then_inc(bct_ready, 1)
                for p in range(2):
                    pe.wait_ge(rl_in, 2 * i + p + 1)
                    nc.tensor.matmul(pg.bank[2 + p][:, :], after[:, :], rl[p][:, :, :].rearrange("p h l -> p (h l)"),
                                     start=True, stop=True).then_inc(lg_ready, 1)
                for p in range(2):
                    pe.wait_ge(bct_copied, 2 * i + p + 1)
                    nc.tensor.matmul(pg.bank[p][:, 256:384], bct[p][:, 0, :], bct[p][:, 1, :],
                                     start=True, stop=True).then_inc(cb_ready, 1)
                for p in range(2):
                    pe.wait_ge(g_done, 2 * i + p + 1)
                    pe.wait_ge(xs_done, 2 * i + p + 1)
                    for h in range(SH):
                        mm = nc.tensor.matmul(pg.bank[4 + p][:, h * NS:(h + 1) * NS], g[p][:, h, :], xs[p][:, h, :],
                                              start=True, stop=True)
                    mm.then_inc(y_ready, 1)
                for p in range(2):
                    pe.wait_ge(y_done, 2 * i + p + 1)
                    for t in range(2):
                        nc.tensor.transpose(pg.bank[4 + p][:, DI + t * P:DI + (t + 1) * P], y[p][:, t * P:(t + 1) * P],
                                            pg.ident[:, :]).then_inc(yt_ready, 1)
                for p in range(2):
                    pe.wait_ge(yt_copied, 2 * i + p + 1)
                    for t in range(2):
                        mm = nc.tensor.matmul(pg.bank[p][:, 384:512], yt[p][:, t, :], w_out[:, t, :],
                                              start=(t == 0), stop=(t == 1))
                    mm.then_inc(o_ready, 1)

        @block.scalar
        def _(act):
            with act.Fori(0, NB // 2) as i:
                for p in range(2):
                    act.wait_ge(bct_ready, 4 * i + 2 * p + 2)
                    nc.scalar.copy(bct[p][:, :, :].rearrange("n k l -> n (k l)"),
                                   pg.bank[p][0:NS, 0:2 * P]).then_inc(bct_copied, 1)
                for p in range(2):
                    act.wait_ge(lg_ready, 2 * i + p + 1)
                    nc.scalar.activation(e[p][:, :, :].rearrange("p h l -> p (h l)"), pg.bank[2 + p][:, :],
                                         ACT.Exp).then_inc(e_done, 1)
                for p in range(2):
                    act.wait_ge(yt_ready, 4 * i + 2 * p + 2)
                    nc.scalar.copy(yt[p][:, :, :].rearrange("p t l -> p (t l)"),
                                   pg.bank[4 + p][:, DI:2 * DI]).then_inc(yt_copied, 1)

        @block.vector
        def _(dve):
            V = nc.vector
            with dve.Fori(0, NB // 2) as i:
                o = Order(dve, order_sem, i, 8)
                for p in range(2):
                    j = 2 * i + p
                    V.tensor_tensor(rl[p][:, :, :], bc(upper[:, :].unsqueeze(1), [P, SH, P]),
                                    bc(logd[:, j].unsqueeze(2), [P, SH, P]), ALU.mult).then_inc(rl_in, 1)
                for p in range(2):
                    j = 2 * i + p
                    xj = zx[:, j, DI:2 * DI].rearrange("p (h n) -> p h n", h=SH)
                    V.tensor_tensor(xs[p][:, :, :], xj, bc(past[:, j].unsqueeze(2), [P, SH, NS]),
                                    ALU.mult).then_inc(xs_done, 1)
                    o.mark(V.tensor_tensor(t1[p][:, :, :], xj, bc(now[:, j].unsqueeze(2), [P, SH, NS]), ALU.mult))
                for p in range(2):
                    dve.wait_ge(cb_ready, 2 * i + p + 1)
                    o.mark(V.tensor_tensor(cbm[p][:, :], pg.bank[p][:, 256:384], strict[:, :], ALU.mult))
                for p in range(2):
                    dve.wait_ge(e_done, 2 * i + p + 1)
                    o.wait(3 + p)
                    V.tensor_tensor(g[p][:, :, :], e[p][:, :, :], bc(cbm[p][:, :].unsqueeze(1), [P, SH, P]),
                                    ALU.mult).then_inc(g_done, 1)
                for p in range(2):
                    j = 2 * i + p
                    t = t1[p][:, :, :].rearrange("p h n -> p (h n)")
                    dve.wait_ge(y_ready, j + 1)
                    o.after(V.tensor_tensor(t, pg.bank[4 + p][:, 0:DI], t, ALU.add))
                    V.tensor_tensor(y[p][:, :], t, sz[:, j, :], ALU.mult).then_inc(y_done, 1)
                for p in range(2):
                    dve.wait_ge(o_ready, 2 * i + p + 1)
                    o.mark(V.tensor_tensor(pg.x[:, 2 * i + p, :], pg.bank[p][:, 384:512], pg.x[:, 2 * i + p, :], ALU.add))
                o.per = o.n
                assert o.n == 8


def cross_weights(pg, ctx, layer):
    w = {n: pg.sbuf(f"c{layer}_{n}", [P if n in "qo" else DC, INNER], ctx=ctx) for n in "qkvo"}
    w["o"] = w["o"][:, :].rearrange("p (t d) -> p t d", t=NT)
    w["bias"] = pg.sbuf(f"c{layer}_bias", [P, D], ctx=ctx)
    if layer:
        w["vw"] = pg.sbuf("c1_vw", [NH * IPA, NB, D], ctx=ctx)
        w["k_ipa"] = pg.sbuf("c1_k_ipa", [DC, INNER], ctx=ctx)
    return w


def load_cross_weights(pg, sp, w, layer, done):
    a, n = pg.a, 0
    if layer == 0:
        kv = a["L0_xattn_w_kv"]
        parts = [(w["q"][:, :], a["L0_xattn_w_q"]), (w["k"][:, :], kv[:, 0:INNER]), (w["v"][:, :], kv[:, INNER:])]
        wo, bias = a["L0_xattn_w_out"], a["L0_xattn_b_out"]
    else:
        parts = [(w[c][:, :], a["L1_xattn_W" + c]) for c in "qkv"] + [(w["k_ipa"][:, :], a["L1_xattn_Wk_ipa"])]
        wo, bias = a["L1_xattn_Wo"], a["L1_xattn_bo"]
    parts += [(w["o"], wo.rearrange("(t p) d -> p t d", p=P)), (w["bias"][:, :], bias.partition_broadcast(P))]
    for dst, src in parts:
        sp.dma_start(dst, src).then_inc(done, 16)
        n += 16
    return n


def fold_low_rank(pg, w):
    nc, a = pg.nc, pg.a
    R = 32
    with ExitStack() as ctx:
        loaded, tr_ready, tr_copied, prod_ready, folded, v2_ready, v2_spread, zeroed, vw_ready, vw_copied, vt_ready, vt_copied, order_sem = pg.sems(
            "fl", "loaded down_transposed down_copied product_ready folded image_v_ready image_v_spread zeroed "
            "vw_ready vw_copied vw_transposed vw_done order")
        down = {n: pg.sbuf(f"fl_down_{n}", [P if n == "q" else DC, R], ctx=ctx) for n in "qkv"}
        down_o = pg.sbuf("fl_down_o", [P, NT, R], ctx=ctx)
        up = {n: pg.sbuf(f"fl_up_{n}", [R, D if n == "o" else INNER], ctx=ctx) for n in "qkvo"}
        alpha = pg.sbuf("fl_alpha", [P, 4], ctx=ctx)
        down_t = {n: pg.sbuf(f"fl_down_t_{n}", [R, INNER if n == "o" else P], ctx=ctx) for n in "qkvo"}
        wv_ipa = pg.sbuf("fl_wv_ipa", [DC, INNER], ctx=ctx)
        v2 = pg.sbuf("fl_v2", [P, NT, 2, NB * IPA], ctx=ctx)
        vwt = pg.sbuf("fl_vwt", [P, NT, 2, NB * IPA], ctx=ctx)
        vwb = pg.sbuf("fl_vwb", [P, NB, NH, IPA], ctx=ctx)
        block = ctx.enter_context(nc.Block())

        @block.sync
        def _(sp):
            n = load_cross_weights(pg, sp, w, 1, loaded)
            for c in "qkv":
                sp.dma_start(down[c][:, :], a[f"L1_xattn_{c}_down"]).then_inc(loaded, 16)
            sp.dma_start(down_o[:, :, :], a["L1_xattn_o_down"].rearrange("(t p) r -> p t r", p=P)).then_inc(loaded, 16)
            for m, c in enumerate("qkvo"):
                sp.dma_start(up[c][:, :], a[f"L1_xattn_{c}_up"]).then_inc(loaded, 16)
                sp.dma_start(alpha[:, m:m + 1], a[f"L1_xattn_{c}_alpha"].partition_broadcast(P)).then_inc(loaded, 16)
            sp.dma_start(wv_ipa[:, :], a["L1_xattn_Wv_ipa"]).then_inc(loaded, 16)

        LOADS = 16 * (6 + 3 + 1 + 8 + 1)

        @block.gpsimd
        def _(pool):
            nc.gpsimd.memset(v2[:, :, :, :], 0.0).then_inc(zeroed, 1)

        @block.tensor
        def _(pe):
            pe.wait_ge(loaded, LOADS)
            for m, c in enumerate("qkv"):
                rows = P if c == "q" else DC
                nc.tensor.transpose(pg.bank[0][0:R, m * P:m * P + rows], down[c][:, :],
                                    pg.ident[0:rows, 0:rows]).then_inc(tr_ready, 1)
            for t in range(NT):
                nc.tensor.transpose(pg.bank[1 + t // 4][0:R, (t % 4) * P:(t % 4 + 1) * P], down_o[:, t, :],
                                    pg.ident[:, :]).then_inc(tr_ready, 1)
            pe.wait_ge(tr_copied, 5)
            for m, c in enumerate("qkvo"):
                for h in range(2):
                    k = 2 * m + h
                    if k >= 4:
                        pe.wait_ge(folded, k - 3)
                    if c != "o":
                        rows = P if c == "q" else DC
                        mm = nc.tensor.matmul(pg.bank[3 + k % 4][0:rows, :], down_t[c][:, 0:rows],
                                              up[c][:, 512 * h:512 * (h + 1)], start=True, stop=True)
                    else:
                        for t in range(4):
                            mm = nc.tensor.matmul(pg.bank[3 + k % 4][:, t * P:(t + 1) * P],
                                                  down_t[c][:, (4 * h + t) * P:(4 * h + t + 1) * P], up[c][:, :],
                                                  start=True, stop=True)
                    mm.then_inc(prod_ready, 1)
            for t in range(NT):
                mm = nc.tensor.matmul(pg.bank[7][:, t * NB * IPA:(t + 1) * NB * IPA], wv_ipa[:, t * P:(t + 1) * P],
                                      pg.ctx_t[:, 0:NB, P - IPA:P], start=True, stop=True)
            mm.then_inc(v2_ready, 1)
            pe.wait_ge(v2_spread, 2)
            pe.wait_ge(folded, 8)
            pe.wait_ge(tr_copied, 5)
            for t in range(NT):
                mm = nc.tensor.matmul(pg.bank[0][:, t * 64:(t + 1) * 64], w["o"][:, t, :],
                                      v2[:, t, :, :].rearrange("p g n -> p (g n)"), start=True, stop=True)
            mm.then_inc(vw_ready, 1)
            pe.wait_ge(vw_copied, 1)
            for b in range(NB):
                nc.tensor.transpose(pg.bank[1 + b // 4][0:NH * IPA, (b % 4) * P:(b % 4 + 1) * P],
                                    vwb[:, b, :, :].rearrange("p h k -> p (h k)"), pg.ident[:, :]).then_inc(vt_ready, 1)

        @block.scalar
        def _(act):
            for m, c in enumerate("qkv"):
                rows = P if c == "q" else DC
                act.wait_ge(tr_ready, 3)
                nc.scalar.copy(down_t[c][:, 0:rows], pg.bank[0][0:R, m * P:m * P + rows]).then_inc(tr_copied, 1)
            for h in range(2):
                act.wait_ge(tr_ready, 3 + 4 * h + 4)
                nc.scalar.copy(down_t["o"][:, 512 * h:512 * (h + 1)], pg.bank[1 + h][0:R, :]).then_inc(tr_copied, 1)
            for h in range(2):
                act.wait_ge(vt_ready, 4 * h + 4)
                nc.scalar.copy(w["vw"][:, 4 * h:4 * h + 4, :].rearrange("n b d -> n (b d)"),
                               pg.bank[1 + h][0:NH * IPA, :]).then_inc(vt_copied, 1)

        @block.vector
        def _(dve):
            o = Order(dve, order_sem)
            dve.wait_ge(loaded, LOADS)
            o.after(nc.vector.tensor_scalar(alpha[:, :], alpha[:, :], 1.0 / R, None, ALU.mult))
            for m, c in enumerate("qkvo"):
                for h in range(2):
                    k = 2 * m + h
                    rows = P if c in "qo" else DC
                    dst = w["o"][:, 4 * h:4 * h + 4, :].rearrange("p t d -> p (t d)") if c == "o" else w[c][:, 512 * h:512 * (h + 1)]
                    dve.wait_ge(prod_ready, k + 1)
                    nc.vector.scalar_tensor_tensor(dst, pg.bank[3 + k % 4][0:rows, :], alpha[0:rows, m:m + 1], dst,
                                                   ALU.mult, ALU.add).then_inc(folded, 1)
            dve.wait_ge(v2_ready, 1)
            dve.wait_ge(zeroed, 1)
            for g in range(2):
                rows = slice(64 * g, 64 * g + 64)
                nc.vector.tensor_copy(v2[rows, :, g, :], pg.bank[7][rows, 0:NT * NB * IPA].rearrange(
                    "p (t n) -> p t n", t=NT)).then_inc(v2_spread, 1)
            dve.wait_ge(vw_ready, 1)
            nc.vector.tensor_copy(vwb[:, :, :, :], pg.bank[0][:, :].rearrange("p (h b k) -> p b h k", h=NH, b=NB)).then_inc(vw_copied, 1)


def cross_attention(pg, w, layer, loads_done=None, loads=0):
    nc = pg.nc
    KS = P - IPA if layer else P
    with ExitStack() as ctx:
        (var_ready, rstd_ready, xn_ready, xt_ready, xt_copied, c_ready, q_ready, q_copied, k_ready, k_copied, v_ready,
         v_copied, s_ready, s_read, nm_ready, nmt_ready, nmt_copied, st_ready, exp_done, av_ready, o_done, ot_ready,
         ot_copied, out_ready, x_done, ones_done, order_sem, pm_ready, pe_done, p2_ready, p2t_ready, p2t_copied) = pg.sems(f"ca{layer}", (
            "var_ready rstd_ready xn_ready xt_ready xt_copied c_ready q_ready q_copied k_ready k_copied v_ready "
            "v_copied s_ready s_read max_ready max_transposed max_copied st_ready exp_done av_ready o_done ot_ready "
            "ot_copied out_ready x_done ones_done order image_shifted image_exp_done image_p_ready image_p_transposed image_p_copied"))
        sb = lambda n, s, dt=F32: pg.sbuf(f"ca{layer}_{n}", s, dt, ctx=ctx)
        st, mv, ve, rs, xn = sb("st", [P, 6]), sb("mv", [P, 2]), sb("ve", [P, 1]), sb("rs", [P, 1]), sb("xn", [P, D])
        xt, ct = sb("xt", [P, P]), sb("ct", [DC, P])
        qt, kt = sb("qt", [P, NT, P]), sb("kt", [P, NT, P])
        v = sb("v", [P, NH, VS])
        m, nm = sb("m", [P, NH]), sb("nm", [P, P // NH, NH], BF16)
        nmt = sb("nmt", [P, P], BF16)
        pt = sb("pt", [P, NCH, HPC * P])
        rinv, on = sb("rinv", [P, NH]), sb("on", [P, NH, HD])
        ot = sb("ot", [P, NT, P])
        s2, m2, sum2, p2t = sb("s2", [P, NH, IPA]), sb("m2", [P, NH]), sb("sum2", [P, NH]), sb("p2t", [NH * IPA, P])
        proj = pg.bank[0:2]
        score = pg.bank[2:4]
        av = pg.bank[4:6]
        xc_bank, misc = pg.bank[6], pg.bank[7]
        nmt_ps = misc[:, 256:512].bitcast(BF16)[:, 0:P]
        p2t_ps = misc[0:NH * IPA, P:2 * P]
        SCALE = HD ** -0.5
        order_per = 10 if layer else 7
        block = ctx.enter_context(nc.Block())

        def heads_of(c):
            return slice(2 * HPC * (c // 2) + c % 2, 2 * HPC * (c // 2 + 1), 2)

        def head(c, r):
            return 2 * HPC * (c // 2) + c % 2 + 2 * r

        def qrow(t, h):
            return t[64 * (h % 2):64 * (h % 2) + 64, h // 2, :]

        @block.gpsimd
        def _(pool):
            nc.gpsimd.memset(v[:, :, HD:VS], 1.0).then_inc(ones_done, 1)
            nc.gpsimd.memset(nm[:, 2:, :], 0.0).then_inc(ones_done, 1)

            def rstd(j):
                pool.wait_ge(var_ready, j + 1)
                nc.gpsimd.tensor_tensor(rs[:, :], ve[:, :], pg.neg_half[:, 0:1], ALU.pow).then_inc(rstd_ready, 1)

            nc.gpsimd.tensor_copy(ct[:, :], pg.ctx_t[:, 0, :]).then_inc(c_ready, 1)
            rstd(0)
            with pool.Fori(0, NB) as j:
                rstd(j + 1)
                pool.wait_ge(v_ready, 2 * j + 2)
                nc.gpsimd.tensor_copy(ct[:, :], pg.ctx_t[:, j + 1, :]).then_inc(c_ready, 1)

        @block.tensor
        def _(pe):
            def x_transpose(j):
                pe.wait_ge(xn_ready, j + 1)
                nc.tensor.transpose(xc_bank[:, 0:P], xn[:, :], pg.ident[:, :]).then_inc(xt_ready, 1)

            def project_q(j, free):
                pe.wait_ge(xt_copied, j + 1)
                for h in range(2):
                    if free is not None:
                        pe.wait_ge(v_copied, 2 * free + h + 1)
                    for t in range(4):
                        mm = nc.tensor.matmul(proj[h][:, t * P:(t + 1) * P],
                                              w["q"][:, (4 * h + t) * P:(4 * h + t + 1) * P], xt[:, :], start=True, stop=True)
                    mm.then_inc(q_ready, 1)

            def project_k(j):
                pe.wait_ge(c_ready, j + 1)
                for h in range(2):
                    pe.wait_ge(q_copied, 2 * j + h + 1)
                    for t in range(4):
                        cols = slice((4 * h + t) * P, (4 * h + t + 1) * P)
                        mm = nc.tensor.matmul(proj[h][:, t * P:t * P + KS], w["k"][:, cols], ct[:, 0:KS],
                                              start=True, stop=True)
                        if layer:
                            mm = nc.tensor.matmul(proj[h][:, t * P + KS:(t + 1) * P], w["k_ipa"][:, cols],
                                                  ct[:, KS:P], start=True, stop=True)
                    mm.then_inc(k_ready, 1)

            pe.wait_ge(ones_done, 2)
            if loads_done is not None:
                pe.wait_ge(loads_done, loads)
            x_transpose(0)
            project_q(0, None)
            project_k(0)
            with pe.Fori(0, NB) as j:
                pe.wait_ge(k_copied, 2 * j + 2)
                for c in range(NCH):
                    if c < 2:
                        pe.wait_ge(exp_done, NCH * j)
                    else:
                        pe.wait_ge(s_read, NCH * j + c - 1)
                    for r in range(HPC):
                        h = head(c, r)
                        mm = nc.tensor.matmul(score[c % 2][:, r * P:(r + 1) * P], qrow(qt, h), qrow(kt, h),
                                              start=True, stop=True)
                    mm.then_inc(s_ready, 1)
                for h in range(2):
                    pe.wait_ge(ot_copied, 2 * j)
                    nc.tensor.matmul(proj[h][0:KS, :], ct[:, 0:KS], w["v"][:, 512 * h:512 * (h + 1)],
                                     start=True, stop=True).then_inc(v_ready, 1)
                x_transpose(j + 1)
                pe.wait_ge(x_done, j)
                pe.wait_ge(nm_ready, 2 * j + 2)
                nc.tensor.transpose(nmt_ps, nm[:, :, :].rearrange("p k h -> p (k h)"), pg.ident_bf[:, :]).then_inc(nmt_ready, 1)

                def scores_t(c):
                    if c < 2:
                        pe.wait_ge(s_read, NCH * j + c + 3)
                    else:
                        pe.wait_ge(exp_done, NCH * j + c - 1)
                    if c == 0:
                        pe.wait_ge(nmt_copied, j + 1)
                    for r in range(HPC):
                        h = head(c, r)
                        dst = score[c % 2][0:KS, r * P:(r + 1) * P]
                        nc.tensor.matmul(dst, qrow(kt, h)[:, 0:KS], qrow(qt, h), start=True, stop=False)
                        mm = nc.tensor.matmul(dst, pg.sel[:, h, 0:KS], nmt[:, :], start=False, stop=True)
                    mm.then_inc(st_ready, 1)

                def values(c):
                    if c < 2:
                        pe.wait_ge(o_done, NCH * j)
                    else:
                        pe.wait_ge(o_done, NCH * j + c - 1)
                    if c == 0:
                        pe.wait_ge(v_copied, 2 * j + 2)
                    pe.wait_ge(exp_done, NCH * j + c + 1)
                    for r in range(HPC):
                        mm = nc.tensor.matmul(av[c % 2][:, r * VS:(r + 1) * VS], pt[0:KS, c, r * P:(r + 1) * P],
                                              v[0:KS, head(c, r), :], start=True, stop=True)
                    mm.then_inc(av_ready, 1)

                for c in range(NCH):
                    scores_t(c)
                    if c >= 1:
                        values(c - 1)
                values(NCH - 1)
                if layer:
                    pe.wait_ge(p2_ready, j + 1)
                project_q(j + 1, j)
                if layer:
                    nc.tensor.transpose(p2t_ps, s2[:, :, :].rearrange("p h k -> p (h k)"), pg.ident[:, :]).then_inc(p2t_ready, 1)
                project_k(j + 1)
                for h in range(2):
                    pe.wait_ge(k_copied, 2 * j + 2 + h + 1)
                    pe.wait_ge(o_done, NCH * j + 2 * h + 2)
                    for t in range(4):
                        mm = nc.tensor.transpose(proj[h][:, t * P:(t + 1) * P],
                                                 on[:, 8 * h + 2 * t:8 * h + 2 * t + 2, :].rearrange("p h d -> p (h d)"),
                                                 pg.ident[:, :])
                    mm.then_inc(ot_ready, 1)
                if layer:
                    pe.wait_ge(p2t_copied, j + 1)
                for t in range(NT):
                    if t % 4 == 0:
                        pe.wait_ge(ot_copied, 2 * j + t // 4 + 1)
                    mm = nc.tensor.matmul(misc[:, 0:D], ot[:, t, :], w["o"][:, t, :], start=(t == 0),
                                          stop=(t == NT - 1 and not layer))
                if layer:
                    mm = nc.tensor.matmul(misc[:, 0:D], p2t[:, :], w["vw"][:, j, :], start=False, stop=True)
                mm.then_inc(out_ready, 1)

        @block.scalar
        def _(act):
            def copy_q(j):
                for h in range(2):
                    act.wait_ge(q_ready, 2 * j + h + 1)
                    nc.scalar.mul(qt[:, 4 * h:4 * h + 4, :].rearrange("p t l -> p (t l)"), proj[h][:, :],
                                  SCALE).then_inc(q_copied, 1)

            def copy_xt(j):
                act.wait_ge(xt_ready, j + 1)
                nc.scalar.copy(xt[:, :], xc_bank[:, 0:P]).then_inc(xt_copied, 1)

            copy_xt(0)
            copy_q(0)
            act.wait_ge(ones_done, 2)
            with act.Fori(0, NB) as j:
                for h in range(2):
                    act.wait_ge(v_ready, 2 * j + h + 1)
                    nc.scalar.copy(v[0:KS, 8 * h:8 * h + 8, 0:HD], proj[h][0:KS, :].rearrange(
                        "p (h d) -> p h d", d=HD)).then_inc(v_copied, 1)
                copy_xt(j + 1)
                act.wait_ge(nmt_ready, j + 1)
                nc.scalar.copy(nmt[:, :], nmt_ps).then_inc(nmt_copied, 1)
                if layer:
                    act.wait_ge(pm_ready, j + 1)
                    nc.scalar.activation(s2[:, :, :], s2[:, :, :], ACT.Exp).then_inc(pe_done, 1)
                for c in range(NCH):
                    act.wait_ge(st_ready, NCH * j + c + 1)
                    nc.scalar.activation(pt[0:KS, c, :], score[c % 2][0:KS, :], ACT.Exp).then_inc(exp_done, 1)
                copy_q(j + 1)
                if layer:
                    act.wait_ge(p2t_ready, j + 1)
                    nc.scalar.copy(p2t[:, :], p2t_ps).then_inc(p2t_copied, 1)
                for h in range(2):
                    act.wait_ge(ot_ready, 2 * j + h + 1)
                    nc.scalar.copy(ot[:, 4 * h:4 * h + 4, :].rearrange("p t l -> p (t l)"),
                                   proj[h][:, :]).then_inc(ot_copied, 1)

        @block.vector
        def _(dve):
            V = nc.vector

            def norm_stats(j, o):
                o.after(V.bn_aggr(mv[:, :], st[:, :]))
                V.tensor_scalar(ve[:, :], mv[:, 1:2], EPS, None, ALU.add).then_inc(var_ready, 1)

            def norm_apply(j):
                dve.wait_ge(rstd_ready, j + 1)
                V.tensor_scalar(xn[:, :], pg.x[:, j, :], mv[:, 0:1], rs[:, 0:1], ALU.subtract,
                                ALU.mult).then_inc(xn_ready, 1)

            def copy_k(j):
                for h in range(2):
                    dve.wait_ge(k_ready, 2 * j + h + 1)
                    V.tensor_copy(kt[:, 4 * h:4 * h + 4, :].rearrange("p t k -> p (t k)"),
                                  proj[h][:, :]).then_inc(k_copied, 1)

            first = Order(dve, order_sem)
            first.after(V.bn_stats(st[:, :], pg.x[:, 0, :]))
            norm_stats(0, first)
            norm_apply(0)
            copy_k(0)
            with dve.Fori(0, NB) as j:
                o = Order(dve, order_sem, j, order_per)
                o.n = first.n
                o.after(V.bn_stats(st[:, :], pg.x[:, j + 1, :]))
                for c in range(NCH):
                    dve.wait_ge(s_ready, NCH * j + c + 1)
                    s = score[c % 2][:, :].rearrange("p (h k) -> p h k", k=P)
                    heads = heads_of(c)
                    V.tensor_reduce(m[:, heads], s[:, :, 0:KS], AX, ALU.max, negate=True).then_inc(s_read, 1) if not layer else \
                        V.tensor_reduce(m[:, heads], s[:, :, 0:KS], AX, ALU.max, negate=True)
                    if layer:
                        V.tensor_copy(s2[:, heads, :], s[:, :, KS:P]).then_inc(s_read, 1)
                    if c == 0:
                        norm_stats(j + 1, o)
                    if c == 1:
                        norm_apply(j + 1)
                dve.wait_ge(s_read, NCH * j + NCH)
                V.tensor_copy(nm[:, 0, :], m[:, :]).then_inc(nm_ready, 1)
                dve.wait_ge(nm_ready, 2 * j + 1)
                V.tensor_tensor(nm[:, 1, :], m[:, :], nm[:, 0, :], ALU.subtract).then_inc(nm_ready, 1)
                if layer:
                    o.after(V.tensor_reduce(m2[:, :], s2[:, :, :], AX, ALU.max))
                    V.tensor_tensor(s2[:, :, :], s2[:, :, :], bc(m2[:, :].unsqueeze(2), [P, NH, IPA]),
                                    ALU.subtract).then_inc(pm_ready, 1)
                    dve.wait_ge(pe_done, j + 1)
                    o.after(V.tensor_reduce(sum2[:, :], s2[:, :, :], AX, ALU.add))
                    o.after(V.reciprocal(sum2[:, :], sum2[:, :]))
                    V.tensor_tensor(s2[:, :, :], s2[:, :, :], bc(sum2[:, :].unsqueeze(2), [P, NH, IPA]),
                                    ALU.mult).then_inc(p2_ready, 1)
                for c in range(NCH):
                    dve.wait_ge(av_ready, NCH * j + c + 1)
                    heads = heads_of(c)
                    src = av[c % 2][:, 0:HPC * VS].rearrange("p (h e) -> p h e", e=VS)
                    o.after(V.reciprocal(rinv[:, heads].unsqueeze(2), src[:, :, HD:HD + 1]))
                    V.tensor_tensor(on[:, heads, :], src[:, :, 0:HD], bc(rinv[:, heads].unsqueeze(2), [P, HPC, HD]),
                                    ALU.mult).then_inc(o_done, 1)
                copy_k(j + 1)
                dve.wait_ge(out_ready, j + 1)
                o.after(V.tensor_tensor(pg.x[:, j, :], misc[:, 0:D], pg.x[:, j, :], ALU.add))
                V.tensor_tensor(pg.x[:, j, :], pg.x[:, j, :], w["bias"][:, :], ALU.add).then_inc(x_done, 1)
                o.n -= first.n
                o.close()


def self_attention(pg):
    nc, a = pg.nc, pg.a
    G, R, W = 4, 4, 8
    VW = W + 2
    SCALE = W ** -0.5
    with ExitStack() as ctx:
        (loaded, wt_ready, zeroed, wt_copied, iota_done, alibi_order, alibi_done, var_ready, rstd_ready, xn_ready, xt_ready, xt_copied,
         q_ready, q_copied, k_ready, k_copied, v_ready, v_copied, s_ready, s_read, nm_ready, nmt_ready, nmt_copied,
         st_ready, st_read, exp_done, av_ready, o_done, ot_ready, ot_copied, out_ready, x_done, order_sem) = pg.sems("sa", (
            "loaded wt_ready zeroed wt_copied iota_done alibi_order alibi_done var_ready rstd_ready xn_ready xt_ready xt_copied "
            "q_ready q_copied k_ready k_copied v_ready v_copied s_ready s_read max_ready max_transposed max_copied "
            "st_ready st_read exp_done av_ready o_done ot_ready ot_copied out_ready x_done order"))
        sb = lambda n, s, dt=F32: pg.sbuf(f"sa_{n}", s, dt, ctx=ctx)
        w_nat = sb("w_nat", [P, 4, D])
        wq, wk = sb("wq", [P, G, R, 32]), sb("wk", [P, G, R, 32])
        wv, wo = sb("wv", [P, D]), sb("wo", [P, D])
        bq, bk = sb("bq", [P, G]), sb("bk", [P, G])
        bv, bo = sb("bv", [P, D]), sb("bo", [P, D])
        dist_i, dist = sb("dist_i", [P, P], mybir.dt.int32), sb("dist", [P, P])
        alibi = sb("alibi", [P, R, G, P])
        st, mv, ve, rs, xn = sb("st", [P, 6]), sb("mv", [P, 2]), sb("ve", [P, 1]), sb("rs", [P, 1]), sb("xn", [P, D])
        xt = sb("xt", [P, P])
        qt, kt = sb("qt", [P, G, P]), sb("kt", [P, G, P])
        v = sb("v", [P, NH, VW])
        t = sb("t", [P, 2, G, P])
        m, nm, nmt = sb("m", [P, NH]), sb("nm", [P, P // NH, NH], BF16), sb("nmt", [P, P], BF16)
        pre, pt = sb("pre", [P, R, G, P]), sb("pt", [P, R, G, P])
        rinv, on, ot = sb("rinv", [P, NH]), sb("on", [P, D]), sb("ot", [P, P])
        proj, score, av, xc_bank, misc = pg.bank[0:2], pg.bank[2:4], pg.bank[4], pg.bank[6], pg.bank[7]
        nmt_ps = misc[:, 256:512].bitcast(BF16)[:, 0:P]
        block = ctx.enter_context(nc.Block())

        @block.sync
        def _(sp):
            sp.dma_start(w_nat[:, 0:3, :], a["L1_attn_W_qkv"].rearrange("(t p) d -> p t d", p=P)).then_inc(loaded, 16)
            sp.dma_start(w_nat[:, 3, :], a["L1_attn_W_out"]).then_inc(loaded, 16)
            sp.dma_start(bv[:, :], a["L1_attn_b_qkv"][2 * D:3 * D].partition_broadcast(P)).then_inc(loaded, 16)
            sp.dma_start(bo[:, :], a["L1_attn_b_out"].partition_broadcast(P)).then_inc(loaded, 16)
            sp.wait_ge(zeroed, 4)
            for k, dst in enumerate((bq, bk)):
                src = a["L1_attn_b_qkv"][k * D:(k + 1) * D].rearrange("(g r w) -> r w g", g=G, r=R)
                with nc.allow_non_contiguous_dma("bias columns"):
                    for r in range(R):
                        sp.dma_start(dst[32 * r:32 * r + W, :], src[r]).then_inc(loaded, 16)

        LOADS = 16 * 12

        @block.gpsimd
        def _(pool):
            for z in (wq, wk):
                nc.gpsimd.memset(z[:, :, :, :], 0.0).then_inc(zeroed, 1)
            for z in (bq, bk):
                nc.gpsimd.memset(z[:, :], 0.0).then_inc(zeroed, 1)
            nc.gpsimd.memset(v[:, :, W:VW], 1.0).then_inc(zeroed, 1)
            nc.gpsimd.memset(nm[:, 2:, :], 0.0).then_inc(zeroed, 1)
            nc.gpsimd.iota(dist_i[:, :], pattern=[[-1, P]], base=0, channel_multiplier=1).then_inc(iota_done, 1)

            def rstd(j):
                pool.wait_ge(var_ready, j + 1)
                nc.gpsimd.tensor_tensor(rs[:, :], ve[:, :], pg.neg_half[:, 0:1], ALU.pow).then_inc(rstd_ready, 1)

            rstd(0)
            with pool.Fori(0, NB) as j:
                rstd(j + 1)

        @block.tensor
        def _(pe):
            pe.wait_ge(loaded, LOADS)
            for k in range(4):
                nc.tensor.transpose(misc[:, k * P:(k + 1) * P], w_nat[:, k, :], pg.ident[:, :]).then_inc(wt_ready, 1)

            def x_transpose(j):
                pe.wait_ge(xn_ready, j + 1)
                nc.tensor.transpose(xc_bank[:, 0:P], xn[:, :], pg.ident[:, :]).then_inc(xt_ready, 1)

            def project(j):
                pe.wait_ge(xt_copied, j + 1)
                for g in range(G):
                    mm = nc.tensor.matmul(proj[0][:, g * P:(g + 1) * P], wq[:, g, :, :].rearrange("p r w -> p (r w)"),
                                          xt[:, :], start=True, stop=True)
                mm.then_inc(q_ready, 1)
                for g in range(G):
                    mm = nc.tensor.matmul(proj[1][:, g * P:(g + 1) * P], wk[:, g, :, :].rearrange("p r w -> p (r w)"),
                                          xt[:, :], start=True, stop=True)
                mm.then_inc(k_ready, 1)
                nc.tensor.matmul(xc_bank[:, 256:256 + D], xt[:, :], wv[:, :], start=True, stop=True).then_inc(v_ready, 1)

            x_transpose(0)
            pe.wait_ge(wt_copied, 4)
            project(0)
            with pe.Fori(0, NB) as j:
                pe.wait_ge(q_copied, j + 1)
                pe.wait_ge(k_copied, j + 1)
                for r in range(R):
                    if r < 2:
                        pe.wait_ge(st_read, R * j)
                    else:
                        pe.wait_ge(s_read, R * j + r - 1)
                    rows = slice(32 * r, 32 * r + W)
                    for g in range(G):
                        mm = nc.tensor.matmul(score[r % 2][:, g * P:(g + 1) * P], qt[rows, g, :], kt[rows, g, :],
                                              start=True, stop=True)
                    mm.then_inc(s_ready, 1)
                pe.wait_ge(v_copied, j + 1)
                x_transpose(j + 1)
                pe.wait_ge(x_done, j)
                pe.wait_ge(nm_ready, 2 * j + 2)
                nc.tensor.transpose(nmt_ps, nm[:, :, :].rearrange("p k h -> p (k h)"), pg.ident_bf[:, :]).then_inc(nmt_ready, 1)

                def scores_t(r):
                    if r < 2:
                        pe.wait_ge(s_read, R * j + r + 3)
                    else:
                        pe.wait_ge(st_read, R * j + r - 1)
                    if r == 0:
                        pe.wait_ge(nmt_copied, j + 1)
                    rows = slice(32 * r, 32 * r + W)
                    for g in range(G):
                        dst = score[r % 2][:, g * P:(g + 1) * P]
                        nc.tensor.matmul(dst, kt[rows, g, :], qt[rows, g, :], start=True, stop=False)
                        mm = nc.tensor.matmul(dst, pg.sel[:, G * r + g, :], nmt[:, :], start=False, stop=True)
                    mm.then_inc(st_ready, 1)

                def values(r):
                    if r == 0:
                        pe.wait_ge(o_done, j)
                    pe.wait_ge(exp_done, R * j + r + 1)
                    for g in range(G):
                        h = R * g + r
                        mm = nc.tensor.matmul(av[:, h * VW:(h + 1) * VW], pt[:, r, g, :], v[:, h, :], start=True, stop=True)
                    mm.then_inc(av_ready, 1)

                for r in range(R):
                    scores_t(r)
                    if r >= 2:
                        values(r - 2)
                values(R - 2)
                values(R - 1)
                project(j + 1)
                pe.wait_ge(q_copied, j + 2)
                pe.wait_ge(o_done, j + 1)
                nc.tensor.transpose(proj[0][:, 0:P], on[:, :], pg.ident[:, :]).then_inc(ot_ready, 1)
                pe.wait_ge(ot_copied, j + 1)
                nc.tensor.matmul(misc[:, 0:D], ot[:, :], wo[:, :], start=True, stop=True).then_inc(out_ready, 1)

        @block.scalar
        def _(act):
            def copy_xt(j):
                act.wait_ge(xt_ready, j + 1)
                nc.scalar.copy(xt[:, :], xc_bank[:, 0:P]).then_inc(xt_copied, 1)

            copy_xt(0)
            with act.Fori(0, NB) as j:
                copy_xt(j + 1)
                act.wait_ge(nmt_ready, j + 1)
                nc.scalar.copy(nmt[:, :], nmt_ps).then_inc(nmt_copied, 1)
                for r in range(R):
                    act.wait_ge(st_read, R * j + r + 1)
                    nc.scalar.activation(pt[:, r, :, :], pre[:, r, :, :], ACT.Exp).then_inc(exp_done, 1)
                act.wait_ge(ot_ready, j + 1)
                nc.scalar.copy(ot[:, :], proj[0][:, 0:P]).then_inc(ot_copied, 1)

        @block.vector
        def _(dve):
            V = nc.vector
            o0 = Order(dve, alibi_order)
            dve.wait_ge(iota_done, 1)
            o0.after(V.tensor_copy(dist[:, :], dist_i[:, :]))
            o0.after(V.scalar_tensor_tensor(dist[:, :], dist[:, :], -1.0, dist[:, :], ALU.mult, ALU.max))
            for h in range(NH):
                V.tensor_scalar(alibi[:, h % R, h // R, :], dist[:, :], -float(np.float32(2.0 ** (-8.0 * h / NH))), None,
                                ALU.mult).then_inc(alibi_done, 1)
            dve.wait_ge(zeroed, 6)
            dve.wait_ge(wt_ready, 4)
            for k, dst in enumerate((wq, wk)):
                V.tensor_copy(dst[:, :, :, 0:W], misc[:, k * P:(k + 1) * P].rearrange("p (g r w) -> p g r w", g=G, r=R)).then_inc(wt_copied, 1)
            for k, dst in enumerate((wv, wo)):
                V.tensor_copy(dst[:, :], misc[:, (2 + k) * P:(3 + k) * P]).then_inc(wt_copied, 1)

            def norm_stats(j, o):
                o.after(V.bn_aggr(mv[:, :], st[:, :]))
                V.tensor_scalar(ve[:, :], mv[:, 1:2], EPS, None, ALU.add).then_inc(var_ready, 1)

            def norm_apply(j):
                dve.wait_ge(rstd_ready, j + 1)
                V.tensor_scalar(xn[:, :], pg.x[:, j, :], mv[:, 0:1], rs[:, 0:1], ALU.subtract,
                                ALU.mult).then_inc(xn_ready, 1)

            def copy_qkv(j):
                for ready, src, bias, dst, done in ((q_ready, proj[0], bq, qt, q_copied), (k_ready, proj[1], bk, kt, k_copied)):
                    dve.wait_ge(ready, j + 1)
                    V.tensor_tensor(dst[:, :, :], src[:, :].rearrange("p (g l) -> p g l", g=G),
                                    bc(bias[:, :].unsqueeze(2), [P, G, P]), ALU.add).then_inc(done, 1)
                dve.wait_ge(v_ready, j + 1)
                V.tensor_tensor(v[:, :, 0:W], xc_bank[:, 256:256 + D].rearrange("p (h w) -> p h w", w=W),
                                bv[:, :].rearrange("p (h w) -> p h w", w=W), ALU.add).then_inc(v_copied, 1)

            first = Order(dve, order_sem)
            first.after(V.bn_stats(st[:, :], pg.x[:, 0, :]))
            norm_stats(0, first)
            norm_apply(0)
            dve.wait_ge(loaded, LOADS)
            copy_qkv(0)
            dve.wait_ge(alibi_done, NH)
            with dve.Fori(0, NB) as j:
                o = Order(dve, order_sem, j, 9)
                o.n = first.n
                o.after(V.bn_stats(st[:, :], pg.x[:, j + 1, :]))
                for r in range(R):
                    dve.wait_ge(s_ready, R * j + r + 1)
                    V.scalar_tensor_tensor(t[:, r % 2, :, :].rearrange("p g k -> p (g k)"), score[r % 2][:, :], SCALE,
                                           alibi[:, r, :, :].rearrange("p g k -> p (g k)"), ALU.mult, ALU.add).then_inc(s_read, 1)
                    if r == 0:
                        norm_stats(j + 1, o)
                    if r == 1:
                        norm_apply(j + 1)
                    dve.wait_ge(s_read, R * j + r + 1)
                    o.mark(V.tensor_reduce(m[:, G * r:G * r + G], t[:, r % 2, :, :], AX, ALU.max, negate=True))
                o.wait()
                o.after(V.tensor_scalar(m[:, :], m[:, :], 1.0 / SCALE, None, ALU.mult))
                V.tensor_copy(nm[:, 0, :], m[:, :]).then_inc(nm_ready, 1)
                dve.wait_ge(nm_ready, 2 * j + 1)
                V.tensor_tensor(nm[:, 1, :], m[:, :], nm[:, 0, :], ALU.subtract).then_inc(nm_ready, 1)
                for r in range(R):
                    dve.wait_ge(st_ready, R * j + r + 1)
                    V.scalar_tensor_tensor(pre[:, r, :, :].rearrange("p g k -> p (g k)"), score[r % 2][:, :], SCALE,
                                           alibi[:, r, :, :].rearrange("p g k -> p (g k)"), ALU.mult, ALU.add).then_inc(st_read, 1)
                dve.wait_ge(av_ready, R * j + R)
                src = av[:, 0:NH * VW].rearrange("p (h e) -> p h e", e=VW)
                o.after(V.reciprocal(rinv[:, :].unsqueeze(2), src[:, :, W:W + 1]))
                V.tensor_tensor(on[:, :].rearrange("p (h w) -> p h w", w=W), src[:, :, 0:W],
                                bc(rinv[:, :].unsqueeze(2), [P, NH, W]), ALU.mult).then_inc(o_done, 1)
                copy_qkv(j + 1)
                dve.wait_ge(out_ready, j + 1)
                o.after(V.tensor_tensor(pg.x[:, j, :], misc[:, 0:D], pg.x[:, j, :], ALU.add))
                V.tensor_tensor(pg.x[:, j, :], pg.x[:, j, :], bo[:, :], ALU.add).then_inc(x_done, 1)
                o.n -= first.n
                o.close()


def feed_forward(pg, layer):
    with ExitStack() as ctx:
        xt = pg.sbuf(f"ff{layer}_xt", [P, NB, P], ctx=ctx)
        cw = pg.sbuf(f"ff{layer}_cw", [P, NE, NB], ctx=ctx)
        route(pg, layer, xt, cw)
        experts(pg, layer, xt, cw)


def route(pg, layer, xt, cw):
    nc, a = pg.nc, pg.a
    K = 2 if layer else 1
    with ExitStack() as ctx:
        (loaded, var_ready, rstd_ready, xn_ready, xt_ready, xt_copied, wt_ready, wt_copied, lg_ready, sub_done, e_done,
         ones_done, lower_done, order_sem) = pg.sems(f"rt{layer}", (
            "loaded var_ready rstd_ready xn_ready xt_ready xt_copied wt_ready wt_copied logits_ready shifted exp_done "
            "ones_done lower_done order"))
        sb = lambda n, s: pg.sbuf(f"rt{layer}_{n}", s, ctx=ctx)
        st, mv, ve, rs, xn = norm_all_buffers(pg, ctx, f"rt{layer}")
        w = sb("w", [P, K * NE])
        w_nat = sb("w_nat", [NE, D])
        lg, mx, sm = sb("lg", [P, NB, K, NE]), sb("mx", [P, NB, K]), sb("sm", [P, NB, K])
        pr = sb("pr", [P, NB, K, NE])
        lower = sb("lower", [P, NE, NE])
        gt, eq, rank = sb("gt", [P, NB, NE, NE]), sb("eq", [P, NB, NE, NE]), sb("rank", [P, NB, NE])
        block = ctx.enter_context(nc.Block())

        @block.sync
        def _(sp):
            if layer:
                with nc.allow_non_contiguous_dma("router weights"):
                    sp.dma_start(w[:, 0:NE], a["L1_ffn_w_router"]).then_inc(loaded, 16)
                    sp.dma_start(w[:, NE:2 * NE], a["L1_ffn_w_gating"]).then_inc(loaded, 16)
            else:
                sp.dma_start(w_nat[:, :], a["L0_ffn_router_w"]).then_inc(loaded, 16)

        @block.gpsimd
        def _(pool):
            nc.gpsimd.memset(lower[:, :, :], 1.0).then_inc(ones_done, 1)
            pool.wait_ge(ones_done, 1)
            nc.gpsimd.affine_select(out=lower[:, :, :], in_=lower[:, :, :], compare_op=ALU.is_gt, fill=0.0, base=0,
                                    pattern=[[1, NE], [-1, NE]], channel_multiplier=0).then_inc(lower_done, 1)
            pool.wait_ge(var_ready, 1)
            nc.gpsimd.tensor_tensor(rs[:, :], ve[:, :], pg.neg_half[:, :], ALU.pow).then_inc(rstd_ready, 1)

        @block.tensor
        def _(pe):
            pe.wait_ge(loaded, 16 * K)
            if not layer:
                nc.tensor.transpose(pg.bank[3][:, 0:NE], w_nat[:, :], pg.ident[0:NE, 0:NE]).then_inc(wt_ready, 1)
            for b in range(NB):
                pe.wait_ge(xn_ready, b + 1)
                nc.tensor.transpose(pg.bank[b // 4][:, (b % 4) * P:(b % 4 + 1) * P], xn[:, b, :],
                                    pg.ident[:, :]).then_inc(xt_ready, 1)
            if not layer:
                pe.wait_ge(wt_copied, 1)
            for b in range(NB):
                pe.wait_ge(xt_copied, b // 4 + 1)
                mm = nc.tensor.matmul(pg.bank[2][:, b * K * NE:(b + 1) * K * NE], xt[:, b, :], w[:, :],
                                      start=True, stop=True)
            mm.then_inc(lg_ready, 1)

        @block.scalar
        def _(act):
            if not layer:
                act.wait_ge(wt_ready, 1)
                nc.scalar.copy(w[:, :], pg.bank[3][:, 0:NE]).then_inc(wt_copied, 1)
            for h in range(2):
                act.wait_ge(xt_ready, 4 * h + 4)
                nc.scalar.copy(xt[:, 4 * h:4 * h + 4, :].rearrange("p b l -> p (b l)"),
                               pg.bank[h][:, :]).then_inc(xt_copied, 1)
            act.wait_ge(sub_done, 1)
            nc.scalar.activation(lg[:, :, :, :], lg[:, :, :, :], ACT.Exp).then_inc(e_done, 1)

        @block.vector
        def _(dve):
            o, V = Order(dve, order_sem), nc.vector
            norm_all(pg, dve, o, st, mv, ve, var_ready, rstd_ready, rs, xn, xn_ready)
            dve.wait_ge(lg_ready, 1)
            src = pg.bank[2][:, 0:NB * K * NE].rearrange("p (b k e) -> p b k e", b=NB, k=K)
            for k in range(K):
                o.mark(V.tensor_scalar(lg[:, :, k, :], src[:, :, k, :], 10.0 if k else 1.0, None, ALU.mult))
            o.wait()
            o.after(V.tensor_reduce(mx[:, :, :], lg[:, :, :, :], AX, ALU.max))
            V.tensor_tensor(lg[:, :, :, :], lg[:, :, :, :], bc(mx[:, :, :].unsqueeze(3), [P, NB, K, NE]),
                            ALU.subtract).then_inc(sub_done, 1)
            dve.wait_ge(e_done, 1)
            o.after(V.tensor_reduce(sm[:, :, :], lg[:, :, :, :], AX, ALU.add))
            o.after(V.reciprocal(sm[:, :, :], sm[:, :, :]))
            o.after(V.tensor_tensor(pr[:, :, :, :], lg[:, :, :, :], bc(sm[:, :, :].unsqueeze(3), [P, NB, K, NE]), ALU.mult))
            cw_be = cw[:, :, :].rearrange("p e b -> p b e")
            if layer:
                both = pr[:, :, 0, :]
                o.after(V.tensor_tensor(both, both, pr[:, :, 1, :], ALU.mult))
                o.after(V.tensor_reduce(rank[:, :, 0], both, AX, ALU.add))
                o.after(V.tensor_scalar(rank[:, :, 0], rank[:, :, 0], 1e-9, None, ALU.add))
                o.after(V.reciprocal(rank[:, :, 0], rank[:, :, 0]))
                o.after(V.tensor_tensor(cw_be, both, bc(rank[:, :, 0:1], [P, NB, NE]), ALU.mult))
            else:
                dve.wait_ge(lower_done, 1)
                other = bc(pr[:, :, 0:1, :], [P, NB, NE, NE])
                own = bc(pr[:, :, 0, :].unsqueeze(3), [P, NB, NE, NE])
                o.mark(V.tensor_tensor(gt[:, :, :, :], other, own, ALU.is_gt))
                o.after(V.tensor_tensor(eq[:, :, :, :], other, own, ALU.is_equal))
                o.after(V.tensor_tensor(eq[:, :, :, :], eq[:, :, :, :], bc(lower[:, :, :].unsqueeze(1), [P, NB, NE, NE]), ALU.mult))
                o.after(V.tensor_tensor(gt[:, :, :, :], gt[:, :, :, :], eq[:, :, :, :], ALU.add))
                o.after(V.tensor_reduce(rank[:, :, :], gt[:, :, :, :], AX, ALU.add))
                o.after(V.tensor_scalar(rank[:, :, :], rank[:, :, :], 1.5, None, ALU.is_lt))
                o.after(V.tensor_tensor(cw_be, rank[:, :, :], pr[:, :, 0, :], ALU.mult))


def experts(pg, layer, xt, cw):
    nc, a = pg.nc, pg.a
    FT = 4 if layer else 2
    TB = HALF // P
    F = FT * P
    with ExitStack() as ctx:
        (w_in_even, w_in_odd, wt_ready, wt_copied, gu_ready, act_done, h_done, y_ready, x_done) = pg.sems(f"ex{layer}", (
            "even_weights_in odd_weights_in weights_transposed weights_copied gate_up_ready act_done h_done y_ready x_done"))
        sb = lambda n, s: pg.sbuf(f"ex{layer}_{n}", s, ctx=ctx)
        gate = [sb(f"gate{p}", [P, F]) for p in range(2)]
        up = [sb(f"up{p}", [P, F]) for p in range(2)]
        down = [sb(f"down{p}", [P, FT, D]) for p in range(2)]
        if not layer:
            w1 = [sb(f"w1_{p}", [P, 2 * FT, D]) for p in range(2)]
            w2 = [sb(f"w2_{p}", [P, F]) for p in range(2)]
        s = sb("s", [P, 2, HALF])
        h = [sb(f"h{n}", [P, FT, HALF]) for n in range(2)]
        gate_ps, up_ps, y_ps, wt_ps = pg.bank[0:2], pg.bank[2:4], pg.bank[4:6], pg.bank[6:8]
        flat = xt[:, :, :].rearrange("p b l -> p (b l)")
        w_in = (w_in_even, w_in_odd)
        N_W = 3 if layer else 2
        PER = 2 * FT
        block = ctx.enter_context(nc.Block())

        @block.sync
        def _(sp):
            def load(e, p):
                if layer:
                    sp.dma_start(gate[p][:, :], a["L1_ffn_w_gate"][e]).then_inc(w_in[p], 16)
                    sp.dma_start(up[p][:, :], a["L1_ffn_w_up"][e]).then_inc(w_in[p], 16)
                    sp.dma_start(down[p][:, :, :], a["L1_ffn_w_down"][e].rearrange("(t p) d -> p t d", p=P)).then_inc(w_in[p], 16)
                else:
                    sp.dma_start(w1[p][:, :, :], a["L0_ffn_w1"][e].rearrange("(t p) d -> p t d", p=P)).then_inc(w_in[p], 16)
                    sp.dma_start(w2[p][:, :], a["L0_ffn_w2"][e]).then_inc(w_in[p], 16)

            for p in range(2):
                load(p, p)
            with sp.Fori(1, NE // 2) as i:
                for p in range(2):
                    if layer:
                        sp.wait_ge(y_ready, 4 * i + 2 * p - 2)
                    else:
                        sp.wait_ge(wt_ready, (2 * i + p - 1) * 3 * FT)
                    load(2 * i + p, p)

        @block.tensor
        def _(pe):
            with pe.Fori(0, NE // 2) as i:
                for p in range(2):
                    e = 2 * i + p
                    pe.wait_ge(w_in[p], 16 * N_W * i + 16 * N_W)
                    if not layer:
                        pe.wait_ge(wt_copied, 3 * e)
                        for t in range(2 * FT):
                            nc.tensor.transpose(wt_ps[0][:, t * P:(t + 1) * P], w1[p][:, t, :], pg.ident[:, :]).then_inc(wt_ready, 1)
                        for t in range(FT):
                            nc.tensor.transpose(wt_ps[1][:, t * P:(t + 1) * P], w2[p][:, t * P:(t + 1) * P], pg.ident[:, :]).then_inc(wt_ready, 1)
                        pe.wait_ge(wt_copied, 3 * e + 3)

                    def hidden(n, t):
                        k = n * FT + t
                        pe.wait_ge(h_done, PER * e if k < 2 else PER * e + k - 1)
                        cols = slice(n * HALF, (n + 1) * HALF)
                        nc.tensor.matmul(gate_ps[k % 2][:, :], gate[p][:, t * P:(t + 1) * P], flat[:, cols], start=True, stop=True)
                        nc.tensor.matmul(up_ps[k % 2][:, :], up[p][:, t * P:(t + 1) * P], flat[:, cols], start=True,
                                         stop=True).then_inc(gu_ready, 1)

                    def output(n):
                        pe.wait_ge(h_done, PER * e + (n + 1) * FT)
                        pe.wait_ge(x_done, 2 * e)
                        for b in range(TB):
                            for t in range(FT):
                                mm = nc.tensor.matmul(y_ps[n][:, b * D:(b + 1) * D], h[n][:, t, b * P:(b + 1) * P],
                                                      down[p][:, t, :], start=(t == 0), stop=(t == FT - 1))
                        mm.then_inc(y_ready, 1)

                    for t in range(FT):
                        hidden(0, t)
                    hidden(1, 0)
                    output(0)
                    for t in range(1, FT):
                        hidden(1, t)
                    output(1)

        @block.scalar
        def _(act):
            with act.Fori(0, NE // 2) as i:
                for p in range(2):
                    e = 2 * i + p
                    if not layer:
                        act.wait_ge(wt_ready, 3 * FT * e + 2 * FT)
                        nc.scalar.copy(gate[p][:, :], wt_ps[0][:, 0:F]).then_inc(wt_copied, 1)
                        nc.scalar.copy(up[p][:, :], wt_ps[0][:, F:2 * F]).then_inc(wt_copied, 1)
                        act.wait_ge(wt_ready, 3 * FT * e + 3 * FT)
                        nc.scalar.copy(down[p][:, :, :].rearrange("p t d -> p (t d)"), wt_ps[1][:, 0:F]).then_inc(wt_copied, 1)
                    for k in range(PER):
                        act.wait_ge(gu_ready, PER * e + k + 1)
                        nc.scalar.activation(s[:, k % 2, :], gate_ps[k % 2][:, :], ACT.Silu).then_inc(act_done, 1)

        @block.vector
        def _(dve):
            V = nc.vector
            with dve.Fori(0, NE // 2) as i:
                for p in range(2):
                    e = 2 * i + p

                    def add(n):
                        dve.wait_ge(y_ready, 2 * e + n + 1)
                        if n == 0:
                            dve.wait_ge(x_done, 2 * e)
                        for b in range(TB):
                            ins = V.scalar_tensor_tensor(pg.x[:, n * TB + b, :], y_ps[n][:, b * D:(b + 1) * D],
                                                         cw[:, e, n * TB + b:n * TB + b + 1], pg.x[:, n * TB + b, :], ALU.mult, ALU.add)
                        ins.then_inc(x_done, 1)

                    for k in range(PER):
                        dve.wait_ge(act_done, PER * e + k + 1)
                        V.tensor_tensor(h[k // FT][:, k % FT, :], s[:, k % 2, :], up_ps[k % 2][:, :], ALU.mult).then_inc(h_done, 1)
                        if k == FT + 1:
                            add(0)
                    add(1)


def cross(pg, layer):
    with ExitStack() as ctx:
        w = cross_weights(pg, ctx, layer)
        if layer:
            fold_low_rank(pg, w)
        else:
            loaded, = pg.sems("cw0", "loaded")
            with pg.nc.Block() as block:
                @block.sync
                def _(sp):
                    n = load_cross_weights(pg, sp, w, 0, loaded)
                    sp.wait_ge(loaded, n)
        cross_attention(pg, w, layer)


def store(pg):
    nc = pg.nc
    with ExitStack() as ctx:
        out_done, = pg.sems("st", "out_done")
        block = ctx.enter_context(nc.Block())

        @block.sync
        def _(sp):
            sp.dma_start(pg.out.rearrange("b l d -> l b d"), pg.x[:, 0:NB, :]).then_inc(out_done, 16)
            sp.wait_ge(out_done, 16)


def decoder(nc, a, out):
    with ExitStack() as ctx:
        pg = Program(nc, ctx, a, out)
        setup(pg)
        state_space(pg)
        cross(pg, 0)
        feed_forward(pg, 0)
        self_attention(pg)
        pg.recycle_sems()
        cross(pg, 1)
        feed_forward(pg, 1)
        store(pg)


_INS = [
    'x', 'ctx_768', 'L0_attn_W_in', 'L0_attn_W_out', 'L0_attn_dt_bias', 'L0_attn_D_param', 'L0_attn_Bn_g',
    'L0_attn_Bn_b', 'L0_attn_Cn_g', 'L0_attn_Cn_b', 'L0_xattn_w_q', 'L0_xattn_w_kv', 'L0_xattn_w_out',
    'L0_xattn_b_out', 'L0_ffn_w1', 'L0_ffn_w2', 'L0_ffn_router_w', 'L1_attn_W_qkv', 'L1_attn_b_qkv',
    'L1_attn_W_out', 'L1_attn_b_out', 'L1_xattn_Wq', 'L1_xattn_Wk', 'L1_xattn_Wv', 'L1_xattn_Wo', 'L1_xattn_bo',
    'L1_xattn_q_down', 'L1_xattn_q_up', 'L1_xattn_q_alpha', 'L1_xattn_k_down', 'L1_xattn_k_up',
    'L1_xattn_k_alpha', 'L1_xattn_v_down', 'L1_xattn_v_up', 'L1_xattn_v_alpha', 'L1_xattn_o_down',
    'L1_xattn_o_up', 'L1_xattn_o_alpha', 'L1_xattn_Wk_ipa', 'L1_xattn_Wv_ipa', 'L1_ffn_w_router',
    'L1_ffn_w_gating', 'L1_ffn_w_gate', 'L1_ffn_w_up', 'L1_ffn_w_down'
]
_OUT_SHAPE = (NB, P, D)


def kernel(**inputs):
    import concourse.bacc as _bacc
    from concourse import mybir as _mybir
    from concourse.bass_utils import run_bass_kernel_spmd as _run

    nc = _bacc.Bacc("TRN2", target_bir_lowering=False, num_devices=1)
    arrays, args = {}, {}
    for name in _INS:
        v = np.ascontiguousarray(inputs[name])
        arrays[f"in_{name}_dram"] = v
        args[name] = nc.dram_tensor(f"in_{name}_dram", v.shape, _mybir.dt.from_np(v.dtype), kind="ExternalInput").ap()
    out = nc.dram_tensor("out_0_dram", _OUT_SHAPE, _mybir.dt.float32, kind="ExternalOutput").ap()
    decoder(nc, args, out)
    r = _run(nc, [arrays], core_ids=[0])
    return r.results[0]["out_0_dram"]
```

```python
from contextlib import ExitStack

import numpy as np

import concourse.bass as bass
from concourse import mybir

F32 = mybir.dt.float32
BF16 = mybir.dt.bfloat16
ALU = mybir.AluOpType
ACT = mybir.ActivationFunctionType
AX = mybir.AxisListType.X

P = 128
NB = 8
D = 128
DC = 96
EPS = 1e-5
NH = 16
HD = 64
INNER = NH * HD
NT = INNER // P
VS = HD + 2
NCH = 4
HPC = NH // NCH
NE = 8
HALF = NB * P // 2
IPA = 4
DI = 256
SH = 4
NS = 64
NA = 32


class Order:

    def __init__(self, eng, sem, i=0, per=0):
        self.eng, self.sem, self.i, self.per, self.n = eng, sem, i, per, 0

    def mark(self, ins):
        ins.then_inc(self.sem, 1)
        self.n += 1
        return self.n

    def wait(self, n=None):
        self.eng.wait_ge(self.sem, self.i * self.per + (self.n if n is None else n))

    def after(self, ins):
        self.mark(ins)
        self.wait()

    def close(self):
        assert self.n == self.per, f"the body has {self.n} ordered steps"


def bc(ap, shape):
    return ap.to_broadcast(list(shape))


class Program:

    def __init__(self, nc, ctx, a, out):
        self.nc, self.ctx, self.a, self.out = nc, ctx, a, out
        sb, self.sb = self.sbuf, self.sbuf
        self.bank = [ctx.enter_context(nc.psum_tensor(f"bank{n}", [P, 512], F32)) for n in range(8)]
        self.x = sb("x", [P, NB + 1, D])
        self.ctx_t = sb("ctx_t", [DC, NB + 1, P])
        self.ident = sb("ident", [P, P])
        self.ident_bf = sb("ident_bf", [P, P], BF16)
        self.sel = sb("sel", [P, NH, P], BF16)
        self.live_sems = []
        self.neg_half = sb("neg_half", [P, NB])
        self.zero = sb("zero", [P, 1])

    def sbuf(self, name, shape, dt=F32, ctx=None):
        return (ctx or self.ctx).enter_context(self.nc.sbuf_tensor("sb_" + name, shape, dt))

    def sems(self, prefix, names):
        got = [self.nc.alloc_semaphore(name=f"{prefix}_{n}") for n in names.split()]
        self.live_sems += got
        return got

    def recycle_sems(self):
        self.nc.clear_and_free_semaphores(self.live_sems)
        self.live_sems = []
        self.nc.all_engine_barrier()


def setup(pg):
    nc, a = pg.nc, pg.a
    with ExitStack() as ctx:
        x_in, ctx_in, zeroed, const_done, ctx_tr, ctx_cp = pg.sems(
            "su", "x_in ctx_in zeroed const_done ctx_transposed ctx_copied")
        ctx_sb = pg.sbuf("ctx_sb", [P, NB, DC], ctx=ctx)
        block = ctx.enter_context(nc.Block())

        @block.sync
        def _(sp):
            sp.dma_start(ctx_sb[:, :, :], a["ctx_768"].rearrange("b k c -> k b c")).then_inc(ctx_in, 16)
            sp.dma_start(pg.x[:, 0:NB, :], a["x"].rearrange("b l d -> l b d")).then_inc(x_in, 16)
            sp.wait_ge(x_in, 16)

        @block.gpsimd
        def _(pool):
            for n, t in enumerate((pg.ident, pg.ident_bf, pg.sel)):
                nc.gpsimd.memset(t[:], 0.0).then_inc(zeroed, 1)
            nc.gpsimd.memset(pg.neg_half[:, :], -0.5).then_inc(const_done, 1)
            nc.gpsimd.memset(pg.zero[:, :], 0.0).then_inc(const_done, 1)
            nc.gpsimd.memset(pg.x[:, NB, :], 0.0).then_inc(const_done, 1)
            nc.gpsimd.memset(pg.ctx_t[:, NB, :], 0.0).then_inc(const_done, 1)
            pool.wait_ge(zeroed, 3)
            for t in (pg.ident, pg.ident_bf):
                nc.gpsimd.affine_select(out=t[:, :], in_=t[:, :], compare_op=ALU.not_equal, fill=1.0,
                                        base=0, pattern=[[-1, P]], channel_multiplier=1).then_inc(const_done, 1)
            for part in range(2):
                pool.wait_ge(const_done, 6 + part)
                nc.gpsimd.affine_select(out=pg.sel[:, :, :], in_=pg.sel[:, :, :], compare_op=ALU.not_equal,
                                        fill=1.0, base=-part * NH, pattern=[[-1, NH], [0, P]],
                                        channel_multiplier=1).then_inc(const_done, 1)

        @block.tensor
        def _(pe):
            pe.wait_ge(const_done, 6)
            pe.wait_ge(ctx_in, 16)
            for b in range(NB):
                nc.tensor.transpose(pg.bank[b // 4][0:DC, (b % 4) * P:(b % 4 + 1) * P], ctx_sb[:, b, :],
                                    pg.ident[:, :]).then_inc(ctx_tr, 1)

        @block.scalar
        def _(act):
            for h in range(2):
                act.wait_ge(ctx_tr, 4 * h + 4)
                nc.scalar.copy(pg.ctx_t[:, 4 * h:4 * h + 4, :].rearrange("c b k -> c (b k)"),
                               pg.bank[h][0:DC, :]).then_inc(ctx_cp, 1)


def norm_all(pg, dve, order, st, mv, ve, var_ready, rstd_ready, rs, xn, xn_ready):
    nc = pg.nc
    for b in range(NB):
        order.mark(nc.vector.bn_stats(st[:, b, :], pg.x[:, b, :]))
    for b in range(NB):
        order.wait(b + 1)
        order.mark(nc.vector.bn_aggr(mv[:, b, :], st[:, b, :]))
    order.wait()
    nc.vector.tensor_scalar(ve[:, :], mv[:, :, 1], EPS, None, ALU.add).then_inc(var_ready, 1)
    dve.wait_ge(rstd_ready, 1)
    for b in range(NB):
        nc.vector.tensor_scalar(xn[:, b, :], pg.x[:, b, :], mv[:, b, 0:1], rs[:, b:b + 1],
                                ALU.subtract, ALU.mult).then_inc(xn_ready, 1)


def norm_all_buffers(pg, ctx, name):
    return (pg.sbuf(f"{name}_st", [P, NB, 6], ctx=ctx), pg.sbuf(f"{name}_mv", [P, NB, 2], ctx=ctx),
            pg.sbuf(f"{name}_ve", [P, NB], ctx=ctx), pg.sbuf(f"{name}_rs", [P, NB], ctx=ctx),
            pg.sbuf(f"{name}_xn", [P, NB, D], ctx=ctx))


def state_space(pg):
    nc, a = pg.nc, pg.a
    with ExitStack() as outer:
        zx = pg.sbuf("ss_zx", [P, NB, 2 * DI], ctx=outer)
        sz = pg.sbuf("ss_sz", [P, NB, DI], ctx=outer)
        br = pg.sbuf("ss_br", [P, NB, 2, NS], ctx=outer)
        logd = pg.sbuf("ss_logd", [P, NB, SH], ctx=outer)
        past = pg.sbuf("ss_past", [P, NB, SH], ctx=outer)
        now = pg.sbuf("ss_now", [P, NB, SH], ctx=outer)
        upper = pg.sbuf("ss_upper", [P, P], ctx=outer)
        strict = pg.sbuf("ss_strict", [P, P], ctx=outer)
        after = pg.sbuf("ss_after", [P, P], ctx=outer)
        w_out = pg.sbuf("ss_w_out", [P, 2, D], ctx=outer)
        w_out_in, = pg.sems("ss", "w_out_in")
        state_space_project(pg, zx, sz, br, logd, past, now, upper, strict, after, w_out, w_out_in)
        state_space_mix(pg, zx, sz, br, logd, past, now, upper, strict, after, w_out, w_out_in)


def state_space_project(pg, zx, sz, br, logd, past, now, upper, strict, after, w_out, w_out_in):
    nc, a = pg.nc, pg.a
    NBC = 2 * NS + 3 * SH + NA
    AN = 2 * NS + 3 * SH
    with ExitStack() as ctx:
        (w_in_in, par_in, var_ready, rstd_ready, xn_ready, xt_ready, xt_copied, zx_ready, small_ready, zx_copied,
         small_copied, bc_var_ready, bc_rstd_ready, masks0, masks_done, order_sem, sp_in, sp_exp, sp_one, sp_ln, sg_done,
         phase_in, phase_ready, trig_in, trig_done, adt_ready, dec_done, shift_in, shifted, silu_done) = pg.sems("sp", (
            "w_in_in par_in var_ready rstd_ready xn_ready xt_ready xt_copied zx_ready small_ready zx_copied "
            "small_copied bc_var_ready bc_rstd_ready masks_zeroed masks_done order softplus_in softplus_exp softplus_one "
            "softplus_ln sigmoid_done phase_in phase_ready trig_in trig_done adt_ready decay_done shift_in shifted silu_done"))
        sb = lambda n, s: pg.sbuf("sp_" + n, s, ctx=ctx)
        w_in = sb("w_in", [P, 2 * DI + NBC])
        st, mv, ve, rs, xn = norm_all_buffers(pg, ctx, "sp")
        xt = sb("xt", [P, NB, P])
        sm = sb("sm", [P, NB, NBC])
        gb = sb("gb", [P, 2, 2, NS])
        dtb = sb("dtb", [P, SH])
        dpar = sb("dpar", [P, SH])
        bst = sb("bst", [P, NB, 2, 6])
        bmv = sb("bmv", [P, NB, 2, 2])
        bve = sb("bve", [P, 2 * NB])
        brs = sb("brs", [P, 2 * NB])
        half2 = sb("half2", [P, 2 * NB])
        bn = sb("bn", [P, NB, 2, NS])
        shift = sb("shift", [P, P])
        u = sb("u", [P, NB, 2, SH])
        au = sb("au", [P, NB, 2, SH])
        eu = sb("eu", [P, NB, 2, SH])
        lu = sb("lu", [P, NB, 2, SH])
        pu = sb("pu", [P, NB, 2, SH])
        tr = sb("tr", [P, NB, SH])
        te = sb("te", [P, NB, SH])
        dtm = sb("dtm", [P, NB, 1])
        ang = sb("ang", [P, NB, NA])
        turns = sb("turns", [P, 2, NB * NA])
        rem = sb("rem", [P, 2, NB * NA])
        trig = sb("trig", [P, 2, NB, NA])
        r0 = sb("r0", [P, NB, NA])
        r1 = sb("r1", [P, NB, NA])
        r2 = sb("r2", [P, NB, NA])
        r3 = sb("r3", [P, NB, NA])
        sh_in = sb("sh_in", [P, 2, NB * SH])
        cb = sb("cb", [P, NB, NS])
        cbd = sb("cbd", [P, NB, 1])
        block = ctx.enter_context(nc.Block())

        @block.sync
        def _(sp):
            sp.dma_start(w_in[:, :], a["L0_attn_W_in"]).then_inc(w_in_in, 16)
            for k, n in enumerate(("Bn_g", "Cn_g", "Bn_b", "Cn_b")):
                sp.dma_start(gb[:, k // 2, k % 2, :], a["L0_attn_" + n].partition_broadcast(P)).then_inc(par_in, 16)
            sp.dma_start(dtb[:, :], a["L0_attn_dt_bias"].partition_broadcast(P)).then_inc(par_in, 16)
            sp.dma_start(dpar[:, :], a["L0_attn_D_param"].partition_broadcast(P)).then_inc(par_in, 16)
            sp.dma_start(w_out[:, :, :], a["L0_attn_W_out"].rearrange("(t p) d -> p t d", p=P)).then_inc(w_out_in, 16)

        @block.gpsimd
        def _(pool):
            nc.gpsimd.memset(half2[:, :], -0.5).then_inc(masks0, 1)
            for m in (upper, strict, after):
                nc.gpsimd.memset(m[:, :], 1.0).then_inc(masks0, 1)
            nc.gpsimd.memset(shift[:, :], 0.0).then_inc(masks0, 1)
            pool.wait_ge(var_ready, 1)
            nc.gpsimd.tensor_tensor(rs[:, :], ve[:, :], pg.neg_half[:, :], ALU.pow).then_inc(rstd_ready, 1)
            pool.wait_ge(masks0, 5)
            for m, base, mul, step, op, fill in ((upper, 0, -1, 1, ALU.is_ge, 0.0), (strict, 0, -1, 1, ALU.is_gt, 0.0),
                                                 (after, -1, 1, -1, ALU.is_gt, 0.0), (shift, -1, 1, -1, ALU.not_equal, 1.0)):
                nc.gpsimd.affine_select(out=m[:, :], in_=m[:, :], compare_op=op, fill=fill, base=base,
                                        pattern=[[step, P]], channel_multiplier=mul).then_inc(masks_done, 1)
            pool.wait_ge(bc_var_ready, 1)
            nc.gpsimd.tensor_tensor(brs[:, :], bve[:, :], half2[:, :], ALU.pow).then_inc(bc_rstd_ready, 1)

        @block.tensor
        def _(pe):
            for b in range(NB):
                pe.wait_ge(xn_ready, b + 1)
                nc.tensor.transpose(pg.bank[b // 4][:, (b % 4) * P:(b % 4 + 1) * P], xn[:, b, :],
                                    pg.ident[:, :]).then_inc(xt_ready, 1)
            pe.wait_ge(w_in_in, 16)
            for b in range(NB):
                pe.wait_ge(xt_copied, b // 4 + 1)
                if b >= 2:
                    pe.wait_ge(zx_copied, b - 1)
                nc.tensor.matmul(pg.bank[2 + b % 2][:, :], xt[:, b, :], w_in[:, 0:2 * DI],
                                 start=True, stop=True).then_inc(zx_ready, 1)
                if b >= 2:
                    pe.wait_ge(small_copied, b - 1)
                nc.tensor.matmul(pg.bank[4 + b % 2][:, 0:NBC], xt[:, b, :], w_in[:, 2 * DI:],
                                 start=True, stop=True).then_inc(small_ready, 1)
            pe.wait_ge(masks_done, 4)
            pe.wait_ge(phase_in, 1)
            nc.tensor.matmul(pg.bank[6][:, 0:NB * NA], upper[:, :], ang[:, :, :].rearrange("p b n -> p (b n)"),
                             start=True, stop=True).then_inc(phase_ready, 1)
            pe.wait_ge(shift_in, 2)
            nc.tensor.matmul(pg.bank[7][:, 0:2 * NB * SH], shift[:, :], sh_in[:, :, :].rearrange("p k n -> p (k n)"),
                             start=True, stop=True).then_inc(shifted, 1)

        @block.scalar
        def _(act):
            for h in range(2):
                act.wait_ge(xt_ready, 4 * h + 4)
                nc.scalar.copy(xt[:, 4 * h:4 * h + 4, :].rearrange("p b l -> p (b l)"),
                               pg.bank[h][:, :]).then_inc(xt_copied, 1)
            for b in range(NB):
                act.wait_ge(zx_ready, b + 1)
                nc.scalar.copy(zx[:, b, :], pg.bank[2 + b % 2][:, :]).then_inc(zx_copied, 1)
            act.wait_ge(sp_in, 1)
            nc.scalar.activation(eu[:, :, :, :], au[:, :, :, :], ACT.Exp, scale=-1.0).then_inc(sp_exp, 1)
            act.wait_ge(sp_exp, 1)
            nc.scalar.activation(lu[:, :, :, :], eu[:, :, :, :], ACT.Ln, bias=1.0).then_inc(sp_ln, 1)
            act.wait_ge(adt_ready, 1)
            nc.scalar.activation(sh_in[:, 0, :], logd[:, :, :].rearrange("p b h -> p (b h)"), ACT.Exp).then_inc(shift_in, 1)
            act.wait_ge(sg_done, 1)
            nc.scalar.activation(te[:, :, :], tr[:, :, :], ACT.Sigmoid).then_inc(dec_done, 1)
            act.wait_ge(trig_in, 1)
            nc.scalar.activation(trig[:, :, :, :].rearrange("p k b n -> p (k b n)"),
                                 rem[:, :, :].rearrange("p k n -> p (k n)"), ACT.Sin).then_inc(trig_done, 1)
            act.wait_ge(zx_copied, NB)
            nc.scalar.activation(sz[:, :, :], zx[:, :, 0:DI], ACT.Silu).then_inc(silu_done, 1)

        @block.vector
        def _(dve):
            o = Order(dve, order_sem)
            V = nc.vector
            norm_all(pg, dve, o, st, mv, ve, var_ready, rstd_ready, rs, xn, xn_ready)
            for b in range(NB):
                dve.wait_ge(small_ready, b + 1)
                V.tensor_copy(sm[:, b, :], pg.bank[4 + b % 2][:, 0:NBC]).then_inc(small_copied, 1)
            dve.wait_ge(small_copied, NB)
            dve.wait_ge(par_in, 16 * 6)
            V.tensor_tensor(u[:, :, 0, :], sm[:, :, 2 * NS:2 * NS + SH],
                            bc(dtb[:, :].unsqueeze(1), [P, NB, SH]), ALU.add).then_inc(order_sem, 1)
            o.n += 1
            o.after(V.tensor_copy(u[:, :, 1, :], sm[:, :, 2 * NS + SH:2 * NS + 2 * SH]))
            V.scalar_tensor_tensor(au[:, :, :, :].rearrange("p b k h -> p (b k h)"), u[:, :, :, :].rearrange("p b k h -> p (b k h)"),
                                   -1.0, u[:, :, :, :].rearrange("p b k h -> p (b k h)"), ALU.mult, ALU.max).then_inc(sp_in, 1)
            V.tensor_copy(tr[:, :, :], sm[:, :, 2 * NS + 2 * SH:AN]).then_inc(sg_done, 1)
            for b in range(NB):
                for k in range(2):
                    o.mark(V.bn_stats(bst[:, b, k, :], sm[:, b, k * NS:(k + 1) * NS]))
            o.wait()
            for b in range(NB):
                for k in range(2):
                    o.mark(V.bn_aggr(bmv[:, b, k, :], bst[:, b, k, :]))
            o.wait()
            V.tensor_scalar(bve[:, :], bmv[:, :, :, 1].rearrange("p b k -> p (b k)"), EPS, None,
                            ALU.add).then_inc(bc_var_ready, 1)
            dve.wait_ge(sp_ln, 1)
            o.after(V.scalar_tensor_tensor(pu[:, :, :, :].rearrange("p b k h -> p (b k h)"), u[:, :, :, :].rearrange("p b k h -> p (b k h)"),
                                           0.0, lu[:, :, :, :].rearrange("p b k h -> p (b k h)"), ALU.max, ALU.add))
            dt = pu[:, :, 0, :]
            o.mark(V.tensor_scalar(au[:, :, 1, :], pu[:, :, 1, :], -1.0, -1e-4, ALU.mult, ALU.min))
            o.after(V.tensor_reduce(dtm[:, :, 0], dt, AX, ALU.add))
            V.tensor_tensor(logd[:, :, :], au[:, :, 1, :], dt, ALU.mult).then_inc(adt_ready, 1)
            o.after(V.tensor_scalar(dtm[:, :, :], dtm[:, :, :], 1.0 / SH, None, ALU.mult))
            V.tensor_tensor(ang[:, :, :], sm[:, :, AN:], bc(dtm[:, :, :], [P, NB, NA]), ALU.mult).then_inc(phase_in, 1)
            dve.wait_ge(dec_done, 1)
            o.after(V.tensor_tensor(now[:, :, :], te[:, :, :], dt, ALU.mult))
            V.tensor_tensor(sh_in[:, 1, :].rearrange("p (b h) -> p b h", b=NB), dt, now[:, :, :],
                            ALU.subtract).then_inc(shift_in, 1)
            MAGIC, TP = 1.5 * 2.0 ** 23, 2 * np.pi
            HI = 6.28125
            ph = pg.bank[6][:, 0:NB * NA]
            dve.wait_ge(phase_ready, 1)
            for k in range(2):
                o.mark(V.tensor_scalar(turns[:, k, :], ph, 1 / TP, 0.25 * k, ALU.mult, ALU.add))
            o.wait()
            o.after(V.tensor_scalar(turns[:, :, :], turns[:, :, :], MAGIC, None, ALU.add))
            o.after(V.tensor_scalar(turns[:, :, :], turns[:, :, :], -MAGIC, None, ALU.add))
            for k in range(2):
                o.mark(V.scalar_tensor_tensor(rem[:, k, :], turns[:, k, :], -HI, ph, ALU.mult, ALU.add))
            o.wait()
            o.after(V.scalar_tensor_tensor(rem[:, :, :].rearrange("p k n -> p (k n)"), turns[:, :, :].rearrange("p k n -> p (k n)"),
                                           -(TP - HI), rem[:, :, :].rearrange("p k n -> p (k n)"), ALU.mult, ALU.add))
            o.after(V.tensor_scalar(rem[:, 1, :], rem[:, 1, :], TP / 4, None, ALU.add))
            PI = float(np.nextafter(np.float32(np.pi), np.float32(0)))
            V.tensor_scalar(rem[:, :, :], rem[:, :, :], PI, -PI, ALU.min, ALU.max).then_inc(trig_in, 1)
            dve.wait_ge(bc_rstd_ready, 1)
            o.after(V.tensor_tensor(bn[:, :, :, :], sm[:, :, 0:2 * NS].rearrange("p b (k n) -> p b k n", k=2),
                                    bc(bmv[:, :, :, 0:1], [P, NB, 2, NS]), ALU.subtract))
            o.after(V.tensor_tensor(bn[:, :, :, :], bn[:, :, :, :],
                                    bc(brs[:, :].rearrange("p (b k) -> p b k", b=NB).unsqueeze(3), [P, NB, 2, NS]), ALU.mult))
            for k, op in ((0, ALU.mult), (1, ALU.add)):
                o.after(V.tensor_tensor(bn[:, :, :, :], bn[:, :, :, :],
                                        bc(gb[:, k:k + 1, :, :], [P, NB, 2, NS]), op))
            dve.wait_ge(trig_done, 1)
            sin, cos = trig[:, 0, :, :], trig[:, 1, :, :]
            for k in range(2):
                ev = bn[:, :, k, 0:NS:2]
                od = bn[:, :, k, 1:NS:2]
                o.mark(V.tensor_tensor(r0[:, :, :], ev, cos, ALU.mult))
                o.mark(V.tensor_tensor(r1[:, :, :], od, sin, ALU.mult))
                o.mark(V.tensor_tensor(r2[:, :, :], ev, sin, ALU.mult))
                o.after(V.tensor_tensor(r3[:, :, :], od, cos, ALU.mult))
                o.mark(V.tensor_tensor(br[:, :, k, 0:NS:2], r0[:, :, :], r1[:, :, :], ALU.subtract))
                o.after(V.tensor_tensor(br[:, :, k, 1:NS:2], r2[:, :, :], r3[:, :, :], ALU.add))
            o.after(V.tensor_tensor(cb[:, :, :], br[:, :, 0, :], br[:, :, 1, :], ALU.mult))
            o.after(V.tensor_reduce(cbd[:, :, 0], cb[:, :, :], AX, ALU.add))
            dve.wait_ge(shifted, 1)
            nd = pg.bank[7][:, 0:2 * NB * SH].rearrange("p (k b h) -> p k b h", k=2, b=NB)
            o.after(V.tensor_tensor(past[:, :, :], nd[:, 0], now[:, :, :], ALU.mult))
            o.mark(V.tensor_tensor(past[:, :, :], nd[:, 1], past[:, :, :], ALU.add))
            o.after(V.tensor_tensor(now[:, :, :], now[:, :, :], bc(cbd[:, :, :], [P, NB, SH]), ALU.mult))
            o.after(V.tensor_tensor(now[:, :, :], now[:, :, :], bc(dpar[:, :].unsqueeze(1), [P, NB, SH]), ALU.add))


def state_space_mix(pg, zx, sz, br, logd, past, now, upper, strict, after, w_out, w_out_in):
    nc = pg.nc
    with ExitStack() as ctx:
        (bc_in, rl_in, bct_ready, bct_copied, cb_ready, lg_ready, cbm_done, e_done, g_done, xs_done, y_ready,
         y_done, yt_ready, yt_copied, o_ready, order_sem) = pg.sems("sm", (
            "bc_in rl_in bct_ready bct_copied cb_ready decay_sum_ready cb_masked decay_done mix_ready xs_done y_ready "
            "y_done yt_ready yt_copied out_ready order"))
        two = lambda n, s: [pg.sbuf(f"sm_{n}{p}", s, ctx=ctx) for p in range(2)]
        bcs, bct = two("bcs", [P, 3 * NS]), two("bct", [NS, 2, P])
        rl, e, g = two("rl", [P, SH, P]), two("e", [P, SH, P]), two("g", [P, SH, P])
        cbm, xs = two("cbm", [P, P]), two("xs", [P, SH, NS])
        t1, y, yt = two("t1", [P, SH, NS]), two("y", [P, DI]), two("yt", [P, 2, P])
        block = ctx.enter_context(nc.Block())

        @block.gpsimd
        def _(pool):
            with pool.Fori(0, NB // 2) as i:
                for p in range(2):
                    pool.wait_ge(bct_ready, 4 * i)
                    nc.gpsimd.tensor_copy(bcs[p][:, 0:2 * NS], br[:, 2 * i + p].rearrange("p k n -> p (k n)")).then_inc(bc_in, 1)
                    nc.gpsimd.tensor_copy(bcs[p][:, 2 * NS:], br[:, 2 * i + p, 0, :]).then_inc(bc_in, 1)

        @block.tensor
        def _(pe):
            pe.wait_ge(w_out_in, 16)
            with pe.Fori(0, NB // 2) as i:
                for p in range(2):
                    A = pg.bank[p]
                    pe.wait_ge(bc_in, 4 * i + 2 * p + 2)
                    pe.wait_ge(order_sem, 8 * i)
                    for k in range(2):
                        nc.tensor.transpose(A[:, k * P:(k + 1) * P], bcs[p][:, k * NS:k * NS + P],
                                            pg.ident[:, :]).then_inc(bct_ready, 1)
                for p in range(2):
                    pe.wait_ge(rl_in, 2 * i + p + 1)
                    nc.tensor.matmul(pg.bank[2 + p][:, :], after[:, :], rl[p][:, :, :].rearrange("p h l -> p (h l)"),
                                     start=True, stop=True).then_inc(lg_ready, 1)
                for p in range(2):
                    pe.wait_ge(bct_copied, 2 * i + p + 1)
                    nc.tensor.matmul(pg.bank[p][:, 256:384], bct[p][:, 0, :], bct[p][:, 1, :],
                                     start=True, stop=True).then_inc(cb_ready, 1)
                for p in range(2):
                    pe.wait_ge(g_done, 2 * i + p + 1)
                    pe.wait_ge(xs_done, 2 * i + p + 1)
                    for h in range(SH):
                        mm = nc.tensor.matmul(pg.bank[4 + p][:, h * NS:(h + 1) * NS], g[p][:, h, :], xs[p][:, h, :],
                                              start=True, stop=True)
                    mm.then_inc(y_ready, 1)
                for p in range(2):
                    pe.wait_ge(y_done, 2 * i + p + 1)
                    for t in range(2):
                        nc.tensor.transpose(pg.bank[4 + p][:, DI + t * P:DI + (t + 1) * P], y[p][:, t * P:(t + 1) * P],
                                            pg.ident[:, :]).then_inc(yt_ready, 1)
                for p in range(2):
                    pe.wait_ge(yt_copied, 2 * i + p + 1)
                    for t in range(2):
                        mm = nc.tensor.matmul(pg.bank[p][:, 384:512], yt[p][:, t, :], w_out[:, t, :],
                                              start=(t == 0), stop=(t == 1))
                    mm.then_inc(o_ready, 1)

        @block.scalar
        def _(act):
            with act.Fori(0, NB // 2) as i:
                for p in range(2):
                    act.wait_ge(bct_ready, 4 * i + 2 * p + 2)
                    nc.scalar.copy(bct[p][:, :, :].rearrange("n k l -> n (k l)"),
                                   pg.bank[p][0:NS, 0:2 * P]).then_inc(bct_copied, 1)
                for p in range(2):
                    act.wait_ge(lg_ready, 2 * i + p + 1)
                    nc.scalar.activation(e[p][:, :, :].rearrange("p h l -> p (h l)"), pg.bank[2 + p][:, :],
                                         ACT.Exp).then_inc(e_done, 1)
                for p in range(2):
                    act.wait_ge(yt_ready, 4 * i + 2 * p + 2)
                    nc.scalar.copy(yt[p][:, :, :].rearrange("p t l -> p (t l)"),
                                   pg.bank[4 + p][:, DI:2 * DI]).then_inc(yt_copied, 1)

        @block.vector
        def _(dve):
            V = nc.vector
            with dve.Fori(0, NB // 2) as i:
                o = Order(dve, order_sem, i, 8)
                for p in range(2):
                    j = 2 * i + p
                    V.tensor_tensor(rl[p][:, :, :], bc(upper[:, :].unsqueeze(1), [P, SH, P]),
                                    bc(logd[:, j].unsqueeze(2), [P, SH, P]), ALU.mult).then_inc(rl_in, 1)
                for p in range(2):
                    j = 2 * i + p
                    xj = zx[:, j, DI:2 * DI].rearrange("p (h n) -> p h n", h=SH)
                    V.tensor_tensor(xs[p][:, :, :], xj, bc(past[:, j].unsqueeze(2), [P, SH, NS]),
                                    ALU.mult).then_inc(xs_done, 1)
                    o.mark(V.tensor_tensor(t1[p][:, :, :], xj, bc(now[:, j].unsqueeze(2), [P, SH, NS]), ALU.mult))
                for p in range(2):
                    dve.wait_ge(cb_ready, 2 * i + p + 1)
                    o.mark(V.tensor_tensor(cbm[p][:, :], pg.bank[p][:, 256:384], strict[:, :], ALU.mult))
                for p in range(2):
                    dve.wait_ge(e_done, 2 * i + p + 1)
                    o.wait(3 + p)
                    V.tensor_tensor(g[p][:, :, :], e[p][:, :, :], bc(cbm[p][:, :].unsqueeze(1), [P, SH, P]),
                                    ALU.mult).then_inc(g_done, 1)
                for p in range(2):
                    j = 2 * i + p
                    t = t1[p][:, :, :].rearrange("p h n -> p (h n)")
                    dve.wait_ge(y_ready, j + 1)
                    o.after(V.tensor_tensor(t, pg.bank[4 + p][:, 0:DI], t, ALU.add))
                    V.tensor_tensor(y[p][:, :], t, sz[:, j, :], ALU.mult).then_inc(y_done, 1)
                for p in range(2):
                    dve.wait_ge(o_ready, 2 * i + p + 1)
                    o.mark(V.tensor_tensor(pg.x[:, 2 * i + p, :], pg.bank[p][:, 384:512], pg.x[:, 2 * i + p, :], ALU.add))
                o.per = o.n
                assert o.n == 8


def cross_weights(pg, ctx, layer):
    w = {n: pg.sbuf(f"c{layer}_{n}", [P if n in "qo" else DC, INNER], ctx=ctx) for n in "qkvo"}
    w["o"] = w["o"][:, :].rearrange("p (t d) -> p t d", t=NT)
    w["bias"] = pg.sbuf(f"c{layer}_bias", [P, D], ctx=ctx)
    if layer:
        w["vw"] = pg.sbuf("c1_vw", [NH * IPA, NB, D], ctx=ctx)
        w["qk_image"] = pg.sbuf("c1_qk_image", [P, NB, NH * IPA], ctx=ctx)
    return w


def load_cross_weights(pg, sp, w, layer, done):
    a, n = pg.a, 0
    if layer == 0:
        kv = a["L0_xattn_w_kv"]
        parts = [(w["q"][:, :], a["L0_xattn_w_q"]), (w["k"][:, :], kv[:, 0:INNER]), (w["v"][:, :], kv[:, INNER:])]
        wo, bias = a["L0_xattn_w_out"], a["L0_xattn_b_out"]
    else:
        parts = [(w[c][:, :], a["L1_xattn_W" + c]) for c in "qkv"]
        wo, bias = a["L1_xattn_Wo"], a["L1_xattn_bo"]
    parts += [(w["o"], wo.rearrange("(t p) d -> p t d", p=P)), (w["bias"][:, :], bias.partition_broadcast(P))]
    for dst, src in parts:
        sp.dma_start(dst, src).then_inc(done, 16)
        n += 16
    return n


def fold_low_rank(pg, w):
    nc, a = pg.nc, pg.a
    R = 32
    NI = NB * IPA
    with ExitStack() as ctx:
        (loaded, tr_ready, tr_copied, prod_ready, folded, img_ready, spread, zeroed, wq_t_ready, wq_t_copied, vw_ready,
         vw_copied, qk_ready, qk_copied, vt_ready, vt_copied, order_sem) = pg.sems("fl", (
            "loaded down_transposed down_copied product_ready folded image_kv_ready image_kv_spread zeroed wq_transposed "
            "wq_copied vw_ready vw_copied qk_ready qk_copied vw_transposed vw_done order"))
        down = {n: pg.sbuf(f"fl_down_{n}", [P if n == "q" else DC, R], ctx=ctx) for n in "qkv"}
        down_o = pg.sbuf("fl_down_o", [P, NT, R], ctx=ctx)
        up = {n: pg.sbuf(f"fl_up_{n}", [R, D if n == "o" else INNER], ctx=ctx) for n in "qkvo"}
        alpha = pg.sbuf("fl_alpha", [P, 4], ctx=ctx)
        down_t = {n: pg.sbuf(f"fl_down_t_{n}", [R, INNER if n == "o" else P], ctx=ctx) for n in "qkvo"}
        w_ipa = [pg.sbuf(f"fl_w{n}_ipa", [DC, INNER], ctx=ctx) for n in "vk"]
        img2 = [pg.sbuf(f"fl_{n}2", [P, NT, 2, NI], ctx=ctx) for n in "vk"]
        wq_t = pg.sbuf("fl_wq_t", [P, NT, P], ctx=ctx)
        vwb = pg.sbuf("fl_vwb", [P, NB, NH, IPA], ctx=ctx)
        block = ctx.enter_context(nc.Block())

        @block.sync
        def _(sp):
            n = load_cross_weights(pg, sp, w, 1, loaded)
            for c in "qkv":
                sp.dma_start(down[c][:, :], a[f"L1_xattn_{c}_down"]).then_inc(loaded, 16)
            sp.dma_start(down_o[:, :, :], a["L1_xattn_o_down"].rearrange("(t p) r -> p t r", p=P)).then_inc(loaded, 16)
            for m, c in enumerate("qkvo"):
                sp.dma_start(up[c][:, :], a[f"L1_xattn_{c}_up"]).then_inc(loaded, 16)
                sp.dma_start(alpha[:, m:m + 1], a[f"L1_xattn_{c}_alpha"].partition_broadcast(P)).then_inc(loaded, 16)
            for k, c in enumerate("vk"):
                sp.dma_start(w_ipa[k][:, :], a[f"L1_xattn_W{c}_ipa"]).then_inc(loaded, 16)

        LOADS = 16 * (5 + 3 + 1 + 8 + 2)

        @block.gpsimd
        def _(pool):
            for t in img2:
                nc.gpsimd.memset(t[:, :, :, :], 0.0).then_inc(zeroed, 1)

        @block.tensor
        def _(pe):
            pe.wait_ge(loaded, LOADS)
            for m, c in enumerate("qkv"):
                rows = P if c == "q" else DC
                nc.tensor.transpose(pg.bank[0][0:R, m * P:m * P + rows], down[c][:, :],
                                    pg.ident[0:rows, 0:rows]).then_inc(tr_ready, 1)
            for t in range(NT):
                nc.tensor.transpose(pg.bank[1 + t // 4][0:R, (t % 4) * P:(t % 4 + 1) * P], down_o[:, t, :],
                                    pg.ident[:, :]).then_inc(tr_ready, 1)
            for k in range(2):
                for t in range(NT):
                    mm = nc.tensor.matmul(pg.bank[7][:, (NT * k + t) * NI:(NT * k + t + 1) * NI],
                                          w_ipa[k][:, t * P:(t + 1) * P], pg.ctx_t[:, 0:NB, P - IPA:P],
                                          start=True, stop=True)
            mm.then_inc(img_ready, 1)
            pe.wait_ge(tr_copied, 5)
            for m, c in enumerate("qkvo"):
                for h in range(2):
                    k = 2 * m + h
                    if k >= 4:
                        pe.wait_ge(folded, k - 3)
                    if c != "o":
                        rows = P if c == "q" else DC
                        mm = nc.tensor.matmul(pg.bank[3 + k % 4][0:rows, :], down_t[c][:, 0:rows],
                                              up[c][:, 512 * h:512 * (h + 1)], start=True, stop=True)
                    else:
                        for t in range(4):
                            mm = nc.tensor.matmul(pg.bank[3 + k % 4][:, t * P:(t + 1) * P],
                                                  down_t[c][:, (4 * h + t) * P:(4 * h + t + 1) * P], up[c][:, :],
                                                  start=True, stop=True)
                    mm.then_inc(prod_ready, 1)
            pe.wait_ge(folded, 4)
            for t in range(NT):
                nc.tensor.transpose(pg.bank[1 + t // 4][:, (t % 4) * P:(t % 4 + 1) * P], w["q"][:, t * P:(t + 1) * P],
                                    pg.ident[:, :]).then_inc(wq_t_ready, 1)
            pe.wait_ge(spread, 4)
            pe.wait_ge(folded, 8)
            for t in range(NT):
                mm = nc.tensor.matmul(pg.bank[0][:, t * 2 * NI:(t + 1) * 2 * NI], w["o"][:, t, :],
                                      img2[0][:, t, :, :].rearrange("p g n -> p (g n)"), start=True, stop=True)
            mm.then_inc(vw_ready, 1)
            pe.wait_ge(wq_t_copied, 2)
            for t in range(NT):
                mm = nc.tensor.matmul(pg.bank[3][:, t * 2 * NI:(t + 1) * 2 * NI], wq_t[:, t, :],
                                      img2[1][:, t, :, :].rearrange("p g n -> p (g n)"), start=True, stop=True)
            mm.then_inc(qk_ready, 1)
            pe.wait_ge(vw_copied, 1)
            for b in range(NB):
                nc.tensor.transpose(pg.bank[4 + b // 4][0:NH * IPA, (b % 4) * P:(b % 4 + 1) * P],
                                    vwb[:, b, :, :].rearrange("p h k -> p (h k)"), pg.ident[:, :]).then_inc(vt_ready, 1)

        @block.scalar
        def _(act):
            for m, c in enumerate("qkv"):
                rows = P if c == "q" else DC
                act.wait_ge(tr_ready, 3)
                nc.scalar.copy(down_t[c][:, 0:rows], pg.bank[0][0:R, m * P:m * P + rows]).then_inc(tr_copied, 1)
            for h in range(2):
                act.wait_ge(tr_ready, 3 + 4 * h + 4)
                nc.scalar.copy(down_t["o"][:, 512 * h:512 * (h + 1)], pg.bank[1 + h][0:R, :]).then_inc(tr_copied, 1)
            for h in range(2):
                act.wait_ge(wq_t_ready, 4 * h + 4)
                nc.scalar.copy(wq_t[:, 4 * h:4 * h + 4, :].rearrange("p t d -> p (t d)"), pg.bank[1 + h][:, :]).then_inc(wq_t_copied, 1)
            act.wait_ge(qk_ready, 1)
            nc.scalar.mul(w["qk_image"][:, :, :].rearrange("p b (h k) -> p b h k", k=IPA),
                          pg.bank[3][:, :].rearrange("p (h b k) -> p b h k", h=NH, b=NB), HD ** -0.5).then_inc(qk_copied, 1)
            for h in range(2):
                act.wait_ge(vt_ready, 4 * h + 4)
                nc.scalar.copy(w["vw"][:, 4 * h:4 * h + 4, :].rearrange("n b d -> n (b d)"),
                               pg.bank[4 + h][0:NH * IPA, :]).then_inc(vt_copied, 1)

        @block.vector
        def _(dve):
            o = Order(dve, order_sem)
            dve.wait_ge(loaded, LOADS)
            o.after(nc.vector.tensor_scalar(alpha[:, :], alpha[:, :], 1.0 / R, None, ALU.mult))
            dve.wait_ge(img_ready, 1)
            dve.wait_ge(zeroed, 2)
            for k in range(2):
                for g in range(2):
                    rows = slice(64 * g, 64 * g + 64)
                    nc.vector.tensor_copy(img2[k][rows, :, g, :], pg.bank[7][rows, NT * k * NI:NT * (k + 1) * NI].rearrange(
                        "p (t n) -> p t n", t=NT)).then_inc(spread, 1)
            for m, c in enumerate("qkvo"):
                for h in range(2):
                    k = 2 * m + h
                    rows = P if c in "qo" else DC
                    dst = w["o"][:, 4 * h:4 * h + 4, :].rearrange("p t d -> p (t d)") if c == "o" else w[c][:, 512 * h:512 * (h + 1)]
                    dve.wait_ge(prod_ready, k + 1)
                    nc.vector.scalar_tensor_tensor(dst, pg.bank[3 + k % 4][0:rows, :], alpha[0:rows, m:m + 1], dst,
                                                   ALU.mult, ALU.add).then_inc(folded, 1)
            dve.wait_ge(vw_ready, 1)
            nc.vector.tensor_copy(vwb[:, :, :, :], pg.bank[0][:, :].rearrange("p (h b k) -> p b h k", h=NH, b=NB)).then_inc(vw_copied, 1)


def cross_attention(pg, w, layer):
    nc = pg.nc
    KS = P - IPA if layer else P
    with ExitStack() as ctx:
        (var_ready, rstd_ready, xn_ready, xt_ready, xt_copied, c_ready, q_ready, q_copied, qb_ready, k_ready, k_copied,
         kb_ready, v_ready, v_copied, s_ready, s_read, nm_ready, nmt_ready, nmt_copied, st_ready, exp_done, av_ready,
         o_done, ot_ready, ot_copied, out_ready, x_done, ones_done, order_sem, norm_order) = pg.sems(f"ca{layer}", (
            "var_ready rstd_ready xn_ready xt_ready xt_copied c_ready q_ready q_copied q_bf_ready k_ready k_copied "
            "k_bf_ready v_ready v_copied s_ready s_read max_ready max_transposed max_copied st_ready exp_done av_ready "
            "o_done ot_ready ot_copied out_ready x_done ones_done order norm_order"))
        if layer:
            (img_ready, img_order, img_shifted, img_exp, p2_ready, p2t_ready, p2t_copied) = pg.sems("ca1_image", (
                "scores_ready order shifted exp_done p_ready p_transposed p_copied"))
        sb = lambda n, s, dt=F32: pg.sbuf(f"ca{layer}_{n}", s, dt, ctx=ctx)
        two = lambda n, s, dt=F32: [sb(f"{n}{p}", s, dt) for p in range(2)]
        st, mv, ve, rs, xn = sb("st", [P, 6]), sb("mv", [P, 2]), sb("ve", [P, 1]), sb("rs", [P, 1]), sb("xn", [P, D])
        xt, ct = sb("xt", [P, P]), sb("ct", [DC, P])
        qt, kt = two("qt", [P, NT, P]), two("kt", [P, NT, P])
        qb, kb = two("qb", [P, NT, P], BF16), two("kb", [P, NT, P], BF16)
        v = two("v", [P, NH, VS])
        m, nm = sb("m", [P, NH]), sb("nm", [P, P // NH, NH], BF16)
        nmt = two("nmt", [P, P], BF16)
        pt = sb("pt", [P, NCH, HPC * P])
        rinv, on = sb("rinv", [P, NH]), sb("on", [P, NH, HD])
        ot = sb("ot", [P, NT, P])
        if layer:
            s2, m2, sum2, p2t = sb("s2", [P, NH, IPA]), sb("m2", [P, NH]), sb("sum2", [P, NH]), sb("p2t", [NH * IPA, P])
        proj = pg.bank[0:2]
        score_t = pg.bank[2:4]
        score, misc = pg.bank[4], pg.bank[5]
        av = pg.bank[6:8]
        nmt_ps = misc[:, 256:320].bitcast(BF16)[:, 0:P]
        p2t_ps = misc[0:NH * IPA, P:2 * P]
        img_ps = misc[:, 320:320 + NH * IPA]
        SCALE = HD ** -0.5
        block = ctx.enter_context(nc.Block())

        def heads_of(c):
            return slice(2 * HPC * (c // 2) + c % 2, 2 * HPC * (c // 2 + 1), 2)

        def head(c, r):
            return 2 * HPC * (c // 2) + c % 2 + 2 * r

        def qrow(t, h):
            return t[64 * (h % 2):64 * (h % 2) + 64, h // 2, :]

        def turns(eng, turn):
            with eng.Fori(0, NB // 2 - 1) as i:
                for p in range(2):
                    turn(2 * i + p, p, True, True)
            turn(NB - 2, 0, True, False)
            turn(NB - 1, 1, False, False)

        @block.gpsimd
        def _(pool):
            for p in range(2):
                nc.gpsimd.memset(v[p][:, :, HD:VS], 1.0).then_inc(ones_done, 1)
            nc.gpsimd.memset(nm[:, 2:, :], 0.0).then_inc(ones_done, 1)

            def rstd(n):
                pool.wait_ge(var_ready, n + 1)
                nc.gpsimd.tensor_tensor(rs[:, :], ve[:, :], pg.neg_half[:, 0:1], ALU.pow).then_inc(rstd_ready, 1)

            def cast_q(n, p, h):
                pool.wait_ge(q_copied, 2 * n + h + 1)
                half = qt[p][:, 4 * h:4 * h + 4, :]
                nc.gpsimd.tensor_tensor(qb[p][:, 4 * h:4 * h + 4, :], half, bc(pg.zero[:, :].unsqueeze(2), [P, 4, P]),
                                        ALU.add).then_inc(qb_ready, 1)

            def copy_ctx(n):
                nc.gpsimd.tensor_copy(ct[:, :], pg.ctx_t[:, n, :]).then_inc(c_ready, 1)

            rstd(0)
            copy_ctx(0)
            rstd(1)
            for h in range(2):
                cast_q(0, 0, h)
            pool.wait_ge(v_ready, 2)
            copy_ctx(1)

            def turn(j, p, nxt, nxt2):
                if nxt:
                    for h in range(2):
                        cast_q(j + 1, 1 - p, h)
                if nxt2:
                    rstd(j + 2)
                    pool.wait_ge(v_ready, 2 * j + 4)
                    copy_ctx(j + 2)

            turns(pool, turn)

        @block.tensor
        def _(pe):
            def x_transpose(n):
                pe.wait_ge(xn_ready, n + 1)
                nc.tensor.transpose(misc[:, 0:P], xn[:, :], pg.ident[:, :]).then_inc(xt_ready, 1)

            def project_q(n, h):
                if h == 0:
                    pe.wait_ge(xt_copied, n + 1)
                for t in range(4):
                    mm = nc.tensor.matmul(proj[h][:, t * P:(t + 1) * P],
                                          w["q"][:, (4 * h + t) * P:(4 * h + t + 1) * P], xt[:, :], start=True, stop=True)
                mm.then_inc(q_ready, 1)

            def project_k(n, h):
                if h == 0:
                    pe.wait_ge(c_ready, n + 1)
                pe.wait_ge(q_copied, 2 * n + h + 1)
                for t in range(4):
                    mm = nc.tensor.matmul(proj[h][:, t * P:(t + 1) * P], w["k"][:, (4 * h + t) * P:(4 * h + t + 1) * P],
                                          ct[:, :], start=True, stop=True)
                mm.then_inc(k_ready, 1)

            def project_v(n, h):
                pe.wait_ge(k_copied, 2 * n + h + 1)
                nc.tensor.matmul(proj[h][0:KS, :], ct[:, 0:KS], w["v"][:, 512 * h:512 * (h + 1)],
                                 start=True, stop=True).then_inc(v_ready, 1)

            def image_scores(n):
                nc.tensor.matmul(img_ps, xt[:, :], w["qk_image"][:, n, :], start=True, stop=True).then_inc(img_ready, 1)

            def scores(n, p, c, first=False):
                if c % 2 == 0:
                    pe.wait_ge(qb_ready, 2 * n + c // 2 + 1)
                    pe.wait_ge(kb_ready, 2 * n + c // 2 + 1)
                if not first:
                    pe.wait_ge(s_read, NCH * n + c)
                for r in range(HPC):
                    h = head(c, r)
                    mm = nc.tensor.matmul(score[:, r * P:r * P + KS], qrow(qb[p], h), qrow(kb[p], h)[:, 0:KS],
                                          start=True, stop=True)
                mm.then_inc(s_ready, 1)

            def max_transpose(n):
                pe.wait_ge(nm_ready, 2 * n + 2)
                nc.tensor.transpose(nmt_ps, nm[:, :, :].rearrange("p k h -> p (k h)"), pg.ident_bf[:, :]).then_inc(nmt_ready, 1)

            def scores_t(j, p, c):
                if c == 0:
                    pe.wait_ge(nmt_copied, j + 1)
                for r in range(HPC):
                    h = head(c, r)
                    dst = score_t[c % 2][0:KS, r * P:(r + 1) * P]
                    nc.tensor.matmul(dst, qrow(kt[p], h)[:, 0:KS], qrow(qt[p], h), start=True, stop=False)
                    mm = nc.tensor.matmul(dst, pg.sel[:, h, 0:KS], nmt[p][:, :], start=False, stop=True)
                mm.then_inc(st_ready, 1)

            def values(j, p, c):
                if c >= 2:
                    pe.wait_ge(o_done, NCH * j + c - 1)
                pe.wait_ge(exp_done, NCH * j + c + 1)
                for r in range(HPC):
                    mm = nc.tensor.matmul(av[c % 2][:, r * VS:(r + 1) * VS], pt[0:KS, c, r * P:(r + 1) * P],
                                          v[p][0:KS, head(c, r), :], start=True, stop=True)
                mm.then_inc(av_ready, 1)

            def out_transpose(j, h, nxt):
                if nxt:
                    pe.wait_ge(v_copied, 2 * j + 2 + h + 1)
                pe.wait_ge(o_done, NCH * j + 2 * h + 2)
                for t in range(4):
                    mm = nc.tensor.transpose(proj[h][:, t * P:(t + 1) * P],
                                             on[:, 8 * h + 2 * t:8 * h + 2 * t + 2, :].rearrange("p h d -> p (h d)"),
                                             pg.ident[:, :])
                mm.then_inc(ot_ready, 1)

            def project_out(j):
                for t in range(NT):
                    if t % 4 == 0:
                        pe.wait_ge(ot_copied, 2 * j + t // 4 + 1)
                    mm = nc.tensor.matmul(misc[:, 0:D], ot[:, t, :], w["o"][:, t, :], start=(t == 0),
                                          stop=(t == NT - 1 and not layer))
                if layer:
                    mm = nc.tensor.matmul(misc[:, 0:D], p2t[:, :], w["vw"][:, j, :], start=False, stop=True)
                mm.then_inc(out_ready, 1)

            pe.wait_ge(ones_done, 3)
            x_transpose(0)
            for h in range(2):
                project_q(0, h)
            if layer:
                image_scores(0)
            for h in range(2):
                project_k(0, h)
            for h in range(2):
                project_v(0, h)
            for c in range(NCH):
                scores(0, 0, c, first=(c == 0))
            if layer:
                pe.wait_ge(img_shifted, 1)
            x_transpose(1)
            pe.wait_ge(xt_copied, 2)
            max_transpose(0)
            pe.wait_ge(v_copied, 2)

            def turn(j, p, nxt, nxt2):
                n, q = j + 1, 1 - p
                scores_t(j, p, 0)
                if layer:
                    pe.wait_ge(x_done, j)
                    pe.wait_ge(p2_ready, j + 1)
                if nxt:
                    project_q(n, 0)
                if layer:
                    nc.tensor.transpose(p2t_ps, s2[:, :, :].rearrange("p h k -> p (h k)"), pg.ident[:, :]).then_inc(p2t_ready, 1)
                scores_t(j, p, 1)
                if nxt:
                    project_q(n, 1)
                    if layer:
                        pe.wait_ge(p2t_copied, j + 1)
                        image_scores(n)
                values(j, p, 0)
                if nxt:
                    project_k(n, 0)
                scores_t(j, p, 2)
                if nxt:
                    project_k(n, 1)
                values(j, p, 1)
                scores_t(j, p, 3)
                if nxt:
                    scores(n, q, 0)
                values(j, p, 2)
                if nxt:
                    project_v(n, 0)
                    scores(n, q, 1)
                values(j, p, 3)
                if nxt:
                    project_v(n, 1)
                    scores(n, q, 2)
                if nxt2:
                    pe.wait_ge(x_done, j)
                    if layer:
                        pe.wait_ge(img_shifted, n + 1)
                    x_transpose(j + 2)
                out_transpose(j, 0, nxt)
                if nxt:
                    scores(n, q, 3)
                out_transpose(j, 1, nxt)
                if nxt:
                    if nxt2:
                        pe.wait_ge(xt_copied, j + 3)
                    else:
                        pe.wait_ge(x_done, j)
                        if layer:
                            pe.wait_ge(img_shifted, n + 1)
                    max_transpose(n)
                    pe.wait_ge(nmt_copied, n + 1)
                else:
                    pe.wait_ge(x_done, j)
                    if layer:
                        pe.wait_ge(p2t_copied, j + 1)
                project_out(j)

            turns(pe, turn)

        @block.scalar
        def _(act):
            def copy_q(n, p, h):
                act.wait_ge(q_ready, 2 * n + h + 1)
                nc.scalar.mul(qt[p][:, 4 * h:4 * h + 4, :].rearrange("p t l -> p (t l)"), proj[h][:, :],
                              SCALE).then_inc(q_copied, 1)

            def copy_xt(n):
                act.wait_ge(xt_ready, n + 1)
                nc.scalar.copy(xt[:, :], misc[:, 0:P]).then_inc(xt_copied, 1)

            def copy_v(n, p, h):
                act.wait_ge(v_ready, 2 * n + h + 1)
                nc.scalar.copy(v[p][0:KS, 8 * h:8 * h + 8, 0:HD], proj[h][0:KS, :].rearrange(
                    "p (h d) -> p h d", d=HD)).then_inc(v_copied, 1)

            def copy_max(n, p):
                act.wait_ge(nmt_ready, n + 1)
                nc.scalar.copy(nmt[p][:, :], nmt_ps).then_inc(nmt_copied, 1)

            def image_exp(n):
                act.wait_ge(img_shifted, n + 1)
                nc.scalar.activation(s2[:, :, :], s2[:, :, :], ACT.Exp).then_inc(img_exp, 1)

            def exp(j, c):
                act.wait_ge(st_ready, NCH * j + c + 1)
                nc.scalar.activation(pt[0:KS, c, :], score_t[c % 2][0:KS, :], ACT.Exp).then_inc(exp_done, 1)

            act.wait_ge(ones_done, 3)
            copy_xt(0)
            for h in range(2):
                copy_q(0, 0, h)
            if layer:
                image_exp(0)
            for h in range(2):
                copy_v(0, 0, h)
            copy_xt(1)
            copy_max(0, 0)

            def turn(j, p, nxt, nxt2):
                n, q = j + 1, 1 - p
                if layer:
                    act.wait_ge(p2t_ready, j + 1)
                    nc.scalar.copy(p2t[:, :], p2t_ps).then_inc(p2t_copied, 1)
                exp(j, 0)
                if nxt:
                    copy_q(n, q, 0)
                exp(j, 1)
                if nxt:
                    copy_q(n, q, 1)
                exp(j, 2)
                if layer and nxt:
                    image_exp(n)
                exp(j, 3)
                if nxt:
                    copy_v(n, q, 0)
                    copy_v(n, q, 1)
                if nxt2:
                    copy_xt(j + 2)
                for h in range(2):
                    act.wait_ge(ot_ready, 2 * j + h + 1)
                    nc.scalar.copy(ot[:, 4 * h:4 * h + 4, :].rearrange("p t l -> p (t l)"),
                                   proj[h][:, :]).then_inc(ot_copied, 1)
                if nxt:
                    copy_max(n, q)

            turns(act, turn)

        @block.vector
        def _(dve):
            V = nc.vector

            def norm_stats(n):
                V.bn_stats(st[:, :], pg.x[:, n, :]).then_inc(norm_order, 1)

            def wait_stats(n):
                dve.wait_ge(norm_order, 2 * n + 1)

            def norm_aggregate(n):
                V.bn_aggr(mv[:, :], st[:, :]).then_inc(norm_order, 1)
                dve.wait_ge(norm_order, 2 * n + 2)
                V.tensor_scalar(ve[:, :], mv[:, 1:2], EPS, None, ALU.add).then_inc(var_ready, 1)

            def norm_apply(n):
                dve.wait_ge(rstd_ready, n + 1)
                V.tensor_scalar(xn[:, :], pg.x[:, n, :], mv[:, 0:1], rs[:, 0:1], ALU.subtract,
                                ALU.mult).then_inc(xn_ready, 1)

            def copy_k(n, p, h):
                half = slice(4 * h, 4 * h + 4)
                dve.wait_ge(k_ready, 2 * n + h + 1)
                V.tensor_copy(kt[p][:, half, :].rearrange("p t k -> p (t k)"), proj[h][:, :]).then_inc(k_copied, 1)
                dve.wait_ge(k_copied, 2 * n + h + 1)
                V.tensor_copy(kb[p][:, half, :], kt[p][:, half, :]).then_inc(kb_ready, 1)

            def row_max(n, c):
                dve.wait_ge(s_ready, NCH * n + c + 1)
                s = score[:, :].rearrange("p (h k) -> p h k", k=P)
                V.tensor_reduce(m[:, heads_of(c)], s[:, :, 0:KS], AX, ALU.max, negate=True).then_inc(s_read, 1)

            def split_max(n):
                dve.wait_ge(s_read, NCH * n + NCH)
                V.tensor_copy(nm[:, 0, :], m[:, :]).then_inc(nm_ready, 1)
                dve.wait_ge(nm_ready, 2 * n + 1)
                V.tensor_tensor(nm[:, 1, :], m[:, :], nm[:, 0, :], ALU.subtract).then_inc(nm_ready, 1)

            def image_shift(n):
                dve.wait_ge(img_ready, n + 1)
                s = img_ps.rearrange("p (h k) -> p h k", k=IPA)
                o = Order(dve, img_order, n, 3)
                o.after(V.tensor_reduce(m2[:, :], s, AX, ALU.max))
                V.tensor_tensor(s2[:, :, :], s, bc(m2[:, :].unsqueeze(2), [P, NH, IPA]), ALU.subtract).then_inc(img_shifted, 1)
                return o

            def image_softmax(n, o):
                dve.wait_ge(img_exp, n + 1)
                o.after(V.tensor_reduce(sum2[:, :], s2[:, :, :], AX, ALU.add))
                o.after(V.reciprocal(sum2[:, :], sum2[:, :]))
                V.tensor_tensor(s2[:, :, :], s2[:, :, :], bc(sum2[:, :].unsqueeze(2), [P, NH, IPA]),
                                ALU.mult).then_inc(p2_ready, 1)
                o.close()

            def normalise(j, c, o):
                dve.wait_ge(av_ready, NCH * j + c + 1)
                heads = heads_of(c)
                src = av[c % 2][:, 0:HPC * VS].rearrange("p (h e) -> p h e", e=VS)
                o.after(V.reciprocal(rinv[:, heads].unsqueeze(2), src[:, :, HD:HD + 1]))
                V.tensor_tensor(on[:, heads, :], src[:, :, 0:HD], bc(rinv[:, heads].unsqueeze(2), [P, HPC, HD]),
                                ALU.mult).then_inc(o_done, 1)

            for n in range(2):
                norm_stats(n)
                wait_stats(n)
                norm_aggregate(n)
                if n == 0:
                    norm_apply(0)
            if layer:
                image = image_shift(0)
            for h in range(2):
                copy_k(0, 0, h)
            norm_apply(1)
            if layer:
                image_softmax(0, image)
            for c in range(NCH):
                row_max(0, c)
            split_max(0)

            def turn(j, p, nxt, nxt2):
                n, q = j + 1, 1 - p
                o = Order(dve, order_sem, j, NCH + 1)
                if nxt2:
                    norm_stats(j + 2)
                if layer and nxt:
                    image = image_shift(n)
                if nxt2:
                    wait_stats(j + 2)
                normalise(j, 0, o)
                if nxt2:
                    norm_aggregate(j + 2)
                if nxt:
                    copy_k(n, q, 0)
                    copy_k(n, q, 1)
                if nxt2:
                    norm_apply(j + 2)
                if layer and nxt:
                    image_softmax(n, image)
                normalise(j, 1, o)
                for c in (0, 1):
                    if nxt:
                        row_max(n, c)
                    normalise(j, 2 + c, o)
                if nxt:
                    row_max(n, 2)
                    row_max(n, 3)
                    split_max(n)
                dve.wait_ge(out_ready, j + 1)
                o.after(V.tensor_tensor(pg.x[:, j, :], misc[:, 0:D], pg.x[:, j, :], ALU.add))
                V.tensor_tensor(pg.x[:, j, :], pg.x[:, j, :], w["bias"][:, :], ALU.add).then_inc(x_done, 1)
                o.close()

            turns(dve, turn)


def self_attention(pg):
    nc, a = pg.nc, pg.a
    W = D // NH
    VW = W + 2
    SLOTS, USED = 8, 6
    SCALE = W ** -0.5
    QS = {"h": (0, 3, 5), "m": (1, 4), "l": (2,)}
    KS = {"h": (0, 2, 4), "m": (1, 5), "l": (3,)}
    with ExitStack() as ctx:
        (loaded, wt_ready, zeroed, wt_copied, bias_scaled, iota_done, alibi_order, alibi_done, var_ready, rstd_ready,
         norm_order, xn_ready, xt_ready, xt_copied, qkv_ready, qk_added, v_added, split_order, split_done, dup_done,
         qt_ready, qt_copied, kt_ready, kt_copied, s_ready, s_read, nm_ready, nmt_ready, nmt_copied, st_ready,
         st_read, exp_done, av_ready, o_done, ot_ready, ot_copied, out_ready, x_done, order_sem) = pg.sems("sa", (
            "loaded wt_ready zeroed wt_copied bias_scaled iota_done alibi_order alibi_done var_ready rstd_ready "
            "norm_order xn_ready xt_ready xt_copied qkv_ready qk_added v_added split_order split_done dup_done "
            "qt_ready qt_copied kt_ready kt_copied s_ready s_read max_ready max_transposed max_copied st_ready "
            "st_read exp_done av_ready o_done ot_ready ot_copied out_ready x_done order"))
        sb = lambda n, s, dt=F32: pg.sbuf(f"sa_{n}", s, dt, ctx=ctx)
        two = lambda n, s, dt=F32: [sb(f"{n}{p}", s, dt) for p in range(2)]
        w_nat = sb("w_nat", [P, 4, D])
        wt = sb("wt", [P, 4, D])
        bqkv, bo = sb("bqkv", [P, 3 * D]), sb("bo", [P, D])
        dist_i, dist = sb("dist_i", [P, P], mybir.dt.int32), sb("dist", [P, P])
        alibi, alibi_bf = sb("alibi", [P, NCH, HPC, P]), sb("alibi_bf", [P, NCH, HPC, P], BF16)
        st, mv, ve, rs, xn = sb("st", [P, 6]), sb("mv", [P, 2]), sb("ve", [P, 1]), sb("rs", [P, 1]), sb("xn", [P, D])
        xt = sb("xt", [P, P])
        qk, rest = sb("qk", [P, 2, NH, W]), sb("rest", [P, 2, NH, W])
        parts = sb("parts", [P, 2, NH, SLOTS, W], BF16)
        qt, kt = two("qt", [P, NT, P], BF16), two("kt", [P, NT, P], BF16)
        v = sb("v", [P, NB, NH, VW])
        m, nm, nmt = sb("m", [P, NH]), sb("nm", [P, P // NH, NH], BF16), two("nmt", [P, P], BF16)
        pre, pt = two("pre", [P, HPC * P]), sb("pt", [P, NCH, HPC, P])
        rinv, on, ot = sb("rinv", [P, NH]), sb("on", [P, D]), sb("ot", [P, P])
        qt_bank, kt_bank, score_t, score, misc, av, qkv = (
            pg.bank[0], pg.bank[1], pg.bank[2:4], pg.bank[4], pg.bank[5], pg.bank[6], pg.bank[7])
        ot_ps, nmt_ps, out_ps = misc[:, P:2 * P], misc[:, 256:320].bitcast(BF16)[:, 0:P], misc[:, 384:512]
        block = ctx.enter_context(nc.Block())

        def heads_of(c):
            return slice(2 * HPC * (c // 2) + c % 2, 2 * HPC * (c // 2 + 1), 2)

        def head(c, r):
            return 2 * HPC * (c // 2) + c % 2 + 2 * r

        def rows_of(t, h):
            return t[64 * (h % 2):64 * (h % 2) + USED * W, h // 2, :]

        def turns(eng, turn):
            with eng.Fori(0, NB // 2 - 1) as i:
                for p in range(2):
                    turn(2 * i + p, p, True, True)
            turn(NB - 2, 0, True, False)
            turn(NB - 1, 1, False, False)

        @block.sync
        def _(sp):
            sp.dma_start(w_nat[:, 0:3, :], a["L1_attn_W_qkv"].rearrange("(t p) d -> p t d", p=P)).then_inc(loaded, 16)
            sp.dma_start(w_nat[:, 3, :], a["L1_attn_W_out"]).then_inc(loaded, 16)
            sp.dma_start(bqkv[:, :], a["L1_attn_b_qkv"].partition_broadcast(P)).then_inc(loaded, 16)
            sp.dma_start(bo[:, :], a["L1_attn_b_out"].partition_broadcast(P)).then_inc(loaded, 16)

        LOADS = 16 * 4

        @block.gpsimd
        def _(pool):
            nc.gpsimd.iota(dist_i[:, :], pattern=[[-1, P]], base=0, channel_multiplier=1).then_inc(iota_done, 1)
            nc.gpsimd.memset(parts[:, :, :, :, :], 0.0).then_inc(zeroed, 1)
            nc.gpsimd.memset(v[:, :, :, W:VW], 1.0).then_inc(zeroed, 1)
            nc.gpsimd.memset(nm[:, 2:, :], 0.0).then_inc(zeroed, 1)

            def rstd(n):
                pool.wait_ge(var_ready, n + 1)
                nc.gpsimd.tensor_tensor(rs[:, :], ve[:, :], pg.neg_half[:, 0:1], ALU.pow).then_inc(rstd_ready, 1)

            def duplicate(n):
                for part, count in (("h", 1), ("m", 3)):
                    for k, slots in enumerate((QS[part], KS[part])):
                        first, again = slots[0], slots[1:]
                        dst = parts[:, k, :, again[0]:again[-1] + 1:2, :]
                        src = bc(parts[:, k, :, first:first + 1, :], [P, NH, len(again), W])
                        if k == 0:
                            pool.wait_ge(split_order, 3 * n + count)
                        nc.gpsimd.tensor_tensor(dst, src, bc(pg.zero[:, :].unsqueeze(2).unsqueeze(3), [P, NH, len(again), W]),
                                                ALU.add).then_inc(dup_done, 1)

            for n in range(3):
                rstd(n)
            for n in range(2):
                if n:
                    pool.wait_ge(kt_ready, 1)
                duplicate(n)

            def turn(j, p, nxt, ahead):
                if ahead:
                    rstd(j + 3)
                    duplicate(j + 2)

            turns(pool, turn)

        @block.tensor
        def _(pe):
            pe.wait_ge(loaded, LOADS)
            for k in range(4):
                nc.tensor.transpose(score_t[0][:, k * P:(k + 1) * P], w_nat[:, k, :], pg.ident[:, :]).then_inc(wt_ready, 1)

            def x_transpose(n):
                pe.wait_ge(xn_ready, n + 1)
                nc.tensor.transpose(misc[:, 0:P], xn[:, :], pg.ident[:, :]).then_inc(xt_ready, 1)

            def project(n):
                pe.wait_ge(xt_copied, n + 1)
                pe.wait_ge(v_added, n)
                nc.tensor.matmul(qkv[:, 0:3 * D], xt[:, :], wt[:, 0:3, :].rearrange("p t d -> p (t d)"),
                                 start=True, stop=True).then_inc(qkv_ready, 1)

            def transpose_parts(n, k, bank, ready):
                if k == 0:
                    pe.wait_ge(split_done, 2 * n + 2)
                    pe.wait_ge(dup_done, 4 * n + 4)
                ps = bank[:, :].bitcast(BF16)
                for t in range(NT):
                    mm = nc.tensor.transpose(ps[:, t * P:(t + 1) * P],
                                             parts[:, k, 2 * t:2 * t + 2, :, :].rearrange("p h s w -> p (h s w)"),
                                             pg.ident_bf[:, :])
                mm.then_inc(ready, 1)

            def scores(n, p, c, first=False):
                if c == 0:
                    pe.wait_ge(qt_copied, n + 1)
                    pe.wait_ge(kt_copied, n + 1)
                if not first:
                    pe.wait_ge(s_read, NCH * n + c)
                nc.tensor.matmul(score[:, :], pg.ident_bf[:, :], alibi_bf[:, c, :, :].rearrange("p r k -> p (r k)"),
                                 start=True, stop=False)
                for r in range(HPC):
                    h = head(c, r)
                    mm = nc.tensor.matmul(score[:, r * P:(r + 1) * P], rows_of(qt[p], h), rows_of(kt[p], h),
                                          start=False, stop=(r == HPC - 1))
                mm.then_inc(s_ready, 1)

            def max_transpose(n):
                pe.wait_ge(nm_ready, 2 * n + 2)
                nc.tensor.transpose(nmt_ps, nm[:, :, :].rearrange("p k h -> p (k h)"), pg.ident_bf[:, :]).then_inc(nmt_ready, 1)

            def scores_t(j, p, c):
                if c == 0:
                    pe.wait_ge(nmt_copied, j + 1)
                if c >= 2:
                    pe.wait_ge(st_read, NCH * j + c - 1)
                for r in range(HPC):
                    h = head(c, r)
                    dst = score_t[c % 2][:, r * P:(r + 1) * P]
                    nc.tensor.matmul(dst, rows_of(kt[p], h), rows_of(qt[p], h), start=True, stop=False)
                    mm = nc.tensor.matmul(dst, pg.sel[:, h, :], nmt[p][:, :], start=False, stop=True)
                mm.then_inc(st_ready, 1)

            def values(j, c):
                if c == 0:
                    pe.wait_ge(v_added, j + 1)
                pe.wait_ge(exp_done, NCH * j + c + 1)
                for r in range(HPC):
                    h = head(c, r)
                    mm = nc.tensor.matmul(av[:, h * VW:(h + 1) * VW], pt[:, c, r, :], v[:, j, h, :], start=True, stop=True)
                mm.then_inc(av_ready, 1)

            x_transpose(0)
            pe.wait_ge(wt_copied, 4)
            project(0)
            x_transpose(1)
            project(1)
            pe.wait_ge(zeroed, 3)
            for k, (bank, ready) in enumerate(((qt_bank, qt_ready), (kt_bank, kt_ready))):
                transpose_parts(0, k, bank, ready)
            x_transpose(2)
            pe.wait_ge(alibi_done, 2 * NH)
            for c in range(NCH):
                scores(0, 0, c, first=(c == 0))
            for k, (bank, ready) in enumerate(((qt_bank, qt_ready), (kt_bank, kt_ready))):
                transpose_parts(1, k, bank, ready)
            pe.wait_ge(xt_copied, 3)
            max_transpose(0)

            def turn(j, p, nxt, ahead):
                n, q = j + 1, 1 - p
                scores_t(j, p, 0)
                scores_t(j, p, 1)
                if nxt:
                    scores(n, q, 0)
                values(j, 0)
                scores_t(j, p, 2)
                if ahead:
                    project(j + 2)
                if nxt:
                    scores(n, q, 1)
                values(j, 1)
                if ahead:
                    pe.wait_ge(x_done, j)
                    x_transpose(j + 3)
                scores_t(j, p, 3)
                if nxt:
                    scores(n, q, 2)
                values(j, 2)
                if nxt:
                    scores(n, q, 3)
                values(j, 3)
                if ahead:
                    pe.wait_ge(xt_copied, j + 4)
                else:
                    pe.wait_ge(x_done, j)
                if nxt:
                    max_transpose(n)
                if ahead:
                    transpose_parts(j + 2, 0, qt_bank, qt_ready)
                if nxt:
                    pe.wait_ge(nmt_copied, n + 1)
                pe.wait_ge(o_done, j + 1)
                nc.tensor.transpose(ot_ps, on[:, :], pg.ident[:, :]).then_inc(ot_ready, 1)
                if ahead:
                    transpose_parts(j + 2, 1, kt_bank, kt_ready)
                pe.wait_ge(ot_copied, j + 1)
                nc.tensor.matmul(out_ps, ot[:, :], wt[:, 3, :], start=True, stop=True).then_inc(out_ready, 1)

            turns(pe, turn)

        @block.scalar
        def _(act):
            def copy_xt(n):
                act.wait_ge(xt_ready, n + 1)
                nc.scalar.copy(xt[:, :], misc[:, 0:P]).then_inc(xt_copied, 1)

            def copy_parts(n, p, dst, bank, ready, done):
                act.wait_ge(ready, n + 1)
                nc.scalar.copy(dst[p][:, :, :].rearrange("p t l -> p (t l)"), bank[:, :].bitcast(BF16)).then_inc(done, 1)

            def copy_max(n, p):
                act.wait_ge(nmt_ready, n + 1)
                nc.scalar.copy(nmt[p][:, :], nmt_ps).then_inc(nmt_copied, 1)

            def exp(j, c):
                act.wait_ge(st_read, NCH * j + c + 1)
                nc.scalar.activation(pt[:, c, :, :].rearrange("p r l -> p (r l)"), pre[c % 2][:, :], ACT.Exp).then_inc(exp_done, 1)

            copy_xt(0)
            act.wait_ge(qkv_ready, 1)
            copy_xt(1)
            copy_parts(0, 0, qt, qt_bank, qt_ready, qt_copied)
            copy_parts(0, 0, kt, kt_bank, kt_ready, kt_copied)
            copy_xt(2)
            copy_parts(1, 1, qt, qt_bank, qt_ready, qt_copied)
            copy_parts(1, 1, kt, kt_bank, kt_ready, kt_copied)
            copy_max(0, 0)

            def turn(j, p, nxt, ahead):
                n, q = j + 1, 1 - p
                for c in range(3):
                    exp(j, c)
                if ahead:
                    copy_xt(j + 3)
                exp(j, 3)
                if nxt:
                    copy_max(n, q)
                if ahead:
                    copy_parts(j + 2, p, qt, qt_bank, qt_ready, qt_copied)
                act.wait_ge(ot_ready, j + 1)
                nc.scalar.copy(ot[:, :], ot_ps).then_inc(ot_copied, 1)
                if ahead:
                    copy_parts(j + 2, p, kt, kt_bank, kt_ready, kt_copied)

            turns(act, turn)

        @block.vector
        def _(dve):
            V = nc.vector
            o0 = Order(dve, alibi_order)
            dve.wait_ge(iota_done, 1)
            o0.after(V.tensor_copy(dist[:, :], dist_i[:, :]))
            o0.after(V.scalar_tensor_tensor(dist[:, :], dist[:, :], -1.0, dist[:, :], ALU.mult, ALU.max))

            def norm_stats(n):
                V.bn_stats(st[:, :], pg.x[:, n, :]).then_inc(norm_order, 1)

            def wait_stats(n):
                dve.wait_ge(norm_order, 2 * n + 1)

            def norm_aggregate(n):
                V.bn_aggr(mv[:, :], st[:, :]).then_inc(norm_order, 1)
                dve.wait_ge(norm_order, 2 * n + 2)
                V.tensor_scalar(ve[:, :], mv[:, 1:2], EPS, None, ALU.add).then_inc(var_ready, 1)

            def norm_apply(n):
                dve.wait_ge(rstd_ready, n + 1)
                V.tensor_scalar(xn[:, :], pg.x[:, n, :], mv[:, 0:1], rs[:, 0:1], ALU.subtract,
                                ALU.mult).then_inc(xn_ready, 1)

            def split(n):
                dve.wait_ge(qkv_ready, n + 1)
                V.tensor_tensor(qk[:, :, :, :].rearrange("p k h w -> p (k h w)"), qkv[:, 0:2 * D], bqkv[:, 0:2 * D],
                                ALU.add).then_inc(qk_added, 1)
                V.tensor_tensor(v[:, n, :, 0:W], qkv[:, 2 * D:3 * D].rearrange("p (h w) -> p h w", w=W),
                                bqkv[:, 2 * D:3 * D].rearrange("p (h w) -> p h w", w=W), ALU.add).then_inc(v_added, 1)
                o = Order(dve, split_order, n, 3)
                dve.wait_ge(qk_added, n + 1)
                high, middle = parts[:, :, :, 0, :], parts[:, :, :, 1, :]
                o.after(V.tensor_copy(high, qk[:, :, :, :]))
                o.after(V.tensor_tensor(rest[:, :, :, :], qk[:, :, :, :], high, ALU.subtract))
                o.after(V.tensor_copy(middle, rest[:, :, :, :]))
                for k, slots in enumerate((QS["l"], KS["l"])):
                    V.tensor_tensor(parts[:, k, :, slots[0], :], rest[:, k, :, :], middle[:, k], ALU.subtract).then_inc(split_done, 1)
                o.close()

            def row_max(n, c):
                dve.wait_ge(s_ready, NCH * n + c + 1)
                V.tensor_reduce(m[:, heads_of(c)], score[:, :].rearrange("p (h k) -> p h k", k=P), AX, ALU.max,
                                negate=True).then_inc(s_read, 1)

            def split_max(n):
                dve.wait_ge(s_read, NCH * n + NCH)
                V.tensor_copy(nm[:, 0, :], m[:, :]).then_inc(nm_ready, 1)
                dve.wait_ge(nm_ready, 2 * n + 1)
                V.tensor_tensor(nm[:, 1, :], m[:, :], nm[:, 0, :], ALU.subtract).then_inc(nm_ready, 1)

            def add_bias(j, c):
                dve.wait_ge(st_ready, NCH * j + c + 1)
                V.tensor_tensor(pre[c % 2][:, :], score_t[c % 2][:, :], alibi[:, c, :, :].rearrange("p r k -> p (r k)"),
                                ALU.add).then_inc(st_read, 1)

            for n in range(2):
                norm_stats(n)
                wait_stats(n)
                norm_aggregate(n)
                if n:
                    dve.wait_ge(xt_ready, n)
                norm_apply(n)
                if n == 0:
                    dve.wait_ge(wt_ready, 4)
                    for k in range(4):
                        V.tensor_scalar(wt[:, k, :], score_t[0][:, k * P:(k + 1) * P], SCALE if k == 0 else 1.0, None,
                                        ALU.mult).then_inc(wt_copied, 1)
                    V.tensor_scalar(bqkv[:, 0:D], bqkv[:, 0:D], SCALE, None, ALU.mult).then_inc(bias_scaled, 1)
            dve.wait_ge(bias_scaled, 1)
            dve.wait_ge(zeroed, 3)
            split(0)
            norm_stats(2)
            wait_stats(2)
            norm_aggregate(2)
            dve.wait_ge(xt_ready, 2)
            norm_apply(2)
            for c in range(NCH):
                for r in range(HPC):
                    slope = -float(np.float32(2.0 ** (-8.0 * head(c, r) / NH)))
                    for t in (alibi, alibi_bf):
                        V.tensor_scalar(t[:, c, r, :], dist[:, :], slope, None, ALU.mult).then_inc(alibi_done, 1)
            dve.wait_ge(kt_ready, 1)
            split(1)
            for c in range(NCH):
                row_max(0, c)
            split_max(0)
            dve.wait_ge(alibi_done, 2 * NH)

            def turn(j, p, nxt, ahead):
                n = j + 1
                o = Order(dve, order_sem, j, 2)
                if ahead:
                    norm_stats(j + 3)
                    wait_stats(j + 3)
                add_bias(j, 0)
                if ahead:
                    norm_aggregate(j + 3)
                add_bias(j, 1)
                if nxt:
                    row_max(n, 0)
                if ahead:
                    norm_apply(j + 3)
                add_bias(j, 2)
                if ahead:
                    split(j + 2)
                if nxt:
                    row_max(n, 1)
                add_bias(j, 3)
                if nxt:
                    row_max(n, 2)
                    row_max(n, 3)
                    split_max(n)
                dve.wait_ge(av_ready, NCH * j + NCH)
                src = av[:, 0:NH * VW].rearrange("p (h e) -> p h e", e=VW)
                o.after(V.reciprocal(rinv[:, :].unsqueeze(2), src[:, :, W:W + 1]))
                V.tensor_tensor(on[:, :].rearrange("p (h w) -> p h w", w=W), src[:, :, 0:W],
                                bc(rinv[:, :].unsqueeze(2), [P, NH, W]), ALU.mult).then_inc(o_done, 1)
                dve.wait_ge(out_ready, j + 1)
                o.after(V.tensor_tensor(pg.x[:, j, :], out_ps, pg.x[:, j, :], ALU.add))
                V.tensor_tensor(pg.x[:, j, :], pg.x[:, j, :], bo[:, :], ALU.add).then_inc(x_done, 1)
                o.close()

            turns(dve, turn)


def feed_forward(pg, layer):
    with ExitStack() as ctx:
        xt = pg.sbuf(f"ff{layer}_xt", [P, NB, P], ctx=ctx)
        cw = pg.sbuf(f"ff{layer}_cw", [P, NE, NB], ctx=ctx)
        route(pg, layer, xt, cw)
        experts(pg, layer, xt, cw)


def route(pg, layer, xt, cw):
    nc, a = pg.nc, pg.a
    K = 2 if layer else 1
    with ExitStack() as ctx:
        (loaded, var_ready, rstd_ready, xn_ready, xt_ready, xt_copied, wt_ready, wt_copied, lg_ready, sub_done, e_done,
         ones_done, lower_done, order_sem) = pg.sems(f"rt{layer}", (
            "loaded var_ready rstd_ready xn_ready xt_ready xt_copied wt_ready wt_copied logits_ready shifted exp_done "
            "ones_done lower_done order"))
        sb = lambda n, s: pg.sbuf(f"rt{layer}_{n}", s, ctx=ctx)
        st, mv, ve, rs, xn = norm_all_buffers(pg, ctx, f"rt{layer}")
        w = sb("w", [P, K * NE])
        w_nat = sb("w_nat", [NE, D])
        lg, mx, sm = sb("lg", [P, NB, K, NE]), sb("mx", [P, NB, K]), sb("sm", [P, NB, K])
        pr = sb("pr", [P, NB, K, NE])
        lower = sb("lower", [P, NE, NE])
        gt, eq, rank = sb("gt", [P, NB, NE, NE]), sb("eq", [P, NB, NE, NE]), sb("rank", [P, NB, NE])
        block = ctx.enter_context(nc.Block())

        @block.sync
        def _(sp):
            if layer:
                with nc.allow_non_contiguous_dma("router weights"):
                    sp.dma_start(w[:, 0:NE], a["L1_ffn_w_router"]).then_inc(loaded, 16)
                    sp.dma_start(w[:, NE:2 * NE], a["L1_ffn_w_gating"]).then_inc(loaded, 16)
            else:
                sp.dma_start(w_nat[:, :], a["L0_ffn_router_w"]).then_inc(loaded, 16)

        @block.gpsimd
        def _(pool):
            nc.gpsimd.memset(lower[:, :, :], 1.0).then_inc(ones_done, 1)
            pool.wait_ge(ones_done, 1)
            nc.gpsimd.affine_select(out=lower[:, :, :], in_=lower[:, :, :], compare_op=ALU.is_gt, fill=0.0, base=0,
                                    pattern=[[1, NE], [-1, NE]], channel_multiplier=0).then_inc(lower_done, 1)
            pool.wait_ge(var_ready, 1)
            nc.gpsimd.tensor_tensor(rs[:, :], ve[:, :], pg.neg_half[:, :], ALU.pow).then_inc(rstd_ready, 1)

        @block.tensor
        def _(pe):
            pe.wait_ge(loaded, 16 * K)
            if not layer:
                nc.tensor.transpose(pg.bank[3][:, 0:NE], w_nat[:, :], pg.ident[0:NE, 0:NE]).then_inc(wt_ready, 1)
            for b in range(NB):
                pe.wait_ge(xn_ready, b + 1)
                nc.tensor.transpose(pg.bank[b // 4][:, (b % 4) * P:(b % 4 + 1) * P], xn[:, b, :],
                                    pg.ident[:, :]).then_inc(xt_ready, 1)
            if not layer:
                pe.wait_ge(wt_copied, 1)
            for b in range(NB):
                pe.wait_ge(xt_copied, b // 4 + 1)
                mm = nc.tensor.matmul(pg.bank[2][:, b * K * NE:(b + 1) * K * NE], xt[:, b, :], w[:, :],
                                      start=True, stop=True)
            mm.then_inc(lg_ready, 1)

        @block.scalar
        def _(act):
            if not layer:
                act.wait_ge(wt_ready, 1)
                nc.scalar.copy(w[:, :], pg.bank[3][:, 0:NE]).then_inc(wt_copied, 1)
            for h in range(2):
                act.wait_ge(xt_ready, 4 * h + 4)
                nc.scalar.copy(xt[:, 4 * h:4 * h + 4, :].rearrange("p b l -> p (b l)"),
                               pg.bank[h][:, :]).then_inc(xt_copied, 1)
            act.wait_ge(sub_done, 1)
            nc.scalar.activation(lg[:, :, :, :], lg[:, :, :, :], ACT.Exp).then_inc(e_done, 1)

        @block.vector
        def _(dve):
            o, V = Order(dve, order_sem), nc.vector
            norm_all(pg, dve, o, st, mv, ve, var_ready, rstd_ready, rs, xn, xn_ready)
            dve.wait_ge(lg_ready, 1)
            src = pg.bank[2][:, 0:NB * K * NE].rearrange("p (b k e) -> p b k e", b=NB, k=K)
            for k in range(K):
                o.mark(V.tensor_scalar(lg[:, :, k, :], src[:, :, k, :], 10.0 if k else 1.0, None, ALU.mult))
            o.wait()
            o.after(V.tensor_reduce(mx[:, :, :], lg[:, :, :, :], AX, ALU.max))
            V.tensor_tensor(lg[:, :, :, :], lg[:, :, :, :], bc(mx[:, :, :].unsqueeze(3), [P, NB, K, NE]),
                            ALU.subtract).then_inc(sub_done, 1)
            dve.wait_ge(e_done, 1)
            o.after(V.tensor_reduce(sm[:, :, :], lg[:, :, :, :], AX, ALU.add))
            o.after(V.reciprocal(sm[:, :, :], sm[:, :, :]))
            o.after(V.tensor_tensor(pr[:, :, :, :], lg[:, :, :, :], bc(sm[:, :, :].unsqueeze(3), [P, NB, K, NE]), ALU.mult))
            cw_be = cw[:, :, :].rearrange("p e b -> p b e")
            if layer:
                both = pr[:, :, 0, :]
                o.after(V.tensor_tensor(both, both, pr[:, :, 1, :], ALU.mult))
                o.after(V.tensor_reduce(rank[:, :, 0], both, AX, ALU.add))
                o.after(V.tensor_scalar(rank[:, :, 0], rank[:, :, 0], 1e-9, None, ALU.add))
                o.after(V.reciprocal(rank[:, :, 0], rank[:, :, 0]))
                o.after(V.tensor_tensor(cw_be, both, bc(rank[:, :, 0:1], [P, NB, NE]), ALU.mult))
            else:
                dve.wait_ge(lower_done, 1)
                other = bc(pr[:, :, 0:1, :], [P, NB, NE, NE])
                own = bc(pr[:, :, 0, :].unsqueeze(3), [P, NB, NE, NE])
                o.mark(V.tensor_tensor(gt[:, :, :, :], other, own, ALU.is_gt))
                o.after(V.tensor_tensor(eq[:, :, :, :], other, own, ALU.is_equal))
                o.after(V.tensor_tensor(eq[:, :, :, :], eq[:, :, :, :], bc(lower[:, :, :].unsqueeze(1), [P, NB, NE, NE]), ALU.mult))
                o.after(V.tensor_tensor(gt[:, :, :, :], gt[:, :, :, :], eq[:, :, :, :], ALU.add))
                o.after(V.tensor_reduce(rank[:, :, :], gt[:, :, :, :], AX, ALU.add))
                o.after(V.tensor_scalar(rank[:, :, :], rank[:, :, :], 1.5, None, ALU.is_lt))
                o.after(V.tensor_tensor(cw_be, rank[:, :, :], pr[:, :, 0, :], ALU.mult))


def experts(pg, layer, xt, cw):
    nc, a = pg.nc, pg.a
    FT = 4 if layer else 2
    TB = HALF // P
    F = FT * P
    with ExitStack() as ctx:
        (w_in_even, w_in_odd, wt_ready, wt_copied, gu_ready, act_done, h_done, y_ready, x_done) = pg.sems(f"ex{layer}", (
            "even_weights_in odd_weights_in weights_transposed weights_copied gate_up_ready act_done h_done y_ready x_done"))
        sb = lambda n, s: pg.sbuf(f"ex{layer}_{n}", s, ctx=ctx)
        gate = [sb(f"gate{p}", [P, F]) for p in range(2)]
        up = [sb(f"up{p}", [P, F]) for p in range(2)]
        down = [sb(f"down{p}", [P, FT, D]) for p in range(2)]
        if not layer:
            w1 = [sb(f"w1_{p}", [P, 2 * FT, D]) for p in range(2)]
            w2 = [sb(f"w2_{p}", [P, F]) for p in range(2)]
        s = sb("s", [P, 2, HALF])
        h = [sb(f"h{n}", [P, FT, HALF]) for n in range(2)]
        gate_ps, up_ps, y_ps, wt_ps = pg.bank[0:2], pg.bank[2:4], pg.bank[4:6], pg.bank[6:8]
        flat = xt[:, :, :].rearrange("p b l -> p (b l)")
        w_in = (w_in_even, w_in_odd)
        N_W = 3 if layer else 2
        PER = 2 * FT
        block = ctx.enter_context(nc.Block())

        @block.sync
        def _(sp):
            def load(e, p):
                if layer:
                    sp.dma_start(gate[p][:, :], a["L1_ffn_w_gate"][e]).then_inc(w_in[p], 16)
                    sp.dma_start(up[p][:, :], a["L1_ffn_w_up"][e]).then_inc(w_in[p], 16)
                    sp.dma_start(down[p][:, :, :], a["L1_ffn_w_down"][e].rearrange("(t p) d -> p t d", p=P)).then_inc(w_in[p], 16)
                else:
                    sp.dma_start(w1[p][:, :, :], a["L0_ffn_w1"][e].rearrange("(t p) d -> p t d", p=P)).then_inc(w_in[p], 16)
                    sp.dma_start(w2[p][:, :], a["L0_ffn_w2"][e]).then_inc(w_in[p], 16)

            for p in range(2):
                load(p, p)
            with sp.Fori(1, NE // 2) as i:
                for p in range(2):
                    if layer:
                        sp.wait_ge(y_ready, 4 * i + 2 * p - 2)
                    else:
                        sp.wait_ge(wt_ready, (2 * i + p - 1) * 3 * FT)
                    load(2 * i + p, p)

        @block.tensor
        def _(pe):
            with pe.Fori(0, NE // 2) as i:
                for p in range(2):
                    e = 2 * i + p
                    pe.wait_ge(w_in[p], 16 * N_W * i + 16 * N_W)
                    if not layer:
                        pe.wait_ge(wt_copied, 3 * e)
                        for t in range(2 * FT):
                            nc.tensor.transpose(wt_ps[0][:, t * P:(t + 1) * P], w1[p][:, t, :], pg.ident[:, :]).then_inc(wt_ready, 1)
                        for t in range(FT):
                            nc.tensor.transpose(wt_ps[1][:, t * P:(t + 1) * P], w2[p][:, t * P:(t + 1) * P], pg.ident[:, :]).then_inc(wt_ready, 1)
                        pe.wait_ge(wt_copied, 3 * e + 3)

                    def hidden(n, t):
                        k = n * FT + t
                        pe.wait_ge(h_done, PER * e if k < 2 else PER * e + k - 1)
                        cols = slice(n * HALF, (n + 1) * HALF)
                        nc.tensor.matmul(gate_ps[k % 2][:, :], gate[p][:, t * P:(t + 1) * P], flat[:, cols], start=True, stop=True)
                        nc.tensor.matmul(up_ps[k % 2][:, :], up[p][:, t * P:(t + 1) * P], flat[:, cols], start=True,
                                         stop=True).then_inc(gu_ready, 1)

                    def output(n):
                        pe.wait_ge(h_done, PER * e + (n + 1) * FT)
                        pe.wait_ge(x_done, 2 * e)
                        for b in range(TB):
                            for t in range(FT):
                                mm = nc.tensor.matmul(y_ps[n][:, b * D:(b + 1) * D], h[n][:, t, b * P:(b + 1) * P],
                                                      down[p][:, t, :], start=(t == 0), stop=(t == FT - 1))
                        mm.then_inc(y_ready, 1)

                    for t in range(FT):
                        hidden(0, t)
                    hidden(1, 0)
                    output(0)
                    for t in range(1, FT):
                        hidden(1, t)
                    output(1)

        @block.scalar
        def _(act):
            with act.Fori(0, NE // 2) as i:
                for p in range(2):
                    e = 2 * i + p
                    if not layer:
                        act.wait_ge(wt_ready, 3 * FT * e + 2 * FT)
                        nc.scalar.copy(gate[p][:, :], wt_ps[0][:, 0:F]).then_inc(wt_copied, 1)
                        nc.scalar.copy(up[p][:, :], wt_ps[0][:, F:2 * F]).then_inc(wt_copied, 1)
                        act.wait_ge(wt_ready, 3 * FT * e + 3 * FT)
                        nc.scalar.copy(down[p][:, :, :].rearrange("p t d -> p (t d)"), wt_ps[1][:, 0:F]).then_inc(wt_copied, 1)
                    for k in range(PER):
                        act.wait_ge(gu_ready, PER * e + k + 1)
                        nc.scalar.activation(s[:, k % 2, :], gate_ps[k % 2][:, :], ACT.Silu).then_inc(act_done, 1)

        @block.vector
        def _(dve):
            V = nc.vector
            with dve.Fori(0, NE // 2) as i:
                for p in range(2):
                    e = 2 * i + p

                    def add(n):
                        dve.wait_ge(y_ready, 2 * e + n + 1)
                        if n == 0:
                            dve.wait_ge(x_done, 2 * e)
                        for b in range(TB):
                            ins = V.scalar_tensor_tensor(pg.x[:, n * TB + b, :], y_ps[n][:, b * D:(b + 1) * D],
                                                         cw[:, e, n * TB + b:n * TB + b + 1], pg.x[:, n * TB + b, :], ALU.mult, ALU.add)
                        ins.then_inc(x_done, 1)

                    for k in range(PER):
                        dve.wait_ge(act_done, PER * e + k + 1)
                        V.tensor_tensor(h[k // FT][:, k % FT, :], s[:, k % 2, :], up_ps[k % 2][:, :], ALU.mult).then_inc(h_done, 1)
                        if k == FT + 1:
                            add(0)
                    add(1)


def cross(pg, layer):
    with ExitStack() as ctx:
        w = cross_weights(pg, ctx, layer)
        if layer:
            fold_low_rank(pg, w)
        else:
            loaded, = pg.sems("cw0", "loaded")
            with pg.nc.Block() as block:
                @block.sync
                def _(sp):
                    n = load_cross_weights(pg, sp, w, 0, loaded)
                    sp.wait_ge(loaded, n)
        cross_attention(pg, w, layer)


def store(pg):
    nc = pg.nc
    with ExitStack() as ctx:
        out_done, = pg.sems("st", "out_done")
        block = ctx.enter_context(nc.Block())

        @block.sync
        def _(sp):
            sp.dma_start(pg.out.rearrange("b l d -> l b d"), pg.x[:, 0:NB, :]).then_inc(out_done, 16)
            sp.wait_ge(out_done, 16)


def decoder(nc, a, out):
    with ExitStack() as ctx:
        pg = Program(nc, ctx, a, out)
        setup(pg)
        state_space(pg)
        cross(pg, 0)
        feed_forward(pg, 0)
        self_attention(pg)
        pg.recycle_sems()
        cross(pg, 1)
        feed_forward(pg, 1)
        store(pg)


_INS = [
    'x', 'ctx_768', 'L0_attn_W_in', 'L0_attn_W_out', 'L0_attn_dt_bias', 'L0_attn_D_param', 'L0_attn_Bn_g',
    'L0_attn_Bn_b', 'L0_attn_Cn_g', 'L0_attn_Cn_b', 'L0_xattn_w_q', 'L0_xattn_w_kv', 'L0_xattn_w_out',
    'L0_xattn_b_out', 'L0_ffn_w1', 'L0_ffn_w2', 'L0_ffn_router_w', 'L1_attn_W_qkv', 'L1_attn_b_qkv',
    'L1_attn_W_out', 'L1_attn_b_out', 'L1_xattn_Wq', 'L1_xattn_Wk', 'L1_xattn_Wv', 'L1_xattn_Wo', 'L1_xattn_bo',
    'L1_xattn_q_down', 'L1_xattn_q_up', 'L1_xattn_q_alpha', 'L1_xattn_k_down', 'L1_xattn_k_up',
    'L1_xattn_k_alpha', 'L1_xattn_v_down', 'L1_xattn_v_up', 'L1_xattn_v_alpha', 'L1_xattn_o_down',
    'L1_xattn_o_up', 'L1_xattn_o_alpha', 'L1_xattn_Wk_ipa', 'L1_xattn_Wv_ipa', 'L1_ffn_w_router',
    'L1_ffn_w_gating', 'L1_ffn_w_gate', 'L1_ffn_w_up', 'L1_ffn_w_down'
]
_OUT_SHAPE = (NB, P, D)


def kernel(**inputs):
    import concourse.bacc as _bacc
    from concourse import mybir as _mybir
    from concourse.bass_utils import run_bass_kernel_spmd as _run

    nc = _bacc.Bacc("TRN2", target_bir_lowering=False, num_devices=1)
    arrays, args = {}, {}
    for name in _INS:
        v = np.ascontiguousarray(inputs[name])
        arrays[f"in_{name}_dram"] = v
        args[name] = nc.dram_tensor(f"in_{name}_dram", v.shape, _mybir.dt.from_np(v.dtype), kind="ExternalInput").ap()
    out = nc.dram_tensor("out_0_dram", _OUT_SHAPE, _mybir.dt.float32, kind="ExternalOutput").ap()
    decoder(nc, args, out)
    r = _run(nc, [arrays], core_ids=[0])
    return r.results[0]["out_0_dram"]
```

```python
from contextlib import ExitStack

import numpy as np

import concourse.bass as bass
from concourse import mybir

F32 = mybir.dt.float32
BF16 = mybir.dt.bfloat16
F32R = mybir.dt.float32r
ALU = mybir.AluOpType
ACT = mybir.ActivationFunctionType
AX = mybir.AxisListType.X

P = 128
NB = 8
D = 128
DC = 96
EPS = 1e-5
NH = 16
HD = 64
INNER = NH * HD
NT = INNER // P
VS = HD + 2
NCH = 4
HPC = NH // NCH
NE = 8
HALF = NB * P // 2
RANK = 32
IPA = 4
DI = 256
SH = 4
NS = 64
NA = 32


class Order:

    def __init__(self, eng, sem, i=0, per=0):
        self.eng, self.sem, self.i, self.per, self.n = eng, sem, i, per, 0

    def mark(self, ins):
        ins.then_inc(self.sem, 1)
        self.n += 1
        return self.n

    def wait(self, n=None):
        self.eng.wait_ge(self.sem, self.i * self.per + (self.n if n is None else n))

    def after(self, ins):
        self.mark(ins)
        self.wait()

    def close(self):
        assert self.n == self.per, f"the body has {self.n} ordered steps"


def bc(ap, shape):
    return ap.to_broadcast(list(shape))


class Program:

    def __init__(self, nc, ctx, a, out):
        self.nc, self.ctx, self.a, self.out = nc, ctx, a, out
        sb, self.sb = self.sbuf, self.sbuf
        self.bank = [ctx.enter_context(nc.psum_tensor(f"bank{n}", [P, 512], F32)) for n in range(8)]
        self.x = sb("x", [P, NB + 1, D])
        self.ctx_t = sb("ctx_t", [DC, NB + 1, P])
        self.ident = sb("ident", [P, P])
        self.ident_bf = sb("ident_bf", [P, P], BF16)
        self.sel = sb("sel", [P, NH, P], BF16)
        self.live_sems = []
        self.neg_half = sb("neg_half", [P, NB])
        self.zero = sb("zero", [P, 1])
        self.first = sb("first", [P, 1])
        self.dist_i, self.dist = sb("dist_i", [P, P], mybir.dt.int32), sb("dist", [P, P])
        self.alibi, self.alibi_bf = sb("alibi", [P, NCH, HPC, P]), sb("alibi_bf", [P, NCH, HPC, P], BF16)
        self.in_sem = {n: ctx.enter_context(nc.semaphore(f"{n}_in")) for n in (
            "w_in", "ssm_par", "w_out", "cross0", "self", "cross1")}
        self.in_count = dict.fromkeys(self.in_sem, 0)
        self.ssm = {"w_in": sb("ss_w_in", [P, 2 * DI + 2 * NS + 3 * SH + NA]), "gb": sb("ss_gb", [P, 2, 2, NS]),
                    "dtb": sb("ss_dtb", [P, SH]), "dpar": sb("ss_dpar", [P, SH]), "w_out": sb("ss_w_out", [P, 2, D])}
        self.cross_w = [cross_weights(self, layer) for layer in range(2)]
        self.self_w = {"w_nat": sb("sa_w_nat", [P, 4, D]), "bqkv": sb("sa_bqkv", [P, 3 * D]), "bo": sb("sa_bo", [P, D])}

    def load(self, sp, group, dst, src):
        sp.dma_start(dst, src).then_inc(self.in_sem[group], 16)
        self.in_count[group] += 16

    def wait_loads(self, eng, group):
        eng.wait_ge(self.in_sem[group], self.in_count[group])

    def sbuf(self, name, shape, dt=F32, ctx=None):
        return (ctx or self.ctx).enter_context(self.nc.sbuf_tensor("sb_" + name, shape, dt))

    def sems(self, prefix, names):
        got = [self.nc.alloc_semaphore(name=f"{prefix}_{n}") for n in names.split()]
        self.live_sems += got
        return got

    def recycle_sems(self):
        self.nc.clear_and_free_semaphores(self.live_sems)
        self.live_sems = []
        self.nc.all_engine_barrier()


def heads_of(c):
    return slice(2 * HPC * (c // 2) + c % 2, 2 * HPC * (c // 2 + 1), 2)


def head(c, r):
    return 2 * HPC * (c // 2) + c % 2 + 2 * r


def load_first_weights(pg, sp):
    a, ssm = pg.a, pg.ssm
    pg.load(sp, "w_in", ssm["w_in"][:, :], a["L0_attn_W_in"])
    for k, n in enumerate(("Bn_g", "Cn_g", "Bn_b", "Cn_b")):
        pg.load(sp, "ssm_par", ssm["gb"][:, k // 2, k % 2, :], a["L0_attn_" + n].partition_broadcast(P))
    pg.load(sp, "ssm_par", ssm["dtb"][:, :], a["L0_attn_dt_bias"].partition_broadcast(P))
    pg.load(sp, "ssm_par", ssm["dpar"][:, :], a["L0_attn_D_param"].partition_broadcast(P))


def load_later_weights(pg, sp):
    a, sw = pg.a, pg.self_w
    pg.load(sp, "w_out", pg.ssm["w_out"][:, :, :], a["L0_attn_W_out"].rearrange("(t p) d -> p t d", p=P))
    load_cross_weights(pg, sp, 0)
    pg.load(sp, "self", sw["w_nat"][:, 0:3, :], a["L1_attn_W_qkv"].rearrange("(t p) d -> p t d", p=P))
    pg.load(sp, "self", sw["w_nat"][:, 3, :], a["L1_attn_W_out"])
    pg.load(sp, "self", sw["bqkv"][:, :], a["L1_attn_b_qkv"].partition_broadcast(P))
    pg.load(sp, "self", sw["bo"][:, :], a["L1_attn_b_out"].partition_broadcast(P))
    load_cross_weights(pg, sp, 1)


def setup(pg):
    nc, a = pg.nc, pg.a
    with ExitStack() as ctx:
        x_in, ctx_in, zeroed, const_done, ctx_tr, ctx_cp, iota_done, dist_done = pg.sems(
            "su", "x_in ctx_in zeroed const_done ctx_transposed ctx_copied iota_done dist_done")
        ctx_sb = pg.sbuf("ctx_sb", [P, NB, DC], ctx=ctx)
        block = ctx.enter_context(nc.Block())

        @block.sync
        def _(sp):
            sp.dma_start(ctx_sb[:, :, :], a["ctx_768"].rearrange("b k c -> k b c")).then_inc(ctx_in, 16)
            sp.dma_start(pg.x[:, 0:NB, :], a["x"].rearrange("b l d -> l b d")).then_inc(x_in, 16)
            load_first_weights(pg, sp)
            sp.wait_ge(x_in, 16)

        @block.gpsimd
        def _(pool):
            nc.gpsimd.iota(pg.dist_i[:, :], pattern=[[-1, P]], base=0, channel_multiplier=1).then_inc(iota_done, 1)
            for n, t in enumerate((pg.ident, pg.ident_bf, pg.sel)):
                nc.gpsimd.memset(t[:], 0.0).then_inc(zeroed, 1)
            nc.gpsimd.memset(pg.neg_half[:, :], -0.5).then_inc(const_done, 1)
            nc.gpsimd.memset(pg.zero[:, :], 0.0).then_inc(const_done, 1)
            nc.gpsimd.memset(pg.x[:, NB, :], 0.0).then_inc(const_done, 1)
            nc.gpsimd.memset(pg.ctx_t[:, NB, :], 0.0).then_inc(const_done, 1)
            pool.wait_ge(zeroed, 3)
            for t in (pg.ident, pg.ident_bf):
                nc.gpsimd.affine_select(out=t[:, :], in_=t[:, :], compare_op=ALU.not_equal, fill=1.0,
                                        base=0, pattern=[[-1, P]], channel_multiplier=1).then_inc(const_done, 1)
            for part in range(2):
                pool.wait_ge(const_done, 6 + part)
                nc.gpsimd.affine_select(out=pg.sel[:, :, :], in_=pg.sel[:, :, :], compare_op=ALU.not_equal,
                                        fill=1.0, base=-part * NH, pattern=[[-1, NH], [0, P]],
                                        channel_multiplier=1).then_inc(const_done, 1)

        @block.vector
        def _(dve):
            dve.wait_ge(iota_done, 1)
            nc.vector.tensor_copy(pg.dist[:, :], pg.dist_i[:, :]).then_inc(dist_done, 1)
            dve.wait_ge(dist_done, 1)
            nc.vector.scalar_tensor_tensor(pg.dist[:, :], pg.dist[:, :], -1.0, pg.dist[:, :], ALU.mult, ALU.max).then_inc(dist_done, 1)

        @block.tensor
        def _(pe):
            pe.wait_ge(const_done, 6)
            pe.wait_ge(ctx_in, 16)
            for b in range(NB):
                nc.tensor.transpose(pg.bank[b // 4][0:DC, (b % 4) * P:(b % 4 + 1) * P], ctx_sb[:, b, :],
                                    pg.ident[:, :]).then_inc(ctx_tr, 1)

        @block.scalar
        def _(act):
            for h in range(2):
                act.wait_ge(ctx_tr, 4 * h + 4)
                nc.scalar.copy(pg.ctx_t[:, 4 * h:4 * h + 4, :].rearrange("c b k -> c (b k)"),
                               pg.bank[h][0:DC, :]).then_inc(ctx_cp, 1)


def norm_all(pg, dve, order, st, mv, ve, var_ready, rstd_ready, rs, xn, xn_ready):
    nc = pg.nc
    for b in range(NB):
        order.mark(nc.vector.bn_stats(st[:, b, :], pg.x[:, b, :]))
    for b in range(NB):
        order.wait(b + 1)
        order.mark(nc.vector.bn_aggr(mv[:, b, :], st[:, b, :]))
    order.wait()
    nc.vector.tensor_scalar(ve[:, :], mv[:, :, 1], EPS, None, ALU.add).then_inc(var_ready, 1)
    dve.wait_ge(rstd_ready, 1)
    for b in range(NB):
        nc.vector.tensor_scalar(xn[:, b, :], pg.x[:, b, :], mv[:, b, 0:1], rs[:, b:b + 1],
                                ALU.subtract, ALU.mult).then_inc(xn_ready, 1)


def norm_all_buffers(pg, ctx, name):
    return (pg.sbuf(f"{name}_st", [P, NB, 6], ctx=ctx), pg.sbuf(f"{name}_mv", [P, NB, 2], ctx=ctx),
            pg.sbuf(f"{name}_ve", [P, NB], ctx=ctx), pg.sbuf(f"{name}_rs", [P, NB], ctx=ctx),
            pg.sbuf(f"{name}_xn", [P, NB, D], ctx=ctx))


def state_space(pg):
    nc, a = pg.nc, pg.a
    with ExitStack() as outer:
        zx = pg.sbuf("ss_zx", [P, NB, 2 * DI], ctx=outer)
        sz = pg.sbuf("ss_sz", [P, NB, DI], ctx=outer)
        br = pg.sbuf("ss_br", [P, NB, 2, NS], ctx=outer)
        logd = pg.sbuf("ss_logd", [P, NB, SH], ctx=outer)
        past = pg.sbuf("ss_past", [P, NB, SH], ctx=outer)
        now = pg.sbuf("ss_now", [P, NB, SH], ctx=outer)
        upper = pg.sbuf("ss_upper", [P, P], ctx=outer)
        strict = pg.sbuf("ss_strict", [P, P], ctx=outer)
        after = pg.sbuf("ss_after", [P, P], ctx=outer)
        state_space_project(pg, zx, sz, br, logd, past, now, upper, strict, after)
        state_space_mix(pg, zx, sz, br, logd, past, now, upper, strict, after)


class FoldLowRank:

    NI = NB * IPA

    def __init__(self, pg, ctx):
        self.pg, self.w = pg, pg.cross_w[1]
        (self.tr_ready, self.tr_copied, self.prod_ready, self.prod_scaled, self.folded, self.img_ready, self.spread,
         self.zeroed, self.wq_t_ready, self.wq_t_copied) = pg.sems("fl", (
            "down_transposed down_copied product_ready product_scaled folded image_kv_ready image_kv_spread "
            "zeroed wq_transposed wq_copied"))
        sb = lambda n, s: pg.sbuf(f"fl_{n}", s, ctx=ctx)
        self.down_t = {n: sb(f"down_t_{n}", [RANK, INNER if n == "o" else P]) for n in "qkvo"}
        self.scaled = [sb(f"scaled{p}", [P, 512]) for p in range(2)]
        self.img2, self.wq_t = self.w["img2"], self.w["wq_t"]
        bank = pg.bank
        self.down_ps, self.down_o_ps, self.img_ps = bank[0], bank[1:3], bank[3]
        self.prod_ps = (bank[4], bank[5], bank[0], bank[1])
        self.wq_t_ps = bank[2:4]

    def halves(self):
        for m, c in enumerate("qkvo"):
            for h in range(2):
                dst = self.w["o"][:, 4 * h:4 * h + 4, :].rearrange("p t d -> p (t d)") if c == "o" else \
                    self.w[c][:, 512 * h:512 * (h + 1)]
                yield 2 * m + h, m, c, h, P if c in "qo" else DC, dst

    def tensor_transposes(self, pe, zx_copied):
        pg, w, nc = self.pg, self.w, self.pg.nc
        pg.wait_loads(pe, "cross1")
        for m, c in enumerate("qkv"):
            rows = P if c == "q" else DC
            nc.tensor.transpose(self.down_ps[0:RANK, m * P:m * P + rows], w["down"][c][:, :],
                                pg.ident[0:rows, 0:rows]).then_inc(self.tr_ready, 1)
        for t in range(NT):
            if t == 4:
                pe.wait_ge(zx_copied, NB - 1)
            nc.tensor.transpose(self.down_o_ps[t // 4][0:RANK, (t % 4) * P:(t % 4 + 1) * P], w["down_o"][:, t, :],
                                pg.ident[:, :]).then_inc(self.tr_ready, 1)
        pe.wait_ge(zx_copied, NB)
        for k in range(2):
            for t in range(NT):
                mm = nc.tensor.matmul(self.img_ps[:, (NT * k + t) * self.NI:(NT * k + t + 1) * self.NI],
                                      w["ipa"][k][:, t * P:(t + 1) * P], pg.ctx_t[:, 0:NB, P - IPA:P],
                                      start=True, stop=True)
        mm.then_inc(self.img_ready, 1)

    def tensor_products(self, pe, small_copied):
        pg, w, nc = self.pg, self.w, self.pg.nc
        pe.wait_ge(self.tr_copied, 5)
        pe.wait_ge(small_copied, NB)
        for k, m, c, h, rows, dst in self.halves():
            ps = self.prod_ps[k % 4]
            if k >= 4:
                pe.wait_ge(self.prod_scaled, k - 3)
            if c != "o":
                mm = nc.tensor.matmul(ps[0:rows, :], self.down_t[c][:, 0:rows], w["up"][c][:, 512 * h:512 * (h + 1)],
                                      start=True, stop=True)
            else:
                for t in range(4):
                    mm = nc.tensor.matmul(ps[:, t * P:(t + 1) * P], self.down_t[c][:, (4 * h + t) * P:(4 * h + t + 1) * P],
                                          w["up"][c][:, :], start=True, stop=True)
            mm.then_inc(self.prod_ready, 1)
        pe.wait_ge(self.spread, 4)
        pe.wait_ge(self.folded, 2)
        for t in range(NT):
            nc.tensor.transpose(self.wq_t_ps[t // 4][:, (t % 4) * P:(t % 4 + 1) * P], w["q"][:, t * P:(t + 1) * P],
                                pg.ident[:, :]).then_inc(self.wq_t_ready, 1)

    def scalar_transposes(self, act):
        nc = self.pg.nc
        for m, c in enumerate("qkv"):
            rows = P if c == "q" else DC
            act.wait_ge(self.tr_ready, 3)
            nc.scalar.mul(self.down_t[c][:, 0:rows], self.down_ps[0:RANK, m * P:m * P + rows], 1 / RANK).then_inc(self.tr_copied, 1)
        for h in range(2):
            act.wait_ge(self.tr_ready, 3 + 4 * h + 4)
            nc.scalar.mul(self.down_t["o"][:, 512 * h:512 * (h + 1)], self.down_o_ps[h][0:RANK, :], 1 / RANK).then_inc(self.tr_copied, 1)
        act.wait_ge(self.img_ready, 1)
        act.wait_ge(self.zeroed, 2)
        for k in range(2):
            for g in range(2):
                rows = slice(64 * g, 64 * g + 64)
                nc.scalar.copy(self.img2[k][rows, :, g, :], self.img_ps[rows, NT * k * self.NI:NT * (k + 1) * self.NI].rearrange(
                    "p (t n) -> p t n", t=NT)).then_inc(self.spread, 1)

    def scalar_products(self, act):
        nc, w = self.pg.nc, self.w
        for k, m, c, h, rows, dst in self.halves():
            act.wait_ge(self.prod_ready, k + 1)
            if k >= 2:
                act.wait_ge(self.folded, k - 1)
            nc.scalar.activation(self.scaled[k % 2][0:rows, :], self.prod_ps[k % 4][0:rows, :], ACT.Identity,
                                 scale=w["alpha"][0:rows, m:m + 1]).then_inc(self.prod_scaled, 1)
        for h in range(2):
            act.wait_ge(self.wq_t_ready, 4 * h + 4)
            nc.scalar.copy(self.wq_t[:, 4 * h:4 * h + 4, :].rearrange("p t d -> p (t d)"), self.wq_t_ps[h][:, :]).then_inc(self.wq_t_copied, 1)

    def gpsimd_zeros(self, pool):
        for t in self.img2:
            self.pg.nc.gpsimd.memset(t[:, :, :, :], 0.0).then_inc(self.zeroed, 1)

    def gpsimd_sums(self, pool):
        for k, m, c, h, rows, dst in self.halves():
            pool.wait_ge(self.prod_scaled, k + 1)
            self.pg.nc.gpsimd.tensor_tensor(dst, dst, self.scaled[k % 2][0:rows, :], ALU.add).then_inc(self.folded, 1)


def alibi_chunk(pg, c, done):
    for r in range(HPC):
        slope = -float(np.float32(2.0 ** (-8.0 * head(c, r) / NH)))
        for t in (pg.alibi, pg.alibi_bf):
            pg.nc.gpsimd.tensor_scalar(t[:, c, r, :], pg.dist[:, :], slope, None, ALU.mult).then_inc(done, 1)


def state_space_project(pg, zx, sz, br, logd, past, now, upper, strict, after):
    nc, a = pg.nc, pg.a
    NBC = 2 * NS + 3 * SH + NA
    AN = 2 * NS + 3 * SH
    with ExitStack() as ctx:
        (var_ready, rstd_ready, xn_ready, xt_ready, xt_copied, zx_ready, small_ready, zx_copied,
         small_copied, bc_var_ready, bc_rstd_ready, masks0, masks_done, order_sem, sp_in, sp_exp, sp_one, sp_ln, sg_done,
         phase_in, phase_ready, trig_in, trig_done, adt_ready, dec_done, shift_in, shifted, silu_done, alibi_done) = pg.sems("sp", (
            "var_ready rstd_ready xn_ready xt_ready xt_copied zx_ready small_ready zx_copied "
            "small_copied bc_var_ready bc_rstd_ready masks_zeroed masks_done order softplus_in softplus_exp softplus_one "
            "softplus_ln sigmoid_done phase_in phase_ready trig_in trig_done adt_ready decay_done shift_in shifted silu_done alibi_done"))
        sb = lambda n, s: pg.sbuf("sp_" + n, s, ctx=ctx)
        w_in, gb, dtb, dpar = (pg.ssm[n] for n in ("w_in", "gb", "dtb", "dpar"))
        st, mv, ve, rs, xn = norm_all_buffers(pg, ctx, "sp")
        xt = sb("xt", [P, NB, P])
        sm = sb("sm", [P, NB, NBC])
        bst = sb("bst", [P, NB, 2, 6])
        bmv = sb("bmv", [P, NB, 2, 2])
        bve = sb("bve", [P, 2 * NB])
        brs = sb("brs", [P, 2 * NB])
        half2 = sb("half2", [P, 2 * NB])
        bn = sb("bn", [P, NB, 2, NS])
        shift = sb("shift", [P, P])
        u = sb("u", [P, NB, 2, SH])
        au = sb("au", [P, NB, 2, SH])
        eu = sb("eu", [P, NB, 2, SH])
        lu = sb("lu", [P, NB, 2, SH])
        pu = sb("pu", [P, NB, 2, SH])
        tr = sb("tr", [P, NB, SH])
        te = sb("te", [P, NB, SH])
        dtm = sb("dtm", [P, NB, 1])
        ang = sb("ang", [P, NB, NA])
        turns = sb("turns", [P, 2, NB * NA])
        rem = sb("rem", [P, 2, NB * NA])
        trig = sb("trig", [P, 2, NB, NA])
        r0 = sb("r0", [P, NB, NA])
        r1 = sb("r1", [P, NB, NA])
        r2 = sb("r2", [P, NB, NA])
        r3 = sb("r3", [P, NB, NA])
        sh_in = sb("sh_in", [P, 2, NB * SH])
        cb = sb("cb", [P, NB, NS])
        cbd = sb("cbd", [P, NB, 1])
        fold = FoldLowRank(pg, ctx)
        block = ctx.enter_context(nc.Block())

        @block.sync
        def _(sp):
            pg.wait_loads(sp, "w_in")
            load_later_weights(pg, sp)

        @block.gpsimd
        def _(pool):
            nc.gpsimd.memset(half2[:, :], -0.5).then_inc(masks0, 1)
            for m in (upper, strict, after):
                nc.gpsimd.memset(m[:, :], 1.0).then_inc(masks0, 1)
            nc.gpsimd.memset(shift[:, :], 0.0).then_inc(masks0, 1)
            pool.wait_ge(var_ready, 1)
            nc.gpsimd.tensor_tensor(rs[:, :], ve[:, :], pg.neg_half[:, :], ALU.pow).then_inc(rstd_ready, 1)
            pool.wait_ge(masks0, 5)
            for m, base, mul, step, op, fill in ((upper, 0, -1, 1, ALU.is_ge, 0.0), (strict, 0, -1, 1, ALU.is_gt, 0.0),
                                                 (after, -1, 1, -1, ALU.is_gt, 0.0), (shift, -1, 1, -1, ALU.not_equal, 1.0)):
                nc.gpsimd.affine_select(out=m[:, :], in_=m[:, :], compare_op=op, fill=fill, base=base,
                                        pattern=[[step, P]], channel_multiplier=mul).then_inc(masks_done, 1)
            fold.gpsimd_zeros(pool)
            for c in range(NCH // 2):
                alibi_chunk(pg, c, alibi_done)
            pool.wait_ge(bc_var_ready, 1)
            nc.gpsimd.tensor_tensor(brs[:, :], bve[:, :], half2[:, :], ALU.pow).then_inc(bc_rstd_ready, 1)
            fold.gpsimd_sums(pool)

        @block.tensor
        def _(pe):
            for b in range(NB):
                pe.wait_ge(xn_ready, b + 1)
                nc.tensor.transpose(pg.bank[b // 4][:, (b % 4) * P:(b % 4 + 1) * P], xn[:, b, :],
                                    pg.ident[:, :]).then_inc(xt_ready, 1)
            pg.wait_loads(pe, "w_in")
            for b in range(NB):
                pe.wait_ge(xt_copied, b // 4 + 1)
                if b >= 2:
                    pe.wait_ge(zx_copied, b - 1)
                nc.tensor.matmul(pg.bank[2 + b % 2][:, :], xt[:, b, :], w_in[:, 0:2 * DI],
                                 start=True, stop=True).then_inc(zx_ready, 1)
                if b >= 2:
                    pe.wait_ge(small_copied, b - 1)
                nc.tensor.matmul(pg.bank[4 + b % 2][:, 0:NBC], xt[:, b, :], w_in[:, 2 * DI:],
                                 start=True, stop=True).then_inc(small_ready, 1)
            fold.tensor_transposes(pe, zx_copied)
            pe.wait_ge(masks_done, 4)
            pe.wait_ge(phase_in, 1)
            nc.tensor.matmul(pg.bank[6][:, 0:NB * NA], upper[:, :], ang[:, :, :].rearrange("p b n -> p (b n)"),
                             start=True, stop=True).then_inc(phase_ready, 1)
            pe.wait_ge(shift_in, 2)
            nc.tensor.matmul(pg.bank[7][:, 0:2 * NB * SH], shift[:, :], sh_in[:, :, :].rearrange("p k n -> p (k n)"),
                             start=True, stop=True).then_inc(shifted, 1)
            fold.tensor_products(pe, small_copied)

        @block.scalar
        def _(act):
            for h in range(2):
                act.wait_ge(xt_ready, 4 * h + 4)
                nc.scalar.copy(xt[:, 4 * h:4 * h + 4, :].rearrange("p b l -> p (b l)"),
                               pg.bank[h][:, :]).then_inc(xt_copied, 1)
            for b in range(NB):
                act.wait_ge(zx_ready, b + 1)
                nc.scalar.copy(zx[:, b, :], pg.bank[2 + b % 2][:, :]).then_inc(zx_copied, 1)
            act.wait_ge(sp_in, 1)
            nc.scalar.activation(eu[:, :, :, :], au[:, :, :, :], ACT.Exp, scale=-1.0).then_inc(sp_exp, 1)
            act.wait_ge(sp_exp, 1)
            nc.scalar.activation(lu[:, :, :, :], eu[:, :, :, :], ACT.Ln, bias=1.0).then_inc(sp_ln, 1)
            act.wait_ge(adt_ready, 1)
            nc.scalar.activation(sh_in[:, 0, :], logd[:, :, :].rearrange("p b h -> p (b h)"), ACT.Exp).then_inc(shift_in, 1)
            act.wait_ge(sg_done, 1)
            nc.scalar.activation(te[:, :, :], tr[:, :, :], ACT.Sigmoid).then_inc(dec_done, 1)
            fold.scalar_transposes(act)
            act.wait_ge(trig_in, 1)
            nc.scalar.activation(trig[:, :, :, :].rearrange("p k b n -> p (k b n)"),
                                 rem[:, :, :].rearrange("p k n -> p (k n)"), ACT.Sin).then_inc(trig_done, 1)
            act.wait_ge(zx_copied, NB)
            nc.scalar.activation(sz[:, :, :], zx[:, :, 0:DI], ACT.Silu).then_inc(silu_done, 1)
            fold.scalar_products(act)

        @block.vector
        def _(dve):
            o = Order(dve, order_sem)
            V = nc.vector
            norm_all(pg, dve, o, st, mv, ve, var_ready, rstd_ready, rs, xn, xn_ready)
            for b in range(NB):
                dve.wait_ge(small_ready, b + 1)
                V.tensor_copy(sm[:, b, :], pg.bank[4 + b % 2][:, 0:NBC]).then_inc(small_copied, 1)
            dve.wait_ge(small_copied, NB)
            pg.wait_loads(dve, "ssm_par")
            V.tensor_tensor(u[:, :, 0, :], sm[:, :, 2 * NS:2 * NS + SH],
                            bc(dtb[:, :].unsqueeze(1), [P, NB, SH]), ALU.add).then_inc(order_sem, 1)
            o.n += 1
            o.after(V.tensor_copy(u[:, :, 1, :], sm[:, :, 2 * NS + SH:2 * NS + 2 * SH]))
            V.scalar_tensor_tensor(au[:, :, :, :].rearrange("p b k h -> p (b k h)"), u[:, :, :, :].rearrange("p b k h -> p (b k h)"),
                                   -1.0, u[:, :, :, :].rearrange("p b k h -> p (b k h)"), ALU.mult, ALU.max).then_inc(sp_in, 1)
            V.tensor_copy(tr[:, :, :], sm[:, :, 2 * NS + 2 * SH:AN]).then_inc(sg_done, 1)
            for b in range(NB):
                for k in range(2):
                    o.mark(V.bn_stats(bst[:, b, k, :], sm[:, b, k * NS:(k + 1) * NS]))
            o.wait()
            for b in range(NB):
                for k in range(2):
                    o.mark(V.bn_aggr(bmv[:, b, k, :], bst[:, b, k, :]))
            o.wait()
            V.tensor_scalar(bve[:, :], bmv[:, :, :, 1].rearrange("p b k -> p (b k)"), EPS, None,
                            ALU.add).then_inc(bc_var_ready, 1)
            dve.wait_ge(sp_ln, 1)
            o.after(V.scalar_tensor_tensor(pu[:, :, :, :].rearrange("p b k h -> p (b k h)"), u[:, :, :, :].rearrange("p b k h -> p (b k h)"),
                                           0.0, lu[:, :, :, :].rearrange("p b k h -> p (b k h)"), ALU.max, ALU.add))
            dt = pu[:, :, 0, :]
            o.mark(V.tensor_scalar(au[:, :, 1, :], pu[:, :, 1, :], -1.0, -1e-4, ALU.mult, ALU.min))
            o.after(V.tensor_reduce(dtm[:, :, 0], dt, AX, ALU.add))
            V.tensor_tensor(logd[:, :, :], au[:, :, 1, :], dt, ALU.mult).then_inc(adt_ready, 1)
            o.after(V.tensor_scalar(dtm[:, :, :], dtm[:, :, :], 1.0 / SH, None, ALU.mult))
            V.tensor_tensor(ang[:, :, :], sm[:, :, AN:], bc(dtm[:, :, :], [P, NB, NA]), ALU.mult).then_inc(phase_in, 1)
            dve.wait_ge(dec_done, 1)
            o.after(V.tensor_tensor(now[:, :, :], te[:, :, :], dt, ALU.mult))
            V.tensor_tensor(sh_in[:, 1, :].rearrange("p (b h) -> p b h", b=NB), dt, now[:, :, :],
                            ALU.subtract).then_inc(shift_in, 1)
            MAGIC, TP = 1.5 * 2.0 ** 23, 2 * np.pi
            HI = 6.28125
            ph = pg.bank[6][:, 0:NB * NA]
            dve.wait_ge(phase_ready, 1)
            for k in range(2):
                o.mark(V.tensor_scalar(turns[:, k, :], ph, 1 / TP, 0.25 * k, ALU.mult, ALU.add))
            o.wait()
            o.after(V.tensor_scalar(turns[:, :, :], turns[:, :, :], MAGIC, None, ALU.add))
            o.after(V.tensor_scalar(turns[:, :, :], turns[:, :, :], -MAGIC, None, ALU.add))
            for k in range(2):
                o.mark(V.scalar_tensor_tensor(rem[:, k, :], turns[:, k, :], -HI, ph, ALU.mult, ALU.add))
            o.wait()
            o.after(V.scalar_tensor_tensor(rem[:, :, :].rearrange("p k n -> p (k n)"), turns[:, :, :].rearrange("p k n -> p (k n)"),
                                           -(TP - HI), rem[:, :, :].rearrange("p k n -> p (k n)"), ALU.mult, ALU.add))
            o.after(V.tensor_scalar(rem[:, 1, :], rem[:, 1, :], TP / 4, None, ALU.add))
            PI = float(np.nextafter(np.float32(np.pi), np.float32(0)))
            V.tensor_scalar(rem[:, :, :], rem[:, :, :], PI, -PI, ALU.min, ALU.max).then_inc(trig_in, 1)
            dve.wait_ge(bc_rstd_ready, 1)
            o.after(V.tensor_tensor(bn[:, :, :, :], sm[:, :, 0:2 * NS].rearrange("p b (k n) -> p b k n", k=2),
                                    bc(bmv[:, :, :, 0:1], [P, NB, 2, NS]), ALU.subtract))
            o.after(V.tensor_tensor(bn[:, :, :, :], bn[:, :, :, :],
                                    bc(brs[:, :].rearrange("p (b k) -> p b k", b=NB).unsqueeze(3), [P, NB, 2, NS]), ALU.mult))
            for k, op in ((0, ALU.mult), (1, ALU.add)):
                o.after(V.tensor_tensor(bn[:, :, :, :], bn[:, :, :, :],
                                        bc(gb[:, k:k + 1, :, :], [P, NB, 2, NS]), op))
            dve.wait_ge(trig_done, 1)
            sin, cos = trig[:, 0, :, :], trig[:, 1, :, :]
            for k in range(2):
                ev = bn[:, :, k, 0:NS:2]
                od = bn[:, :, k, 1:NS:2]
                o.mark(V.tensor_tensor(r0[:, :, :], ev, cos, ALU.mult))
                o.mark(V.tensor_tensor(r1[:, :, :], od, sin, ALU.mult))
                o.mark(V.tensor_tensor(r2[:, :, :], ev, sin, ALU.mult))
                o.after(V.tensor_tensor(r3[:, :, :], od, cos, ALU.mult))
                o.mark(V.tensor_tensor(br[:, :, k, 0:NS:2], r0[:, :, :], r1[:, :, :], ALU.subtract))
                o.after(V.tensor_tensor(br[:, :, k, 1:NS:2], r2[:, :, :], r3[:, :, :], ALU.add))
            o.after(V.tensor_tensor(cb[:, :, :], br[:, :, 0, :], br[:, :, 1, :], ALU.mult))
            o.after(V.tensor_reduce(cbd[:, :, 0], cb[:, :, :], AX, ALU.add))
            dve.wait_ge(shifted, 1)
            nd = pg.bank[7][:, 0:2 * NB * SH].rearrange("p (k b h) -> p k b h", k=2, b=NB)
            o.after(V.tensor_tensor(past[:, :, :], nd[:, 0], now[:, :, :], ALU.mult))
            o.mark(V.tensor_tensor(past[:, :, :], nd[:, 1], past[:, :, :], ALU.add))
            o.after(V.tensor_tensor(now[:, :, :], now[:, :, :], bc(cbd[:, :, :], [P, NB, SH]), ALU.mult))
            o.after(V.tensor_tensor(now[:, :, :], now[:, :, :], bc(dpar[:, :].unsqueeze(1), [P, NB, SH]), ALU.add))


def state_space_mix(pg, zx, sz, br, logd, past, now, upper, strict, after):
    nc = pg.nc
    w_out = pg.ssm["w_out"]
    with ExitStack() as ctx:
        (bc_in, rl_in, bct_ready, bct_copied, cb_ready, lg_ready, cbm_done, e_done, g_done, xs_done, own_done, y_ready,
         summed, y_done, yt_ready, yt_copied, o_ready, x_done, alibi_done) = pg.sems("sm", (
            "bc_in rl_in bct_ready bct_copied cb_ready decay_sum_ready cb_masked decay_done mix_ready xs_done own_done y_ready "
            "summed y_done yt_ready yt_copied out_ready x_done alibi_done"))
        two = lambda n, s: [pg.sbuf(f"sm_{n}{p}", s, ctx=ctx) for p in range(2)]
        bcs, bct = two("bcs", [P, 3 * NS]), two("bct", [NS, 2, P])
        rl, e, g = two("rl", [P, SH, P]), two("e", [P, SH, P]), two("g", [P, SH, P])
        cbm, xs = two("cbm", [P, P]), two("xs", [P, SH, NS])
        t1, y, yt = two("t1", [P, SH, NS]), two("y", [P, DI]), two("yt", [P, 2, P])
        bc_ps, lg_ps, y_ps, out_ps = pg.bank[0:2], pg.bank[2:4], pg.bank[4:6], pg.bank[6:8]
        block = ctx.enter_context(nc.Block())

        def turns(eng, turn):
            with eng.Fori(0, NB // 2 - 1) as i:
                for p in range(2):
                    turn(2 * i + p, p, True, True)
            for p in range(2):
                turn(NB - 2 + p, p, False, p == 0)

        @block.gpsimd
        def _(pool):
            def copy_bc(n, p):
                nc.gpsimd.tensor_copy(bcs[p][:, 0:2 * NS], br[:, n].rearrange("p k n -> p (k n)")).then_inc(bc_in, 1)
                nc.gpsimd.tensor_copy(bcs[p][:, 2 * NS:], br[:, n, 0, :]).then_inc(bc_in, 1)

            for p in range(2):
                copy_bc(p, p)
            with pool.Fori(1, NB // 2) as i:
                for p in range(2):
                    pool.wait_ge(bct_ready, 4 * i + 2 * p - 2)
                    copy_bc(2 * i + p, p)
            for c in range(NCH // 2, NCH):
                alibi_chunk(pg, c, alibi_done)

        @block.tensor
        def _(pe):
            def transpose_bc(n, p):
                pe.wait_ge(bc_in, 2 * n + 2)
                for k in range(2):
                    nc.tensor.transpose(bc_ps[p][:, k * P:(k + 1) * P], bcs[p][:, k * NS:k * NS + P],
                                        pg.ident[:, :]).then_inc(bct_ready, 1)

            def sum_decays(n, p):
                pe.wait_ge(rl_in, n + 1)
                nc.tensor.matmul(lg_ps[p][:, :], after[:, :], rl[p][:, :, :].rearrange("p h l -> p (h l)"),
                                 start=True, stop=True).then_inc(lg_ready, 1)

            def multiply_bc(n, p):
                pe.wait_ge(bct_copied, n + 1)
                nc.tensor.matmul(bc_ps[p][:, 256:384], bct[p][:, 0, :], bct[p][:, 1, :],
                                 start=True, stop=True).then_inc(cb_ready, 1)

            for n in range(2):
                transpose_bc(n, n)
                sum_decays(n, n)
                multiply_bc(n, n)
            pg.wait_loads(pe, "w_out")

            def turn(j, p, ahead, nxt):
                pe.wait_ge(g_done, j + 1)
                pe.wait_ge(xs_done, j + 1)
                for h in range(SH):
                    mm = nc.tensor.matmul(y_ps[p][:, h * NS:(h + 1) * NS], g[p][:, h, :], xs[p][:, h, :],
                                          start=True, stop=True)
                mm.then_inc(y_ready, 1)
                if ahead:
                    transpose_bc(j + 2, p)
                    sum_decays(j + 2, p)
                pe.wait_ge(y_done, j + 1)
                for t in range(2):
                    mm = nc.tensor.transpose(y_ps[p][:, DI + t * P:DI + (t + 1) * P], y[p][:, t * P:(t + 1) * P],
                                             pg.ident[:, :])
                mm.then_inc(yt_ready, 1)
                if ahead:
                    multiply_bc(j + 2, p)
                pe.wait_ge(x_done, j + 1)
                pe.wait_ge(yt_copied, j + 1)
                for t in range(2):
                    mm = nc.tensor.matmul(out_ps[p][:, 0:D], yt[p][:, t, :], w_out[:, t, :],
                                          start=(t == 0), stop=(t == 1))
                mm.then_inc(o_ready, 1)

            turns(pe, turn)

        @block.scalar
        def _(act):
            def copy_bct(n, p):
                act.wait_ge(bct_ready, 2 * n + 2)
                nc.scalar.copy(bct[p][:, :, :].rearrange("n k l -> n (k l)"), bc_ps[p][0:NS, 0:2 * P]).then_inc(bct_copied, 1)

            def exp(n, p):
                act.wait_ge(lg_ready, n + 1)
                nc.scalar.activation(e[p][:, :, :].rearrange("p h l -> p (h l)"), lg_ps[p][:, :], ACT.Exp).then_inc(e_done, 1)

            for n in range(2):
                copy_bct(n, n)
                exp(n, n)

            def turn(j, p, ahead, nxt):
                if ahead:
                    copy_bct(j + 2, p)
                act.wait_ge(yt_ready, j + 1)
                nc.scalar.copy(yt[p][:, :, :].rearrange("p t l -> p (t l)"), y_ps[p][:, DI:2 * DI]).then_inc(yt_copied, 1)
                if ahead:
                    exp(j + 2, p)

            turns(act, turn)

        @block.vector
        def _(dve):
            V = nc.vector

            def triangle_decays(n, p):
                V.tensor_tensor(rl[p][:, :, :], bc(upper[:, :].unsqueeze(1), [P, SH, P]),
                                bc(logd[:, n].unsqueeze(2), [P, SH, P]), ALU.mult).then_inc(rl_in, 1)

            def weigh_x(n, p):
                xn = zx[:, n, DI:2 * DI].rearrange("p (h n) -> p h n", h=SH)
                V.tensor_tensor(xs[p][:, :, :], xn, bc(past[:, n].unsqueeze(2), [P, SH, NS]), ALU.mult).then_inc(xs_done, 1)
                V.tensor_tensor(t1[p][:, :, :], xn, bc(now[:, n].unsqueeze(2), [P, SH, NS]), ALU.mult).then_inc(own_done, 1)

            def mask_bc(n, p):
                dve.wait_ge(cb_ready, n + 1)
                V.tensor_tensor(cbm[p][:, :], bc_ps[p][:, 256:384], strict[:, :], ALU.mult).then_inc(cbm_done, 1)

            def mix(n, p):
                dve.wait_ge(e_done, n + 1)
                dve.wait_ge(cbm_done, n + 1)
                V.tensor_tensor(g[p][:, :, :], e[p][:, :, :], bc(cbm[p][:, :].unsqueeze(1), [P, SH, P]), ALU.mult).then_inc(g_done, 1)

            V.memset(pg.first[:, :], 0.0).then_inc(x_done, 1)
            for n in range(2):
                triangle_decays(n, n)
            for n in range(2):
                weigh_x(n, n)
                mask_bc(n, n)
            mix(0, 0)

            def turn(j, p, ahead, nxt):
                if ahead:
                    triangle_decays(j + 2, p)
                t = t1[p][:, :, :].rearrange("p h n -> p (h n)")
                dve.wait_ge(y_ready, j + 1)
                dve.wait_ge(own_done, j + 1)
                V.tensor_tensor(t, y_ps[p][:, 0:DI], t, ALU.add).then_inc(summed, 1)
                dve.wait_ge(summed, j + 1)
                V.tensor_tensor(y[p][:, :], t, sz[:, j, :], ALU.mult).then_inc(y_done, 1)
                if nxt:
                    mix(j + 1, 1 - p)
                if ahead:
                    dve.wait_ge(y_done, j + 1)
                    weigh_x(j + 2, p)
                    mask_bc(j + 2, p)
                dve.wait_ge(o_ready, j + 1)
                V.tensor_tensor(pg.x[:, j, :], out_ps[p][:, 0:D], pg.x[:, j, :], ALU.add).then_inc(x_done, 1)

            turns(dve, turn)


def cross_weights(pg, layer):
    w = {n: pg.sbuf(f"c{layer}_{n}", [P if n in "qo" else DC, INNER]) for n in "qkvo"}
    w["o"] = w["o"][:, :].rearrange("p (t d) -> p t d", t=NT)
    w["bias"] = pg.sbuf(f"c{layer}_bias", [P, D])
    if layer:
        w["vw"] = pg.sbuf("c1_vw", [NH * IPA, NB, D])
        w["qk_image"] = pg.sbuf("c1_qk_image", [P, NB, NH * IPA])
        w["down"] = {n: pg.sbuf(f"c1_down_{n}", [P if n == "q" else DC, RANK]) for n in "qkv"}
        w["down_o"] = pg.sbuf("c1_down_o", [P, NT, RANK])
        w["up"] = {n: pg.sbuf(f"c1_up_{n}", [RANK, D if n == "o" else INNER]) for n in "qkvo"}
        w["alpha"] = pg.sbuf("c1_alpha", [P, 4])
        w["img2"] = [pg.sbuf(f"c1_{n}2", [P, NT, 2, NB * IPA]) for n in "vk"]
        w["wq_t"] = pg.sbuf("c1_wq_t", [P, NT, P])
        w["ipa"] = [pg.sbuf(f"c1_w{n}_ipa", [DC, INNER]) for n in "vk"]
    return w


def load_cross_weights(pg, sp, layer):
    a, w, group = pg.a, pg.cross_w[layer], f"cross{layer}"
    if layer == 0:
        kv = a["L0_xattn_w_kv"]
        parts = [(w["q"][:, :], a["L0_xattn_w_q"]), (w["k"][:, :], kv[:, 0:INNER]), (w["v"][:, :], kv[:, INNER:])]
        wo, bias = a["L0_xattn_w_out"], a["L0_xattn_b_out"]
    else:
        parts = [(w[c][:, :], a["L1_xattn_W" + c]) for c in "qkv"]
        wo, bias = a["L1_xattn_Wo"], a["L1_xattn_bo"]
    parts += [(w["o"], wo.rearrange("(t p) d -> p t d", p=P)), (w["bias"][:, :], bias.partition_broadcast(P))]
    if layer:
        parts += [(w["down"][c][:, :], a[f"L1_xattn_{c}_down"]) for c in "qkv"]
        parts += [(w["down_o"][:, :, :], a["L1_xattn_o_down"].rearrange("(t p) r -> p t r", p=P))]
        for m, c in enumerate("qkvo"):
            parts += [(w["up"][c][:, :], a[f"L1_xattn_{c}_up"]),
                      (w["alpha"][:, m:m + 1], a[f"L1_xattn_{c}_alpha"].partition_broadcast(P))]
        parts += [(w["ipa"][k][:, :], a[f"L1_xattn_W{c}_ipa"]) for k, c in enumerate("vk")]
    for dst, src in parts:
        pg.load(sp, group, dst, src)


def cross_attention(pg, layer):
    nc = pg.nc
    KS = P - IPA if layer else P
    w = pg.cross_w[layer]
    with ExitStack() as ctx:
        (var_ready, rstd_ready, xn_ready, xt_ready, xt_copied, c_ready, q_ready, q_copied, qb_ready, k_ready, k_copied,
         kb_ready, v_ready, v_copied, s_ready, s_read, nm_ready, nmt_ready, nmt_copied, st_ready, exp_done, av_ready,
         o_done, ot_ready, ot_copied, out_ready, x_done, ones_done, order_sem, norm_order, wv_high_ready, wv_low_ready,
         c_high_ready, c_low_ready) = pg.sems(f"ca{layer}", (
            "var_ready rstd_ready xn_ready xt_ready xt_copied c_ready q_ready q_copied q_bf_ready k_ready k_copied "
            "k_bf_ready v_ready v_copied s_ready s_read max_ready max_transposed max_copied st_ready exp_done av_ready "
            "o_done ot_ready ot_copied out_ready x_done ones_done order norm_order wv_high wv_low c_high "
            "c_low"))
        if layer:
            (img_ready, img_order, img_shifted, img_exp, p2_ready, p2t_ready, p2t_copied) = pg.sems("ca1_image", (
                "scores_ready order shifted exp_done p_ready p_transposed p_copied"))
        sb = lambda n, s, dt=F32: pg.sbuf(f"ca{layer}_{n}", s, dt, ctx=ctx)
        two = lambda n, s, dt=F32: [sb(f"{n}{p}", s, dt) for p in range(2)]
        st, mv, ve, rs, xn = sb("st", [P, 6]), sb("mv", [P, 2]), sb("ve", [P, 1]), sb("rs", [P, 1]), sb("xn", [P, D])
        xt, ct = sb("xt", [P, P]), sb("ct", [DC, P])
        ct_high, ct_low = (sb(f"ct_{n}", [DC, P], F32R) for n in ("high", "low"))
        wv_high, wv_low = (sb(f"wv_{n}", [DC, INNER], F32R) for n in ("high", "low"))
        qt, kt = two("qt", [P, NT, P]), two("kt", [P, NT, P])
        qb, kb = two("qb", [P, NT, P], BF16), two("kb", [P, NT, P], BF16)
        v = two("v", [P, NH, VS])
        m, nm = sb("m", [P, NH]), sb("nm", [P, P // NH, NH], BF16)
        nmt = two("nmt", [P, P], BF16)
        pt = sb("pt", [P, NCH, HPC * P])
        rinv, on = sb("rinv", [P, NH]), sb("on", [P, NH, HD])
        ot = sb("ot", [P, NT, P])
        if layer:
            s2, m2, sum2, p2t = sb("s2", [P, NH, IPA]), sb("m2", [P, NH]), sb("sum2", [P, NH]), sb("p2t", [NH * IPA, P])
        proj = pg.bank[0:2]
        score_t = pg.bank[2:4]
        score, misc = (pg.bank[4], pg.bank[2]), pg.bank[5]
        av = pg.bank[6:8]
        nmt_ps = score[0][:, 0:64].bitcast(BF16)[:, 0:P]
        p2t_ps = misc[0:NH * IPA, P:2 * P]
        img_ps = misc[:, 320:320 + NH * IPA]
        SCALE = HD ** -0.5
        block = ctx.enter_context(nc.Block())

        def qrow(t, h):
            return t[64 * (h % 2):64 * (h % 2) + 64, h // 2, :]

        def turns(eng, turn):
            with eng.Fori(0, NB // 2 - 1) as i:
                for p in range(2):
                    turn(2 * i + p, p, True, True)
            turn(NB - 2, 0, True, False)
            turn(NB - 1, 1, False, False)

        @block.gpsimd
        def _(pool):
            for p in range(2):
                nc.gpsimd.memset(v[p][:, :, HD:VS], 1.0).then_inc(ones_done, 1)
            nc.gpsimd.memset(nm[:, 2:, :], 0.0).then_inc(ones_done, 1)

            def rstd(n):
                pool.wait_ge(var_ready, n + 1)
                nc.gpsimd.tensor_tensor(rs[:, :], ve[:, :], pg.neg_half[:, 0:1], ALU.pow).then_inc(rstd_ready, 1)

            def cast_q(n, p, h):
                pool.wait_ge(q_copied, 2 * n + h + 1)
                half = qt[p][:, 4 * h:4 * h + 4, :]
                nc.gpsimd.tensor_tensor(qb[p][:, 4 * h:4 * h + 4, :], half, bc(pg.zero[:, :].unsqueeze(2), [P, 4, P]),
                                        ALU.add).then_inc(qb_ready, 1)

            def copy_ctx(n):
                nc.gpsimd.tensor_copy(ct[:, :], pg.ctx_t[:, n, :]).then_inc(c_ready, 1)

            def split_ctx(n):
                pool.wait_ge(c_ready, n + 1)
                nc.gpsimd.tensor_tensor(ct_high[:, :], ct[:, :], bc(pg.zero[0:DC, :], [DC, P]),
                                        ALU.add).then_inc(c_high_ready, 1)
                pool.wait_ge(c_high_ready, n)
                nc.gpsimd.tensor_tensor(ct_low[:, :], ct[:, :], ct_high[:, :], ALU.subtract).then_inc(c_low_ready, 1)

            copy_ctx(0)
            rstd(0)
            pg.wait_loads(pool, f"cross{layer}")
            nc.gpsimd.tensor_copy(wv_high[:, :], w["v"][:, :]).then_inc(wv_high_ready, 1)
            pool.wait_ge(wv_high_ready, 1)
            nc.gpsimd.tensor_tensor(wv_low[:, :], w["v"][:, :], wv_high[:, :], ALU.subtract).then_inc(wv_low_ready, 1)
            rstd(1)
            pool.wait_ge(v_ready, 2)
            copy_ctx(1)
            split_ctx(1)

            def turn(j, p, nxt, nxt2):
                if nxt:
                    for h in range(2):
                        cast_q(j + 1, 1 - p, h)
                if nxt2:
                    rstd(j + 2)
                    pool.wait_ge(v_ready, 2 * j + 4)
                    copy_ctx(j + 2)
                    split_ctx(j + 2)

            turns(pool, turn)

        @block.tensor
        def _(pe):
            def x_transpose(n):
                pe.wait_ge(xn_ready, n + 1)
                nc.tensor.transpose(misc[:, 0:P], xn[:, :], pg.ident[:, :]).then_inc(xt_ready, 1)

            def project_q(n, h):
                if h == 0:
                    pe.wait_ge(xt_copied, n + 1)
                for t in range(4):
                    mm = nc.tensor.matmul(proj[h][:, t * P:(t + 1) * P],
                                          w["q"][:, (4 * h + t) * P:(4 * h + t + 1) * P], xt[:, :], start=True, stop=True)
                mm.then_inc(q_ready, 1)

            def project_k(n, h):
                if h == 0:
                    pe.wait_ge(c_ready, n + 1)
                for t in range(4):
                    mm = nc.tensor.matmul(proj[h][:, t * P:(t + 1) * P], w["k"][:, (4 * h + t) * P:(4 * h + t + 1) * P],
                                          ct[:, :], start=True, stop=True)
                mm.then_inc(k_ready, 1)

            def project_first_v(h):
                pe.wait_ge(k_copied, h + 1)
                nc.tensor.matmul(proj[h][0:KS, :], ct[:, 0:KS], w["v"][:, 512 * h:512 * (h + 1)],
                                 start=True, stop=True).then_inc(v_ready, 1)

            def project_v(n, h):
                pe.wait_ge(k_copied, 2 * n + h + 1)
                if h == 0:
                    pe.wait_ge(c_low_ready, n)
                for i, (cp, wp) in enumerate(((ct_low, wv_high), (ct_high, wv_low), (ct_high, wv_high))):
                    mm = nc.tensor.matmul(proj[h][0:KS, :], cp[:, 0:KS], wp[:, 512 * h:512 * (h + 1)],
                                          start=(i == 0), stop=(i == 2))
                mm.then_inc(v_ready, 1)

            def image_scores(n):
                nc.tensor.matmul(img_ps, xt[:, :], w["qk_image"][:, n, :], start=True, stop=True).then_inc(img_ready, 1)

            def scores(n, p, c):
                if c % 2 == 0:
                    pe.wait_ge(qb_ready, 2 * n + c // 2 + 1)
                    pe.wait_ge(kb_ready, 2 * n + c // 2 + 1)
                if c >= 2:
                    pe.wait_ge(s_read, NCH * n + c - 1)
                for r in range(HPC):
                    h = head(c, r)
                    mm = nc.tensor.matmul(score[c % 2][:, r * P:r * P + KS], qrow(qb[p], h), qrow(kb[p], h)[:, 0:KS],
                                          start=True, stop=True)
                mm.then_inc(s_ready, 1)

            def max_transpose(n):
                pe.wait_ge(nm_ready, 2 * n + 2)
                nc.tensor.transpose(nmt_ps, nm[:, :, :].rearrange("p k h -> p (k h)"), pg.ident_bf[:, :]).then_inc(nmt_ready, 1)

            def scores_t(j, p, c):
                if c == 0:
                    pe.wait_ge(nmt_copied, j + 1)
                dst = [score_t[c % 2][0:KS, r * P:(r + 1) * P] for r in range(HPC)]
                for r in range(HPC):
                    nc.tensor.matmul(dst[r], qrow(kt[p], head(c, r))[:, 0:KS], qrow(qt[p], head(c, r)),
                                     start=(r == 0), stop=False)
                for r in range(HPC):
                    mm = nc.tensor.matmul(dst[r], pg.sel[:, head(c, r), 0:KS], nmt[p][:, :], start=False,
                                          stop=(r == HPC - 1))
                mm.then_inc(st_ready, 1)

            def values(j, p, c):
                if c >= 2:
                    pe.wait_ge(o_done, NCH * j + c - 1)
                pe.wait_ge(exp_done, NCH * j + c + 1)
                for r in range(HPC):
                    mm = nc.tensor.matmul(av[c % 2][:, r * VS:(r + 1) * VS], pt[0:KS, c, r * P:(r + 1) * P],
                                          v[p][0:KS, head(c, r), :], start=True, stop=True)
                mm.then_inc(av_ready, 1)

            def out_transpose(j, h, nxt):
                if nxt:
                    pe.wait_ge(v_copied, 2 * j + 2 + h + 1)
                pe.wait_ge(o_done, NCH * j + 2 * h + 2)
                for t in range(4):
                    mm = nc.tensor.transpose(proj[h][:, t * P:(t + 1) * P],
                                             on[:, 8 * h + 2 * t:8 * h + 2 * t + 2, :].rearrange("p h d -> p (h d)"),
                                             pg.ident[:, :])
                mm.then_inc(ot_ready, 1)

            def project_out(j, nxt):
                for t in range(NT):
                    if t % 4 == 0:
                        pe.wait_ge(ot_copied, 2 * j + t // 4 + 1)
                    if t == 4 and nxt:
                        max_transpose(j + 1)
                    mm = nc.tensor.matmul(misc[:, 0:D], ot[:, t, :], w["o"][:, t, :], start=(t == 0),
                                          stop=(t == NT - 1 and not layer))
                if layer:
                    mm = nc.tensor.matmul(misc[:, 0:D], p2t[:, :], w["vw"][:, j, :], start=False, stop=True)
                mm.then_inc(out_ready, 1)

            pg.wait_loads(pe, f"cross{layer}")
            for h in range(2):
                project_k(0, h)
            x_transpose(0)
            for h in range(2):
                project_first_v(h)
            for h in range(2):
                pe.wait_ge(v_copied, h + 1)
                project_q(0, h)
            if layer:
                image_scores(0)
            pe.wait_ge(ones_done, 3)
            for c in range(NCH):
                scores(0, 0, c)
            if layer:
                pe.wait_ge(img_shifted, 1)
            x_transpose(1)
            max_transpose(0)
            pe.wait_ge(wv_low_ready, 1)

            def turn(j, p, nxt, nxt2):
                n, q = j + 1, 1 - p
                scores_t(j, p, 0)
                if layer:
                    pe.wait_ge(x_done, j + 1)
                    pe.wait_ge(p2_ready, j + 1)
                if nxt:
                    project_q(n, 0)
                if layer:
                    nc.tensor.transpose(p2t_ps, s2[:, :, :].rearrange("p h k -> p (h k)"), pg.ident[:, :]).then_inc(p2t_ready, 1)
                scores_t(j, p, 1)
                if nxt:
                    project_q(n, 1)
                    if layer:
                        pe.wait_ge(p2t_copied, j + 1)
                        image_scores(n)
                values(j, p, 0)
                if nxt:
                    pe.wait_ge(q_copied, 2 * n + 1)
                    project_k(n, 0)
                scores_t(j, p, 2)
                if nxt:
                    pe.wait_ge(q_copied, 2 * n + 2)
                    project_k(n, 1)
                values(j, p, 1)
                scores_t(j, p, 3)
                if nxt:
                    scores(n, q, 0)
                    project_v(n, 0)
                values(j, p, 2)
                if nxt:
                    scores(n, q, 1)
                    project_v(n, 1)
                    scores(n, q, 2)
                values(j, p, 3)
                out_transpose(j, 0, nxt)
                if nxt:
                    scores(n, q, 3)
                if nxt2:
                    pe.wait_ge(x_done, j + 1)
                    if layer:
                        pe.wait_ge(img_shifted, n + 1)
                    x_transpose(j + 2)
                out_transpose(j, 1, nxt)
                if nxt2:
                    pe.wait_ge(xt_copied, j + 3)
                else:
                    pe.wait_ge(x_done, j + 1)
                    if layer:
                        pe.wait_ge(img_shifted, n + 1) if nxt else pe.wait_ge(p2t_copied, j + 1)
                project_out(j, nxt)

            turns(pe, turn)

        @block.scalar
        def _(act):
            def copy_q(n, p, h):
                act.wait_ge(q_ready, 2 * n + h + 1)
                nc.scalar.mul(qt[p][:, 4 * h:4 * h + 4, :].rearrange("p t l -> p (t l)"), proj[h][:, :],
                              SCALE).then_inc(q_copied, 1)

            def copy_xt(n):
                act.wait_ge(xt_ready, n + 1)
                nc.scalar.copy(xt[:, :], misc[:, 0:P]).then_inc(xt_copied, 1)

            def copy_v(n, p, h):
                act.wait_ge(v_ready, 2 * n + h + 1)
                nc.scalar.copy(v[p][0:KS, 8 * h:8 * h + 8, 0:HD], proj[h][0:KS, :].rearrange(
                    "p (h d) -> p h d", d=HD)).then_inc(v_copied, 1)

            def copy_ot(j, h):
                act.wait_ge(ot_ready, 2 * j + h + 1)
                nc.scalar.copy(ot[:, 4 * h:4 * h + 4, :].rearrange("p t l -> p (t l)"), proj[h][:, :]).then_inc(ot_copied, 1)

            def copy_max(n, p):
                act.wait_ge(nmt_ready, n + 1)
                nc.scalar.copy(nmt[p][:, :], nmt_ps).then_inc(nmt_copied, 1)

            def image_exp(n):
                act.wait_ge(img_shifted, n + 1)
                nc.scalar.activation(s2[:, :, :], s2[:, :, :], ACT.Exp).then_inc(img_exp, 1)

            def exp(j, c):
                act.wait_ge(st_ready, NCH * j + c + 1)
                nc.scalar.activation(pt[0:KS, c, :], score_t[c % 2][0:KS, :], ACT.Exp).then_inc(exp_done, 1)

            copy_xt(0)
            act.wait_ge(ones_done, 3)
            for h in range(2):
                copy_v(0, 0, h)
            for h in range(2):
                copy_q(0, 0, h)
            if layer:
                image_exp(0)
            copy_xt(1)
            copy_max(0, 0)

            def turn(j, p, nxt, nxt2):
                n, q = j + 1, 1 - p
                if layer:
                    act.wait_ge(p2t_ready, j + 1)
                    nc.scalar.copy(p2t[:, :], p2t_ps).then_inc(p2t_copied, 1)
                exp(j, 0)
                if nxt:
                    copy_q(n, q, 0)
                exp(j, 1)
                if nxt:
                    copy_q(n, q, 1)
                exp(j, 2)
                if layer and nxt:
                    image_exp(n)
                exp(j, 3)
                if nxt:
                    copy_v(n, q, 0)
                    copy_v(n, q, 1)
                copy_ot(j, 0)
                if nxt2:
                    copy_xt(j + 2)
                copy_ot(j, 1)
                if nxt:
                    copy_max(n, q)

            turns(act, turn)

        @block.vector
        def _(dve):
            V = nc.vector

            def norm_stats(n):
                V.bn_stats(st[:, :], pg.x[:, n, :]).then_inc(norm_order, 1)

            def wait_stats(n):
                dve.wait_ge(norm_order, 2 * n + 1)

            def norm_aggregate(n):
                V.bn_aggr(mv[:, :], st[:, :]).then_inc(norm_order, 1)
                dve.wait_ge(norm_order, 2 * n + 2)
                V.tensor_scalar(ve[:, :], mv[:, 1:2], EPS, None, ALU.add).then_inc(var_ready, 1)

            def norm_apply(n):
                dve.wait_ge(rstd_ready, n + 1)
                V.tensor_scalar(xn[:, :], pg.x[:, n, :], mv[:, 0:1], rs[:, 0:1], ALU.subtract,
                                ALU.mult).then_inc(xn_ready, 1)

            def copy_k(n, p, h):
                half = slice(4 * h, 4 * h + 4)
                dve.wait_ge(k_ready, 2 * n + h + 1)
                V.tensor_copy(kt[p][:, half, :].rearrange("p t k -> p (t k)"), proj[h][:, :]).then_inc(k_copied, 1)
                dve.wait_ge(k_copied, 2 * n + h + 1)
                V.tensor_copy(kb[p][:, half, :], kt[p][:, half, :]).then_inc(kb_ready, 1)

            def row_max(n, c):
                dve.wait_ge(s_ready, NCH * n + c + 1)
                s = score[c % 2][:, :].rearrange("p (h k) -> p h k", k=P)
                V.tensor_reduce(m[:, heads_of(c)], s[:, :, 0:KS], AX, ALU.max, negate=True).then_inc(s_read, 1)

            def split_max(n):
                dve.wait_ge(s_read, NCH * n + NCH)
                V.tensor_copy(nm[:, 0, :], m[:, :]).then_inc(nm_ready, 1)
                dve.wait_ge(nm_ready, 2 * n + 1)
                V.tensor_tensor(nm[:, 1, :], m[:, :], nm[:, 0, :], ALU.subtract).then_inc(nm_ready, 1)

            def image_shift(n):
                dve.wait_ge(img_ready, n + 1)
                s = img_ps.rearrange("p (h k) -> p h k", k=IPA)
                o = Order(dve, img_order, n, 3)
                o.after(V.tensor_reduce(m2[:, :], s, AX, ALU.max))
                V.tensor_tensor(s2[:, :, :], s, bc(m2[:, :].unsqueeze(2), [P, NH, IPA]), ALU.subtract).then_inc(img_shifted, 1)
                return o

            def image_softmax(n, o):
                dve.wait_ge(img_exp, n + 1)
                o.after(V.tensor_reduce(sum2[:, :], s2[:, :, :], AX, ALU.add))
                o.after(V.reciprocal(sum2[:, :], sum2[:, :]))
                V.tensor_tensor(s2[:, :, :], s2[:, :, :], bc(sum2[:, :].unsqueeze(2), [P, NH, IPA]),
                                ALU.mult).then_inc(p2_ready, 1)
                o.close()

            def normalise(j, c, o):
                dve.wait_ge(av_ready, NCH * j + c + 1)
                heads = heads_of(c)
                src = av[c % 2][:, 0:HPC * VS].rearrange("p (h e) -> p h e", e=VS)
                o.after(V.reciprocal(rinv[:, heads].unsqueeze(2), src[:, :, HD:HD + 1]))
                V.tensor_tensor(on[:, heads, :], src[:, :, 0:HD], bc(rinv[:, heads].unsqueeze(2), [P, HPC, HD]),
                                ALU.mult).then_inc(o_done, 1)

            nc.vector.memset(pg.first[:, :], 0.0).then_inc(x_done, 1)
            norm_stats(0)
            wait_stats(0)
            norm_aggregate(0)
            copy_k(0, 0, 0)
            norm_apply(0)
            copy_k(0, 0, 1)
            norm_stats(1)
            wait_stats(1)
            norm_aggregate(1)
            dve.wait_ge(xt_ready, 1)
            norm_apply(1)
            for h in range(2):
                dve.wait_ge(q_copied, h + 1)
                V.tensor_copy(qb[0][:, 4 * h:4 * h + 4, :], qt[0][:, 4 * h:4 * h + 4, :]).then_inc(qb_ready, 1)
            if layer:
                image = image_shift(0)
            for c in range(NCH):
                row_max(0, c)
            split_max(0)
            if layer:
                image_softmax(0, image)

            def turn(j, p, nxt, nxt2):
                n, q = j + 1, 1 - p
                o = Order(dve, order_sem, j, NCH + 1)
                if nxt2:
                    norm_stats(j + 2)
                if layer and nxt:
                    image = image_shift(n)
                if nxt2:
                    wait_stats(j + 2)
                normalise(j, 0, o)
                if nxt2:
                    norm_aggregate(j + 2)
                if nxt:
                    copy_k(n, q, 0)
                    copy_k(n, q, 1)
                if nxt2:
                    norm_apply(j + 2)
                if layer and nxt:
                    image_softmax(n, image)
                normalise(j, 1, o)
                if nxt:
                    row_max(n, 0)
                normalise(j, 2, o)
                if nxt:
                    row_max(n, 1)
                    row_max(n, 2)
                normalise(j, 3, o)
                if nxt:
                    row_max(n, 3)
                    split_max(n)
                dve.wait_ge(out_ready, j + 1)
                o.after(V.tensor_tensor(pg.x[:, j, :], misc[:, 0:D], pg.x[:, j, :], ALU.add))
                V.tensor_tensor(pg.x[:, j, :], pg.x[:, j, :], w["bias"][:, :], ALU.add).then_inc(x_done, 1)
                o.close()

            pg.wait_loads(dve, f"cross{layer}")
            turns(dve, turn)


class ImageProducts:

    def __init__(self, pg, ctx):
        self.pg, self.w = pg, pg.cross_w[1]
        (self.qk_ready, self.qk_copied, self.vw_ready, self.vw_copied, self.vt_ready, self.vt_copied) = pg.sems("im", (
            "qk_ready qk_copied vw_ready vw_copied vw_transposed vw_done"))
        self.vwb = pg.sbuf("im_vwb", [P, NB, NH, IPA], ctx=ctx)
        self.ps, self.vt_ps = pg.bank[6], pg.bank[3]

    def tensor_keys(self, pe):
        for t in range(NT):
            mm = self.pg.nc.tensor.matmul(self.ps[:, t * 64:(t + 1) * 64], self.w["wq_t"][:, t, :],
                                          self.w["img2"][1][:, t, :, :].rearrange("p g n -> p (g n)"), start=True, stop=True)
        mm.then_inc(self.qk_ready, 1)

    def tensor_values(self, pe):
        pe.wait_ge(self.qk_copied, 1)
        for t in range(NT):
            mm = self.pg.nc.tensor.matmul(self.ps[:, t * 64:(t + 1) * 64], self.w["o"][:, t, :],
                                          self.w["img2"][0][:, t, :, :].rearrange("p g n -> p (g n)"), start=True, stop=True)
        mm.then_inc(self.vw_ready, 1)

    def tensor_transposes(self, pe, half):
        pe.wait_ge(self.vw_copied, 1)
        if half:
            pe.wait_ge(self.vt_copied, 1)
        for b in range(4 * half, 4 * half + 4):
            mm = self.pg.nc.tensor.transpose(self.vt_ps[0:NH * IPA, (b % 4) * P:(b % 4 + 1) * P],
                                             self.vwb[:, b, :, :].rearrange("p h k -> p (h k)"), self.pg.ident[:, :])
        mm.then_inc(self.vt_ready, 1)

    def scalar_keys(self, act):
        act.wait_ge(self.qk_ready, 1)
        self.pg.nc.scalar.mul(self.w["qk_image"][:, :, :].rearrange("p b (h k) -> p b h k", k=IPA),
                              self.ps[:, :].rearrange("p (h b k) -> p b h k", h=NH, b=NB), HD ** -0.5).then_inc(self.qk_copied, 1)

    def scalar_values(self, act):
        act.wait_ge(self.vw_ready, 1)
        self.pg.nc.scalar.copy(self.vwb[:, :, :, :], self.ps[:, :].rearrange("p (h b k) -> p b h k", h=NH, b=NB)).then_inc(self.vw_copied, 1)

    def scalar_transposes(self, act, half):
        act.wait_ge(self.vt_ready, half + 1)
        self.pg.nc.scalar.copy(self.w["vw"][:, 4 * half:4 * half + 4, :].rearrange("n b d -> n (b d)"),
                               self.vt_ps[0:NH * IPA, :]).then_inc(self.vt_copied, 1)


def self_attention(pg):
    nc, a = pg.nc, pg.a
    W = D // NH
    VW = 32
    SLOTS, USED = 8, 6
    SCALE = W ** -0.5
    QS = {"h": (0, 3, 5), "m": (1, 4), "l": (2,)}
    KS = {"h": (0, 2, 4), "m": (1, 5), "l": (3,)}
    with ExitStack() as ctx:
        (wt_ready, zeroed, wt_copied, bias_scaled, var_ready, rstd_ready,
         norm_order, xn_ready, xt_ready, xt_copied, qkv_ready, qk_added, v_added, split_order, split_done, dup_done,
         qt_ready, qt_copied, kt_ready, kt_copied, s_ready, s_read, nm_ready, nmt_ready, nmt_copied, st_ready,
         st_read, exp_done, av_ready, av_copied, avt_ready, o_done, ot_ready, ot_copied, out_ready, x_done, order_sem) = pg.sems("sa", (
            "wt_ready zeroed wt_copied bias_scaled var_ready rstd_ready "
            "norm_order xn_ready xt_ready xt_copied qkv_ready qk_added v_added split_order split_done dup_done "
            "qt_ready qt_copied kt_ready kt_copied s_ready s_read max_ready max_transposed max_copied st_ready "
            "st_read exp_done av_ready av_copied avt_ready o_done ot_ready ot_copied out_ready x_done order"))
        sb = lambda n, s, dt=F32: pg.sbuf(f"sa_{n}", s, dt, ctx=ctx)
        two = lambda n, s, dt=F32: [sb(f"{n}{p}", s, dt) for p in range(2)]
        w_nat, bqkv, bo = (pg.self_w[n] for n in ("w_nat", "bqkv", "bo"))
        wt = sb("wt", [P, 4, D])
        alibi, alibi_bf = pg.alibi, pg.alibi_bf
        st, mv, ve, rs, xn = sb("st", [P, 6]), sb("mv", [P, 2]), sb("ve", [P, 1]), sb("rs", [P, 1]), sb("xn", [P, D])
        xt = sb("xt", [P, P])
        qk, rest = sb("qk", [P, 2, NH, W]), sb("rest", [P, 2, NH, W])
        parts = sb("parts", [P, 2, NH, SLOTS, W], BF16)
        qt, kt = two("qt", [P, NT, P], BF16), two("kt", [P, NT, P], BF16)
        v = two("v", [P, NH, VW])
        av_sb = sb("av_sb", [P, NCH * P])
        m, nm, nmt = sb("m", [P, NH]), sb("nm", [P, P // NH, NH], BF16), two("nmt", [P, P], BF16)
        pre, pt = two("pre", [P, HPC * P]), sb("pt", [P, NCH, HPC, P])
        rinv, on, ot = sb("rinv", [P, NH]), sb("on", [P, D]), sb("ot", [P, P])
        qt_bank, kt_bank, score_t, score, misc, av, qkv = (
            pg.bank[0], pg.bank[1], pg.bank[2:4], (pg.bank[4], pg.bank[1]), pg.bank[5], pg.bank[6], pg.bank[7])
        avt = kt_bank
        ot_ps, nmt_ps, out_ps = misc[:, P:2 * P], misc[:, 256:320].bitcast(BF16)[:, 0:P], misc[:, 384:512]
        image = ImageProducts(pg, ctx)
        block = ctx.enter_context(nc.Block())

        def rows_of(t, h):
            return t[64 * (h % 2):64 * (h % 2) + USED * W, h // 2, :]

        def turns(eng, turn):
            with eng.Fori(0, NB // 2 - 1) as i:
                for p in range(2):
                    turn(2 * i + p, p, True, True)
            turn(NB - 2, 0, True, False)
            turn(NB - 1, 1, False, False)

        @block.gpsimd
        def _(pool):
            def rstd(n):
                pool.wait_ge(var_ready, n + 1)
                nc.gpsimd.tensor_tensor(rs[:, :], ve[:, :], pg.neg_half[:, 0:1], ALU.pow).then_inc(rstd_ready, 1)

            def duplicate(n):
                for part, count in (("h", 1), ("m", 3)):
                    for k, slots in enumerate((QS[part], KS[part])):
                        first, again = slots[0], slots[1:]
                        dst = parts[:, k, :, again[0]:again[-1] + 1:2, :]
                        src = bc(parts[:, k, :, first:first + 1, :], [P, NH, len(again), W])
                        if k == 0:
                            pool.wait_ge(split_order, 3 * n + count)
                        nc.gpsimd.tensor_tensor(dst, src, bc(pg.zero[:, :].unsqueeze(2).unsqueeze(3), [P, NH, len(again), W]),
                                                ALU.add).then_inc(dup_done, 1)

            rstd(0)
            nc.gpsimd.memset(parts[:, :, :, :, :], 0.0).then_inc(zeroed, 1)
            for p in range(2):
                nc.gpsimd.memset(v[p][:, :, W:W + 1], 1.0).then_inc(zeroed, 1)
                nc.gpsimd.memset(v[p][:, :, W + 1:VW], 0.0).then_inc(zeroed, 1)
            nc.gpsimd.memset(nm[:, 2:, :], 0.0).then_inc(zeroed, 1)
            for n in range(1, 3):
                rstd(n)
            for n in range(2):
                if n:
                    pool.wait_ge(kt_ready, 1)
                duplicate(n)

            def turn(j, p, nxt, ahead):
                if ahead:
                    rstd(j + 3)
                    duplicate(j + 2)

            turns(pool, turn)

        @block.tensor
        def _(pe):
            pg.wait_loads(pe, "self")
            for k in range(4):
                nc.tensor.transpose(score_t[0][:, k * P:(k + 1) * P], w_nat[:, k, :], pg.ident[:, :]).then_inc(wt_ready, 1)

            def x_transpose(n):
                pe.wait_ge(xn_ready, n + 1)
                nc.tensor.transpose(misc[:, 0:P], xn[:, :], pg.ident[:, :]).then_inc(xt_ready, 1)

            def project(n):
                pe.wait_ge(xt_copied, n + 1)
                pe.wait_ge(v_added, n)
                nc.tensor.matmul(qkv[:, 0:3 * D], xt[:, :], wt[:, 0:3, :].rearrange("p t d -> p (t d)"),
                                 start=True, stop=True).then_inc(qkv_ready, 1)

            def transpose_parts(n, k, bank, ready):
                if k == 0:
                    pe.wait_ge(split_done, 2 * n + 2)
                    pe.wait_ge(dup_done, 4 * n + 4)
                ps = bank[:, :].bitcast(BF16)
                for t in range(NT):
                    mm = nc.tensor.transpose(ps[:, t * P:(t + 1) * P],
                                             parts[:, k, 2 * t:2 * t + 2, :, :].rearrange("p h s w -> p (h s w)"),
                                             pg.ident_bf[:, :])
                mm.then_inc(ready, 1)

            def scores(n, p, c):
                if c == 0:
                    pe.wait_ge(qt_copied, n + 1)
                    pe.wait_ge(kt_copied, n + 1)
                if c >= 2:
                    pe.wait_ge(s_read, NCH * n + c - 1)
                nc.tensor.matmul(score[c % 2][:, :], pg.ident_bf[:, :], alibi_bf[:, c, :, :].rearrange("p r k -> p (r k)"),
                                 start=True, stop=False)
                for r in range(HPC):
                    h = head(c, r)
                    mm = nc.tensor.matmul(score[c % 2][:, r * P:(r + 1) * P], rows_of(qt[p], h), rows_of(kt[p], h),
                                          start=False, stop=(r == HPC - 1))
                mm.then_inc(s_ready, 1)

            def max_transpose(n):
                pe.wait_ge(nm_ready, 2 * n + 2)
                nc.tensor.transpose(nmt_ps, nm[:, :, :].rearrange("p k h -> p (k h)"), pg.ident_bf[:, :]).then_inc(nmt_ready, 1)

            def scores_t(j, p, c):
                if c == 0:
                    pe.wait_ge(nmt_copied, j + 1)
                if c >= 2:
                    pe.wait_ge(st_read, NCH * j + c - 1)
                for r in range(HPC):
                    h = head(c, r)
                    dst = score_t[c % 2][:, r * P:(r + 1) * P]
                    nc.tensor.matmul(dst, rows_of(kt[p], h), rows_of(qt[p], h), start=True, stop=False)
                    mm = nc.tensor.matmul(dst, pg.sel[:, h, :], nmt[p][:, :], start=False, stop=True)
                mm.then_inc(st_ready, 1)

            def values(j, p, c):
                if c == 0:
                    pe.wait_ge(v_added, j + 1)
                pe.wait_ge(exp_done, NCH * j + c + 1)
                for r in range(HPC):
                    mm = nc.tensor.matmul(av[VW * r:VW * (r + 1), c * P:(c + 1) * P], v[p][:, head(c, r), :], pt[:, c, r, :],
                                          start=True, stop=True)
                mm.then_inc(av_ready, 1)

            x_transpose(0)
            image.tensor_keys(pe)
            pe.wait_ge(wt_copied, 2)
            project(0)
            x_transpose(1)
            image.tensor_values(pe)
            project(1)
            image.tensor_transposes(pe, 0)
            pe.wait_ge(zeroed, 6)
            for k, (bank, ready) in enumerate(((qt_bank, qt_ready), (kt_bank, kt_ready))):
                transpose_parts(0, k, bank, ready)
            x_transpose(2)
            image.tensor_transposes(pe, 1)
            for c in range(NCH):
                scores(0, 0, c)
            pe.wait_ge(s_read, NCH)
            for k, (bank, ready) in enumerate(((qt_bank, qt_ready), (kt_bank, kt_ready))):
                transpose_parts(1, k, bank, ready)
            pe.wait_ge(xt_copied, 3)
            max_transpose(0)

            for c in range(2):
                scores_t(0, 0, c)

            def turn(j, p, nxt, ahead):
                n, q = j + 1, 1 - p
                values(j, p, 0)
                if nxt:
                    scores(n, q, 0)
                scores_t(j, p, 2)
                if ahead:
                    project(j + 2)
                values(j, p, 1)
                if nxt:
                    scores(n, q, 1)
                if ahead:
                    pe.wait_ge(x_done, j + 1)
                    x_transpose(j + 3)
                scores_t(j, p, 3)
                if nxt:
                    scores(n, q, 2)
                values(j, p, 2)
                if nxt:
                    scores(n, q, 3)
                values(j, p, 3)
                if ahead:
                    pe.wait_ge(xt_copied, j + 4)
                else:
                    pe.wait_ge(x_done, j + 1)
                if nxt:
                    max_transpose(n)
                pe.wait_ge(av_copied, j + 1)
                if nxt:
                    pe.wait_ge(s_read, NCH * n + NCH)
                for c in range(NCH):
                    mm = nc.tensor.transpose(avt[:, c * P:(c + 1) * P], av_sb[:, c * P:(c + 1) * P], pg.ident[:, :])
                mm.then_inc(avt_ready, 1)
                if ahead:
                    transpose_parts(j + 2, 0, qt_bank, qt_ready)
                if nxt:
                    scores_t(n, q, 0)
                pe.wait_ge(o_done, 2 * j + 2)
                nc.tensor.transpose(ot_ps, on[:, :], pg.ident[:, :]).then_inc(ot_ready, 1)
                if ahead:
                    transpose_parts(j + 2, 1, kt_bank, kt_ready)
                if nxt:
                    scores_t(n, q, 1)
                pe.wait_ge(ot_copied, j + 1)
                nc.tensor.matmul(out_ps, ot[:, :], wt[:, 3, :], start=True, stop=True).then_inc(out_ready, 1)

            turns(pe, turn)

        @block.scalar
        def _(act):
            def copy_xt(n):
                act.wait_ge(xt_ready, n + 1)
                nc.scalar.copy(xt[:, :], misc[:, 0:P]).then_inc(xt_copied, 1)

            def copy_parts(n, p, dst, bank, ready, done):
                act.wait_ge(ready, n + 1)
                nc.scalar.copy(dst[p][:, :, :].rearrange("p t l -> p (t l)"), bank[:, :].bitcast(BF16)).then_inc(done, 1)

            def copy_max(n, p):
                act.wait_ge(nmt_ready, n + 1)
                nc.scalar.copy(nmt[p][:, :], nmt_ps).then_inc(nmt_copied, 1)

            def exp(j, c):
                act.wait_ge(st_read, NCH * j + c + 1)
                nc.scalar.activation(pt[:, c, :, :].rearrange("p r l -> p (r l)"), pre[c % 2][:, :], ACT.Exp).then_inc(exp_done, 1)

            act.wait_ge(wt_ready, 4)
            nc.scalar.mul(wt[:, 0, :], score_t[0][:, 0:P], SCALE).then_inc(wt_copied, 1)
            nc.scalar.copy(wt[:, 1:4, :].rearrange("p t d -> p (t d)"), score_t[0][:, P:4 * P]).then_inc(wt_copied, 1)
            copy_xt(0)
            image.scalar_keys(act)
            act.wait_ge(qkv_ready, 1)
            copy_xt(1)
            image.scalar_values(act)
            image.scalar_transposes(act, 0)
            copy_parts(0, 0, qt, qt_bank, qt_ready, qt_copied)
            copy_parts(0, 0, kt, kt_bank, kt_ready, kt_copied)
            copy_xt(2)
            image.scalar_transposes(act, 1)
            copy_parts(1, 1, qt, qt_bank, qt_ready, qt_copied)
            copy_parts(1, 1, kt, kt_bank, kt_ready, kt_copied)
            copy_max(0, 0)

            for c in range(2):
                exp(0, c)

            def turn(j, p, nxt, ahead):
                n, q = j + 1, 1 - p
                exp(j, 2)
                if ahead:
                    copy_xt(j + 3)
                exp(j, 3)
                act.wait_ge(av_ready, NCH * j + NCH)
                nc.scalar.copy(av_sb[:, :], av[:, :]).then_inc(av_copied, 1)
                if nxt:
                    copy_max(n, q)
                if ahead:
                    copy_parts(j + 2, p, qt, qt_bank, qt_ready, qt_copied)
                if nxt:
                    exp(n, 0)
                act.wait_ge(ot_ready, j + 1)
                nc.scalar.copy(ot[:, :], ot_ps).then_inc(ot_copied, 1)
                if ahead:
                    copy_parts(j + 2, p, kt, kt_bank, kt_ready, kt_copied)
                if nxt:
                    exp(n, 1)

            turns(act, turn)

        @block.vector
        def _(dve):
            V = nc.vector

            def norm_stats(n):
                V.bn_stats(st[:, :], pg.x[:, n, :]).then_inc(norm_order, 1)

            def wait_stats(n):
                dve.wait_ge(norm_order, 2 * n + 1)

            def norm_aggregate(n):
                V.bn_aggr(mv[:, :], st[:, :]).then_inc(norm_order, 1)
                dve.wait_ge(norm_order, 2 * n + 2)
                V.tensor_scalar(ve[:, :], mv[:, 1:2], EPS, None, ALU.add).then_inc(var_ready, 1)

            def norm_apply(n):
                dve.wait_ge(rstd_ready, n + 1)
                V.tensor_scalar(xn[:, :], pg.x[:, n, :], mv[:, 0:1], rs[:, 0:1], ALU.subtract,
                                ALU.mult).then_inc(xn_ready, 1)

            def split(n):
                dve.wait_ge(qkv_ready, n + 1)
                V.tensor_tensor(qk[:, :, :, :].rearrange("p k h w -> p (k h w)"), qkv[:, 0:2 * D], bqkv[:, 0:2 * D],
                                ALU.add).then_inc(qk_added, 1)
                o = Order(dve, split_order, n, 3)
                dve.wait_ge(qk_added, n + 1)
                high, middle = parts[:, :, :, 0, :], parts[:, :, :, 1, :]
                o.after(V.tensor_copy(high, qk[:, :, :, :]))
                o.after(V.tensor_tensor(rest[:, :, :, :], qk[:, :, :, :], high, ALU.subtract))
                o.after(V.tensor_copy(middle, rest[:, :, :, :]))
                for k, slots in enumerate((QS["l"], KS["l"])):
                    V.tensor_tensor(parts[:, k, :, slots[0], :], rest[:, k, :, :], middle[:, k], ALU.subtract).then_inc(split_done, 1)
                o.close()

            def add_v(n, p):
                V.tensor_tensor(v[p][:, :, 0:W], qkv[:, 2 * D:3 * D].rearrange("p (h w) -> p h w", w=W),
                                bqkv[:, 2 * D:3 * D].rearrange("p (h w) -> p h w", w=W), ALU.add).then_inc(v_added, 1)

            def row_max(n, c):
                dve.wait_ge(s_ready, NCH * n + c + 1)
                V.tensor_reduce(m[:, heads_of(c)], score[c % 2][:, :].rearrange("p (h k) -> p h k", k=P), AX, ALU.max,
                                negate=True).then_inc(s_read, 1)

            def split_max(n):
                dve.wait_ge(s_read, NCH * n + NCH)
                V.tensor_copy(nm[:, 0, :], m[:, :]).then_inc(nm_ready, 1)
                dve.wait_ge(nm_ready, 2 * n + 1)
                V.tensor_tensor(nm[:, 1, :], m[:, :], nm[:, 0, :], ALU.subtract).then_inc(nm_ready, 1)

            def add_bias(j, c):
                dve.wait_ge(st_ready, NCH * j + c + 1)
                V.tensor_tensor(pre[c % 2][:, :], score_t[c % 2][:, :], alibi[:, c, :, :].rearrange("p r k -> p (r k)"),
                                ALU.add).then_inc(st_read, 1)

            nc.vector.memset(pg.first[:, :], 0.0).then_inc(x_done, 1)
            for n in range(2):
                norm_stats(n)
                wait_stats(n)
                norm_aggregate(n)
                if n:
                    dve.wait_ge(xt_ready, n)
                norm_apply(n)
                if n == 0:
                    pg.wait_loads(dve, "self")
                    V.tensor_scalar(bqkv[:, 0:D], bqkv[:, 0:D], SCALE, None, ALU.mult).then_inc(bias_scaled, 1)
            dve.wait_ge(bias_scaled, 1)
            dve.wait_ge(zeroed, 6)
            split(0)
            add_v(0, 0)
            norm_stats(2)
            wait_stats(2)
            norm_aggregate(2)
            dve.wait_ge(xt_ready, 2)
            norm_apply(2)
            dve.wait_ge(kt_ready, 1)
            split(1)
            add_v(1, 1)
            for c in range(NCH):
                row_max(0, c)
            split_max(0)

            for c in range(2):
                add_bias(0, c)

            def turn(j, p, nxt, ahead):
                n = j + 1
                o = Order(dve, order_sem, j, 3)
                if ahead:
                    norm_stats(j + 3)
                if nxt:
                    if ahead:
                        wait_stats(j + 3)
                    row_max(n, 0)
                if ahead:
                    norm_aggregate(j + 3)
                add_bias(j, 2)
                if ahead:
                    norm_apply(j + 3)
                    split(j + 2)
                if nxt:
                    row_max(n, 1)
                add_bias(j, 3)
                if nxt:
                    row_max(n, 2)
                    row_max(n, 3)
                    split_max(n)
                dve.wait_ge(avt_ready, j + 1)
                if ahead:
                    add_v(j + 2, p)
                src = avt[:, :].rearrange("p (a b r e) -> p a r b e", a=2, b=2, r=HPC)
                pairs = lambda t: t.rearrange("p (a r b w) -> p a r b w", a=2, b=2, r=HPC)
                for u in range(2):
                    o.mark(V.reciprocal(pairs(rinv[:, :])[:, u], src[:, u, :, :, W:W + 1]))
                o.wait()
                for u in range(2):
                    V.tensor_tensor(pairs(on[:, :])[:, u], src[:, u, :, :, 0:W],
                                    bc(pairs(rinv[:, :])[:, u], [P, HPC, 2, W]), ALU.mult).then_inc(o_done, 1)
                if nxt:
                    add_bias(n, 0)
                    add_bias(n, 1)
                dve.wait_ge(out_ready, j + 1)
                o.after(V.tensor_tensor(pg.x[:, j, :], out_ps, pg.x[:, j, :], ALU.add))
                V.tensor_tensor(pg.x[:, j, :], pg.x[:, j, :], bo[:, :], ALU.add).then_inc(x_done, 1)
                o.close()

            turns(dve, turn)


def feed_forward(pg, layer):
    nc, a = pg.nc, pg.a
    K = 2 if layer else 1
    FT = 4 if layer else 2
    TB = HALF // P
    F = FT * P
    with ExitStack() as ctx:
        (router_in, var_ready, rstd_ready, xn_ready, xt_ready, xt_copied, router_t_ready, router_t_copied, lg_ready,
         lg_read, sub_done, e_done, ones_done, lower_done, order_sem, high_ready, low_ready) = pg.sems(f"rt{layer}", (
            "weights_in var_ready rstd_ready xn_ready xt_ready xt_copied weights_transposed weights_copied logits_ready "
            "logits_read shifted exp_done ones_done lower_done order high_ready low_ready"))
        sb = lambda n, s, dt=F32: pg.sbuf(f"ff{layer}_{n}", s, dt, ctx=ctx)
        two = lambda n, s, dt=F32: [sb(f"{n}{p}", s, dt) for p in range(2)]
        xt = sb("xt", [P, NB, P])
        xs = [sb(f"xt_{n}", [P, NB * P], F32R) for n in ("high", "low")]
        cw = sb("cw", [P, NE, NB])
        st, mv, ve, rs, xn = norm_all_buffers(pg, ctx, f"ff{layer}")
        w_router, w_nat = sb("w_router", [P, K * NE]), sb("w_nat", [NE, D])
        lg, mx, sm, pr = sb("lg", [P, NB, K, NE]), sb("mx", [P, NB, K]), sb("sm", [P, NB, K]), sb("pr", [P, NB, K, NE])
        lower, rank = sb("lower", [P, NE, NE]), sb("rank", [P, NB, NE])
        gt, eq = sb("gt", [P, NB, NE, NE]), sb("eq", [P, NB, NE, NE])
        (w_in_even, w_in_odd, wt_ready, down_copied, w_high, w_low, gu_ready, act_done, h_done, y_ready, x_done) = pg.sems(f"ex{layer}", (
            "even_weights_in odd_weights_in weights_transposed down_copied weights_high weights_low gate_up_ready "
            "act_done h_done y_ready x_done"))
        high, low = two("high", [P, 2, F], F32R), two("low", [P, 2, F], F32R)
        down = two("down", [P, FT, D])
        if layer:
            gate_up = two("gate_up", [P, 2, F])
        else:
            w1, w2 = two("w1", [P, 2 * FT, D]), two("w2", [P, F])
        BK = 3 if layer else 2
        s = [sb(f"s{n}", [P, HALF]) for n in range(BK)]
        h = two("h", [P, FT, HALF])
        y_ps, gate_ps, up_ps, wt_ps = pg.bank[0:2], pg.bank[2:2 + BK], pg.bank[2 + BK:2 + 2 * BK], pg.bank[6:8]
        xt_ps, lg_ps, router_ps = y_ps, y_ps[0][:, 0:NB * K * NE], up_ps[0][:, 0:NE]
        w_in = (w_in_even, w_in_odd)
        N_W = 3 if layer else 2
        PER = 2 * FT
        block = ctx.enter_context(nc.Block())

        def turns(eng, turn):
            with eng.Fori(0, NE // 2 - 1) as i:
                for p in range(2):
                    turn(2 * i + p, p, True, i)
            for p in range(2):
                turn(NE - 2 + p, p, p == 0, NE // 2 - 1)

        @block.sync
        def _(sp):
            def load(e, p):
                if layer:
                    sp.dma_start(gate_up[p][:, 0, :], a["L1_ffn_w_gate"][e]).then_inc(w_in[p], 16)
                    sp.dma_start(gate_up[p][:, 1, :], a["L1_ffn_w_up"][e]).then_inc(w_in[p], 16)
                    sp.dma_start(down[p][:, :, :], a["L1_ffn_w_down"][e].rearrange("(t p) d -> p t d", p=P)).then_inc(w_in[p], 16)
                else:
                    sp.dma_start(w1[p][:, :, :], a["L0_ffn_w1"][e].rearrange("(t p) d -> p t d", p=P)).then_inc(w_in[p], 16)
                    sp.dma_start(w2[p][:, :], a["L0_ffn_w2"][e]).then_inc(w_in[p], 16)

            if layer:
                with nc.allow_non_contiguous_dma("router weights"):
                    sp.dma_start(w_router[:, 0:NE], a["L1_ffn_w_router"]).then_inc(router_in, 16)
                    sp.dma_start(w_router[:, NE:2 * NE], a["L1_ffn_w_gating"]).then_inc(router_in, 16)
            else:
                sp.dma_start(w_nat[:, :], a["L0_ffn_router_w"]).then_inc(router_in, 16)
            for p in range(2):
                load(p, p)
            with sp.Fori(1, NE // 2) as i:
                for p in range(2):
                    sp.wait_ge(y_ready, 4 * i + 2 * p - 2)
                    load(2 * i + p, p)

        def weights_low(eng, compute, n, p):
            eng.wait_ge(w_high, n + 1)
            if layer:
                compute.tensor_tensor(low[p][:, :, :], gate_up[p][:, :, :], high[p][:, :, :], ALU.subtract).then_inc(w_low, 1)
            else:
                compute.tensor_tensor(low[p][:, :, :].rearrange("p g f -> p (g f)"), wt_ps[0][:, 0:2 * F],
                                      high[p][:, :, :].rearrange("p g f -> p (g f)"), ALU.subtract).then_inc(w_low, 1)

        @block.gpsimd
        def _(pool):
            nc.gpsimd.memset(lower[:, :, :], 1.0).then_inc(ones_done, 1)
            pool.wait_ge(var_ready, 1)
            nc.gpsimd.tensor_tensor(rs[:, :], ve[:, :], pg.neg_half[:, :], ALU.pow).then_inc(rstd_ready, 1)
            pool.wait_ge(ones_done, 1)
            nc.gpsimd.affine_select(out=lower[:, :, :], in_=lower[:, :, :], compare_op=ALU.is_gt, fill=0.0, base=0,
                                    pattern=[[1, NE], [-1, NE]], channel_multiplier=0).then_inc(lower_done, 1)
            if layer:
                weights_low(pool, nc.gpsimd, 0, 0)

                def turn(e, p, more, i):
                    if more:
                        weights_low(pool, nc.gpsimd, e + 1, 1 - p)

                turns(pool, turn)

        @block.tensor
        def _(pe):
            def transpose_weights(n, p, loads):
                pe.wait_ge(w_in[p], 16 * N_W * loads)
                for t in range(2 * FT):
                    nc.tensor.transpose(wt_ps[0][:, t * P:(t + 1) * P], w1[p][:, t, :], pg.ident[:, :]).then_inc(wt_ready, 1)
                for t in range(FT):
                    nc.tensor.transpose(wt_ps[1][:, t * P:(t + 1) * P], w2[p][:, t * P:(t + 1) * P], pg.ident[:, :]).then_inc(wt_ready, 1)

            def hidden(e, p, n, t):
                k = n * FT + t
                if k >= BK:
                    pe.wait_ge(h_done, PER * e + k - BK + 1)
                cols = slice(n * HALF, (n + 1) * HALF)
                for g, ps in enumerate((gate_ps, up_ps)):
                    for q, (wp, xp) in enumerate(((low, 0), (high, 1), (high, 0))):
                        mm = nc.tensor.matmul(ps[k % BK][:, :], wp[p][:, g, t * P:(t + 1) * P], xs[xp][:, cols],
                                              start=(q == 0), stop=(q == 2))
                mm.then_inc(gu_ready, 1)

            def output(e, p, n):
                pe.wait_ge(h_done, PER * e + (n + 1) * FT)
                pe.wait_ge(x_done, 2 * e + 1)
                pe.wait_ge(lg_read, K)
                for b in range(TB):
                    for t in range(FT):
                        mm = nc.tensor.matmul(y_ps[n][:, b * D:(b + 1) * D], h[n][:, t, b * P:(b + 1) * P],
                                              down[p][:, t, :], start=(t == 0), stop=(t == FT - 1))
                mm.then_inc(y_ready, 1)

            pe.wait_ge(router_in, 16 * K)
            if not layer:
                nc.tensor.transpose(router_ps, w_nat[:, :], pg.ident[0:NE, 0:NE]).then_inc(router_t_ready, 1)
                transpose_weights(0, 0, 1)
            for b in range(NB):
                pe.wait_ge(xn_ready, b + 1)
                nc.tensor.transpose(xt_ps[b // 4][:, (b % 4) * P:(b % 4 + 1) * P], xn[:, b, :],
                                    pg.ident[:, :]).then_inc(xt_ready, 1)
            if not layer:
                pe.wait_ge(router_t_copied, 1)
            pe.wait_ge(high_ready, 1)
            for b in range(NB):
                pe.wait_ge(xt_copied, b // 4 + 1)
                mm = nc.tensor.matmul(lg_ps[:, b * K * NE:(b + 1) * K * NE], xt[:, b, :], w_router[:, :],
                                      start=True, stop=True)
            mm.then_inc(lg_ready, 1)
            pe.wait_ge(high_ready, 2)
            pe.wait_ge(low_ready, 2)

            def turn(e, p, more, i):
                pe.wait_ge(w_low, e + 1)
                if layer:
                    pe.wait_ge(w_in[p], 16 * N_W * i + 16 * N_W)
                else:
                    pe.wait_ge(down_copied, e + 1)
                for t in range(FT):
                    hidden(e, p, 0, t)
                if more and not layer:
                    transpose_weights(e + 1, 1 - p, i + 1 + p)
                for t in range(FT):
                    hidden(e, p, 1, t)
                for n in range(2):
                    output(e, p, n)

            turns(pe, turn)

        @block.scalar
        def _(act):
            def weights_high(n, p, loads):
                if layer:
                    act.wait_ge(w_in[p], 16 * N_W * loads)
                    nc.scalar.copy(high[p][:, :, :], gate_up[p][:, :, :]).then_inc(w_high, 1)
                else:
                    act.wait_ge(wt_ready, 3 * FT * n + 2 * FT)
                    nc.scalar.copy(high[p][:, :, :].rearrange("p g f -> p (g f)"), wt_ps[0][:, 0:2 * F]).then_inc(w_high, 1)
                    act.wait_ge(wt_ready, 3 * FT * n + 3 * FT)
                    nc.scalar.copy(down[p][:, :, :].rearrange("p t d -> p (t d)"), wt_ps[1][:, 0:F]).then_inc(down_copied, 1)

            if not layer:
                act.wait_ge(router_t_ready, 1)
                nc.scalar.copy(w_router[:, :], router_ps).then_inc(router_t_copied, 1)
            weights_high(0, 0, 1)
            for n in range(2):
                act.wait_ge(xt_ready, 4 * n + 4)
                nc.scalar.copy(xt[:, 4 * n:4 * n + 4, :].rearrange("p b l -> p (b l)"),
                               xt_ps[n][:, :]).then_inc(xt_copied, 1)
                nc.scalar.copy(xs[0][:, n * HALF:(n + 1) * HALF], xt_ps[n][:, :]).then_inc(high_ready, 1)
            act.wait_ge(sub_done, 1)
            nc.scalar.activation(lg[:, :, :, :], lg[:, :, :, :], ACT.Exp).then_inc(e_done, 1)

            def turn(e, p, more, i):
                for k in range(PER):
                    act.wait_ge(gu_ready, PER * e + k + 1)
                    nc.scalar.activation(s[k % BK][:, :], gate_ps[k % BK][:, :], ACT.Silu).then_inc(act_done, 1)
                    if more and k == FT:
                        weights_high(e + 1, 1 - p, i + 1 + p)

            turns(act, turn)

        @block.vector
        def _(dve):
            nc.vector.memset(pg.first[:, :], 0.0).then_inc(x_done, 1)
            o, V = Order(dve, order_sem), nc.vector
            norm_all(pg, dve, o, st, mv, ve, var_ready, rstd_ready, rs, xn, xn_ready)
            if not layer:
                weights_low(dve, V, 0, 0)
            for n in range(2):
                half = slice(n * HALF, (n + 1) * HALF)
                dve.wait_ge(xt_copied, n + 1)
                dve.wait_ge(high_ready, n + 1)
                V.tensor_tensor(xs[1][:, half], xt[:, :, :].rearrange("p b l -> p (b l)")[:, half], xs[0][:, half],
                                ALU.subtract).then_inc(low_ready, 1)
            dve.wait_ge(lg_ready, 1)
            src = lg_ps.rearrange("p (b k e) -> p b k e", b=NB, k=K)
            for k in range(K):
                V.tensor_scalar(lg[:, :, k, :], src[:, :, k, :], 10.0 if k else 1.0, None, ALU.mult).then_inc(lg_read, 1)
            dve.wait_ge(lg_read, K)
            o.after(V.tensor_reduce(mx[:, :, :], lg[:, :, :, :], AX, ALU.max))
            V.tensor_tensor(lg[:, :, :, :], lg[:, :, :, :], bc(mx[:, :, :].unsqueeze(3), [P, NB, K, NE]),
                            ALU.subtract).then_inc(sub_done, 1)
            dve.wait_ge(e_done, 1)
            o.after(V.tensor_reduce(sm[:, :, :], lg[:, :, :, :], AX, ALU.add))
            o.after(V.reciprocal(sm[:, :, :], sm[:, :, :]))
            o.after(V.tensor_tensor(pr[:, :, :, :], lg[:, :, :, :], bc(sm[:, :, :].unsqueeze(3), [P, NB, K, NE]), ALU.mult))
            cw_be = cw[:, :, :].rearrange("p e b -> p b e")
            if layer:
                both = pr[:, :, 0, :]
                o.after(V.tensor_tensor(both, both, pr[:, :, 1, :], ALU.mult))
                o.after(V.tensor_reduce(rank[:, :, 0], both, AX, ALU.add))
                o.after(V.tensor_scalar(rank[:, :, 0], rank[:, :, 0], 1e-9, None, ALU.add))
                o.after(V.reciprocal(rank[:, :, 0], rank[:, :, 0]))
                o.after(V.tensor_tensor(cw_be, both, bc(rank[:, :, 0:1], [P, NB, NE]), ALU.mult))

            def keep_two_largest():
                dve.wait_ge(lower_done, 1)
                other = bc(pr[:, :, 0:1, :], [P, NB, NE, NE])
                own = bc(pr[:, :, 0, :].unsqueeze(3), [P, NB, NE, NE])
                o.mark(V.tensor_tensor(gt[:, :, :, :], other, own, ALU.is_gt))
                o.after(V.tensor_tensor(eq[:, :, :, :], other, own, ALU.is_equal))
                o.after(V.tensor_tensor(eq[:, :, :, :], eq[:, :, :, :], bc(lower[:, :, :].unsqueeze(1), [P, NB, NE, NE]), ALU.mult))
                o.after(V.tensor_tensor(gt[:, :, :, :], gt[:, :, :, :], eq[:, :, :, :], ALU.add))
                o.after(V.tensor_reduce(rank[:, :, :], gt[:, :, :, :], AX, ALU.add))
                o.after(V.tensor_scalar(rank[:, :, :], rank[:, :, :], 1.5, None, ALU.is_lt))
                o.after(V.tensor_tensor(cw_be, rank[:, :, :], pr[:, :, 0, :], ALU.mult))

            if not layer:
                keep_two_largest()

            def add(e, n):
                dve.wait_ge(y_ready, 2 * e + n + 1)
                dve.wait_ge(x_done, 2 * e + n + 1)
                for b in range(TB):
                    ins = V.scalar_tensor_tensor(pg.x[:, n * TB + b, :], y_ps[n][:, b * D:(b + 1) * D],
                                                 cw[:, e, n * TB + b:n * TB + b + 1], pg.x[:, n * TB + b, :], ALU.mult, ALU.add)
                ins.then_inc(x_done, 1)

            def turn(e, p, more, i):
                for k in range(PER):
                    dve.wait_ge(act_done, PER * e + k + 1)
                    V.tensor_tensor(h[k // FT][:, k % FT, :], s[k % BK][:, :], up_ps[k % BK][:, :], ALU.mult).then_inc(h_done, 1)
                    if more and not layer and k == FT:
                        weights_low(dve, V, e + 1, 1 - p)
                for n in range(2):
                    add(e, n)

            turns(dve, turn)


def store(pg):
    nc = pg.nc
    with ExitStack() as ctx:
        out_done, = pg.sems("st", "out_done")
        block = ctx.enter_context(nc.Block())

        @block.sync
        def _(sp):
            sp.dma_start(pg.out.rearrange("b l d -> l b d"), pg.x[:, 0:NB, :]).then_inc(out_done, 16)
            sp.wait_ge(out_done, 16)


def decoder(nc, a, out):
    with ExitStack() as ctx:
        pg = Program(nc, ctx, a, out)
        setup(pg)
        state_space(pg)
        pg.recycle_sems()
        cross_attention(pg, 0)
        feed_forward(pg, 0)
        self_attention(pg)
        pg.recycle_sems()
        cross_attention(pg, 1)
        feed_forward(pg, 1)
        store(pg)


_INS = [
    'x', 'ctx_768', 'L0_attn_W_in', 'L0_attn_W_out', 'L0_attn_dt_bias', 'L0_attn_D_param', 'L0_attn_Bn_g',
    'L0_attn_Bn_b', 'L0_attn_Cn_g', 'L0_attn_Cn_b', 'L0_xattn_w_q', 'L0_xattn_w_kv', 'L0_xattn_w_out',
    'L0_xattn_b_out', 'L0_ffn_w1', 'L0_ffn_w2', 'L0_ffn_router_w', 'L1_attn_W_qkv', 'L1_attn_b_qkv',
    'L1_attn_W_out', 'L1_attn_b_out', 'L1_xattn_Wq', 'L1_xattn_Wk', 'L1_xattn_Wv', 'L1_xattn_Wo', 'L1_xattn_bo',
    'L1_xattn_q_down', 'L1_xattn_q_up', 'L1_xattn_q_alpha', 'L1_xattn_k_down', 'L1_xattn_k_up',
    'L1_xattn_k_alpha', 'L1_xattn_v_down', 'L1_xattn_v_up', 'L1_xattn_v_alpha', 'L1_xattn_o_down',
    'L1_xattn_o_up', 'L1_xattn_o_alpha', 'L1_xattn_Wk_ipa', 'L1_xattn_Wv_ipa', 'L1_ffn_w_router',
    'L1_ffn_w_gating', 'L1_ffn_w_gate', 'L1_ffn_w_up', 'L1_ffn_w_down'
]
_OUT_SHAPE = (NB, P, D)


def kernel(**inputs):
    import concourse.bacc as _bacc
    from concourse import mybir as _mybir
    from concourse.bass_utils import run_bass_kernel_spmd as _run

    nc = _bacc.Bacc("TRN2", target_bir_lowering=False, num_devices=1)
    arrays, args = {}, {}
    for name in _INS:
        v = np.ascontiguousarray(inputs[name])
        arrays[f"in_{name}_dram"] = v
        args[name] = nc.dram_tensor(f"in_{name}_dram", v.shape, _mybir.dt.from_np(v.dtype), kind="ExternalInput").ap()
    out = nc.dram_tensor("out_0_dram", _OUT_SHAPE, _mybir.dt.float32, kind="ExternalOutput").ap()
    decoder(nc, args, out)
    r = _run(nc, [arrays], core_ids=[0])
    return r.results[0]["out_0_dram"]
```
